# Optimizing a Trainium2 kernel written in Bass

```python
import numpy as np
import jax
import jax.numpy as jnp

def _softmax(x, axis=-1):
    return jax.nn.softmax(x, axis=axis)

def _gelu(x):
    return jax.nn.gelu(x, approximate=True)

def _silu(x):
    return jax.nn.silu(x)

def _sigmoid(x):
    return jax.nn.sigmoid(x)

def _layernorm(x, axis=-1, eps=1e-05):
    m = jnp.mean(x, axis=axis, keepdims=True)
    v = jnp.var(x, axis=axis, keepdims=True)
    return (x - m) / jnp.sqrt(v + eps)

def _scatter_add(tgt, idx, src, axis=0):
    return tgt.at[idx].add(src)

def _segment_sum(src, seg, n):
    return jax.ops.segment_sum(src, seg, n)
kernel_name = 'mk_prb_d1_jaxref_r4_44e0bf'

def setup_inputs(seed: int=0):
    np.random.seed(seed)
    _w = jnp.asarray

    def _L0_attn_setup():
        import jax, jax.numpy as jnp
        import numpy as np
        D_MODEL = 512
        N_HEADS = 16
        HEAD_DIM = D_MODEL // N_HEADS

        def _alibi_slopes(n_heads: int) -> jnp.ndarray:
            start = 2.0 ** (-8.0 / n_heads)
            return jnp.asarray([start * start ** i for i in range(n_heads)], dtype=jnp.float32)
        key = jax.random.key(seed)
        ks = jax.random.split(key, 9)
        B, S, D = (2, 512, D_MODEL)
        scale = 1.0 / np.sqrt(D)
        return {'x': jax.random.normal(ks[0], (B, S, D), dtype=jnp.float32), 'wq': jax.random.normal(ks[1], (D, D), dtype=jnp.float32) * scale, 'bq': jnp.zeros((D,), dtype=jnp.float32), 'wk': jax.random.normal(ks[2], (D, D), dtype=jnp.float32) * scale, 'bk': jnp.zeros((D,), dtype=jnp.float32), 'wv': jax.random.normal(ks[3], (D, D), dtype=jnp.float32) * scale, 'bv': jnp.zeros((D,), dtype=jnp.float32), 'wo': jax.random.normal(ks[4], (D, D), dtype=jnp.float32) * scale, 'bo': jnp.zeros((D,), dtype=jnp.float32)}
    _L0_attn_in = _L0_attn_setup()

    def _L0_ffn_setup():
        import jax, jax.numpy as jnp
        import numpy as np
        B, S, H = (2, 512, 512)
        E, K, F = (32, 4, 352)
        FS = 1408
        EPS = 1e-06
        CAP = 256
        key = jax.random.key(seed)
        ks = jax.random.split(key, 10)
        s = 0.02
        return {'hidden_states': jax.random.normal(ks[0], (B, S, H), jnp.float32), 'w_norm': 1.0 + 0.02 * jax.random.normal(ks[1], (H,), jnp.float32), 'w_router': s * jax.random.normal(ks[2], (H, E), jnp.float32), 'w_gate': s * jax.random.normal(ks[3], (E, H, F), jnp.float32), 'w_up': s * jax.random.normal(ks[4], (E, H, F), jnp.float32), 'w_down': s * jax.random.normal(ks[5], (E, F, H), jnp.float32), 'sw_gate': s * jax.random.normal(ks[6], (H, FS), jnp.float32), 'sw_up': s * jax.random.normal(ks[7], (H, FS), jnp.float32), 'sw_down': s * jax.random.normal(ks[8], (FS, H), jnp.float32), 'w_shared_gate': s * jax.random.normal(ks[9], (H, 1), jnp.float32)}
    _L0_ffn_in = _L0_ffn_setup()
    _d = {'L0_attn_x': _L0_attn_in['x'], 'L0_attn_wq': _L0_attn_in['wq'], 'L0_attn_bq': _L0_attn_in['bq'], 'L0_attn_wk': _L0_attn_in['wk'], 'L0_attn_bk': _L0_attn_in['bk'], 'L0_attn_wv': _L0_attn_in['wv'], 'L0_attn_bv': _L0_attn_in['bv'], 'L0_attn_wo': _L0_attn_in['wo'], 'L0_attn_bo': _L0_attn_in['bo'], 'L0_ffn_w_norm': _L0_ffn_in['w_norm'], 'L0_ffn_w_router': _L0_ffn_in['w_router'], 'L0_ffn_w_gate': _L0_ffn_in['w_gate'], 'L0_ffn_w_up': _L0_ffn_in['w_up'], 'L0_ffn_w_down': _L0_ffn_in['w_down'], 'L0_ffn_sw_gate': _L0_ffn_in['sw_gate'], 'L0_ffn_sw_up': _L0_ffn_in['sw_up'], 'L0_ffn_sw_down': _L0_ffn_in['sw_down'], 'L0_ffn_w_shared_gate': _L0_ffn_in['w_shared_gate']}
    _x0 = _d['L0_attn_x']
    _d['L0_attn_x'] = jax.random.normal(jax.random.fold_in(jax.random.key(seed), 1), (1, 4096, 512), dtype=_x0.dtype)
    del _x0
    return _d

def reference(L0_attn_x, L0_attn_wq, L0_attn_bq, L0_attn_wk, L0_attn_bk, L0_attn_wv, L0_attn_bv, L0_attn_wo, L0_attn_bo, L0_ffn_w_norm, L0_ffn_w_router, L0_ffn_w_gate, L0_ffn_w_up, L0_ffn_w_down, L0_ffn_sw_gate, L0_ffn_sw_up, L0_ffn_sw_down, L0_ffn_w_shared_gate):

    def _L0_attn_ref(x, wq, bq, wk, bk, wv, bv, wo, bo):
        import jax, jax.numpy as jnp
        import numpy as np
        D_MODEL = 512
        N_HEADS = 16
        HEAD_DIM = D_MODEL // N_HEADS

        def _alibi_slopes(n_heads: int) -> jnp.ndarray:
            start = 2.0 ** (-8.0 / n_heads)
            return jnp.asarray([start * start ** i for i in range(n_heads)], dtype=jnp.float32)
        B, S, D = x.shape
        H, hd = (N_HEADS, HEAD_DIM)

        def heads(y):
            return y.reshape(B, S, H, hd).transpose(0, 2, 1, 3)
        q = heads(x @ wq + bq)
        k = heads(x @ wk + bk)
        v = heads(x @ wv + bv)
        scores = jnp.einsum('bhqd,bhkd->bhqk', q, k) / jnp.sqrt(jnp.float32(hd))
        pos = jnp.arange(S)
        rel = pos[None, :] - pos[:, None]
        slopes = _alibi_slopes(H)
        bias = slopes[:, None, None] * rel.astype(jnp.float32)
        causal = jnp.where(rel > 0, -jnp.inf, 0.0).astype(jnp.float32)
        scores = scores + (bias + causal)[None]
        attn = jax.nn.softmax(scores, axis=-1)
        out = jnp.einsum('bhqk,bhkd->bhqd', attn, v)
        out = out.transpose(0, 2, 1, 3).reshape(B, S, D)
        return out @ wo + bo

    def _L0_ffn_ref(hidden_states, w_norm, w_router, w_gate, w_up, w_down, sw_gate, sw_up, sw_down, w_shared_gate):
        import jax, jax.numpy as jnp
        import numpy as np
        B, S, H = (2, 512, 512)
        E, K, F = (32, 4, 352)
        FS = 1408
        EPS = 1e-06
        CAP = 256
        inp = hidden_states
        xf = inp.astype(jnp.float32)
        var = jnp.mean(xf * xf, axis=-1, keepdims=True)
        x = (w_norm * (xf * jax.lax.rsqrt(var + EPS))).astype(inp.dtype)
        Bq, Sq, Hq = x.shape
        x = x.reshape(-1, Hq)
        T = Bq * Sq
        logits = x @ w_router
        probs = jax.nn.softmax(logits.astype(jnp.float32), axis=-1)
        w_topk, sel = jax.lax.top_k(probs, K)
        w_topk = w_topk.astype(x.dtype)
        flat_e = sel.reshape(-1)
        order = jnp.argsort(flat_e)
        sorted_e = flat_e[order]
        counts = jnp.zeros((E,), jnp.int32).at[flat_e].add(1)
        starts = jnp.cumsum(counts) - counts
        pos = jnp.arange(T * K) - starts[sorted_e]
        tok = order // K
        valid = pos < CAP
        dest = jnp.where(valid, pos, CAP)
        buf = jnp.zeros((E, CAP + 1, Hq), x.dtype).at[sorted_e, dest].set(x[tok])
        buf = buf[:, :CAP]
        g = jnp.einsum('ech,ehf->ecf', buf, w_gate)
        u = jnp.einsum('ech,ehf->ecf', buf, w_up)
        y = jnp.einsum('ecf,efh->ech', jax.nn.silu(g) * u, w_down)
        wv = w_topk.reshape(-1)[order] * valid.astype(x.dtype)
        gath = y[sorted_e, jnp.minimum(pos, CAP - 1)]
        out = jnp.zeros((T, Hq), x.dtype).at[tok].add(gath * wv[:, None])
        sh = jax.nn.silu(x @ sw_gate) * (x @ sw_up) @ sw_down
        sh = jax.nn.sigmoid(x @ w_shared_gate) * sh
        out = out + sh
        return inp + out.reshape(Bq, Sq, Hq)
    x = L0_attn_x
    xn = _layernorm(x, axis=-1)
    x = x + _L0_attn_ref(xn, L0_attn_wq, L0_attn_bq, L0_attn_wk, L0_attn_bk, L0_attn_wv, L0_attn_bv, L0_attn_wo, L0_attn_bo) + _L0_ffn_ref(xn, L0_ffn_w_norm, L0_ffn_w_router, L0_ffn_w_gate, L0_ffn_w_up, L0_ffn_w_down, L0_ffn_sw_gate, L0_ffn_sw_up, L0_ffn_sw_down, L0_ffn_w_shared_gate)
    return x

_drawn_inputs = setup_inputs


def setup_inputs(seed=0):
    import zlib

    import numpy as np

    out = dict(_drawn_inputs(seed))
    spreads = {'L0_attn_bq': (0.0, 2.0),
     'L0_attn_bk': (0.0, 2.0),
     'L0_attn_bv': (0.0, 0.8),
     'L0_attn_bo': (0.0, 0.8)}
    factors = {'L0_ffn_w_norm': 8.0,
     'L0_ffn_w_router': 8.0,
     'L0_ffn_w_gate': 8.0,
     'L0_ffn_w_up': 8.0,
     'L0_ffn_w_down': 8.0,
     'L0_ffn_sw_gate': 2.819,
     'L0_ffn_sw_up': 2.756,
     'L0_ffn_sw_down': 2.756,
     'L0_ffn_w_shared_gate': 8.0,
     'L0_attn_wq': 8.0,
     'L0_attn_wk': 8.0,
     'L0_attn_wv': 8.0,
     'L0_attn_wo': 8.0}
    for name, (base, spread) in spreads.items():
        noise = np.random.default_rng([zlib.crc32(name.encode()), seed]).standard_normal(out[name].shape)
        drawn = base * np.exp(spread * noise) if base else spread * noise
        out[name] = jnp.asarray(drawn.astype(out[name].dtype))
    for name, factor in factors.items():
        out[name] = (out[name] * factor).astype(out[name].dtype)
    return out
```

```python
from contextlib import ExitStack

import concourse.bass as bass
import numpy as np
from concourse import mybir

ALU = mybir.AluOpType
ACT = mybir.ActivationFunctionType
AX = mybir.AxisListType
F32 = mybir.dt.float32
F32R = mybir.dt.float32r
BF16 = mybir.dt.bfloat16
I32 = mybir.dt.int32
U32 = mybir.dt.uint32

P = 128
S = 4096
D = 512
KC = D // P
H = H_ALL = 16
HD = D // H
E = 32
TOPK = 4
CAP = 256
F = 352
FS = 1408
BLK = 512
NB = S // BLK
TB = BLK // P
NT = S // P
RW = E + 2
HPC = P // HD
LN_EPS = 1e-5
RMS_EPS = 1e-6
Q_SCALE = float(1.0 / np.sqrt(np.float32(HD)))
MASKED = -1e30


THREE = ((0, 0), (0, 1), (1, 0))


def as_f32(ap):
    return ap.bitcast(F32)


def open_scope(nc):
    ctx = ExitStack()

    def sb(name, shape, dt=F32):
        return ctx.enter_context(nc.sbuf_tensor(name, shape, dt))

    def ps(name, shape, dt=F32):
        return ctx.enter_context(nc.psum_tensor(name, shape, dt))

    def sem(name):
        return ctx.enter_context(nc.semaphore(name))

    return ctx, sb, ps, sem


def statistics_phase(nc, t, kept):
    ctx, sb, ps, sem = open_scope(nc)
    PER = 2 * TB
    with ctx:
        x_in = sb("st_x", [P, 2, TB, D])
        six = sb("st_six", [P, PER, 6])
        mean_var = sb("st_mv", [P, PER, 2])
        mv_all = sb("st_mv_all", [P, NT, 2])
        a1 = sb("st_a1", [P, NT])
        a2 = sb("st_a2", [P, NT])
        root = sb("st_root", [P, NT])
        tmp = sb("st_tmp", [P, NT])
        raw = sb("st_raw", [P, 3, KC, D])
        raw_r = sb("st_raw_r", [P, KC, RW])
        x_loaded = [sem("st_x_loaded0"), sem("st_x_loaded1")]
        w_loaded = [sem(f"st_w_loaded{i}") for i in range(4)]
        consts_loaded = sem("st_consts_loaded")
        six_done = sem("st_six_done")
        mv_done = sem("st_mv_done")
        mv_copied = sem("st_mv_copied")
        chain = sem("st_chain")
        root_done = sem("st_root_done")
        hi_done = sem("st_hi_done")
        lo_done = sem("st_lo_done")
        pad_done = sem("st_pad_done")
        passed = sem("st_passed")
        x_rows = t["x"].rearrange("a (b t p) d -> (a b) p t d", p=P, t=TB)

        with nc.Block() as block:
            @block.sync
            def _(sp):
                with sp.Fori(0, NB // 2) as it:
                    for s in range(2):
                        sp.wait_ge(mv_copied, it + 1)
                        sp.dma_start(x_in[:, s], x_rows[2 * it + s]).then_inc(x_loaded[s], 16)

            @block.scalar
            def _(act):
                for i, name in enumerate(("wq", "wk", "wv")):
                    act.dma_start(raw[:, i], t[name].rearrange("(c p) n -> p c n", p=P)).then_inc(w_loaded[i], 16)
                act.wait_ge(pad_done, 1)
                act.dma_start(raw_r[:, :, 0:E], t["w_router"].rearrange("(c p) n -> p c n", p=P)).then_inc(w_loaded[3], 16)
                with nc.allow_non_contiguous_dma(reason="one column, once"):
                    act.dma_start(raw_r[:, :, E:E + 1], t["w_sgate"].rearrange("(c p) n -> p c n", p=P)).then_inc(w_loaded[3], 16)
                act.dma_start(kept["w_norm"][:, :], t["w_norm"].partition_broadcast(P)).then_inc(consts_loaded, 16)
                act.dma_start(kept["bv"][:, :], t["bv"].partition_broadcast(P)).then_inc(consts_loaded, 16)
                act.dma_start(kept["bo"][:, :], t["bo"].partition_broadcast(P)).then_inc(consts_loaded, 16)
                with nc.allow_non_contiguous_dma(reason="2 KB, once"):
                    act.dma_start(kept["bqk"][:, 0:KC], t["bq"].rearrange("(c p) -> p c", p=P)).then_inc(consts_loaded, 16)
                    act.dma_start(kept["bqk"][:, KC:2 * KC], t["bk"].rearrange("(c p) -> p c", p=P)).then_inc(consts_loaded, 16)
                act.dma_start(kept["ident"][:, :], t["ident"]).then_inc(consts_loaded, 16)
                act.wait_ge(chain, 1)
                act.activation(root[:, :], a1[:, :], ACT.Sqrt).then_inc(root_done, 1)
                act.wait_ge(chain, 9)
                act.activation(root[:, :], a2[:, :], ACT.Sqrt).then_inc(root_done, 1)
                for i in range(3):
                    act.wait_ge(w_loaded[i], 16)
                    act.activation(kept["w_qkv"][:, 0, i], raw[:, i], ACT.Copy).then_inc(hi_done, 1)
                act.wait_ge(w_loaded[3], 32)
                act.activation(kept["w_r"][:, 0], raw_r[:, :, :], ACT.Copy).then_inc(hi_done, 1)
                act.dma_start(t["alibi_s"], t["alibi"]).then_inc(consts_loaded, 16)
                act.wait_ge(consts_loaded, 16 * 7)

            @block.gpsimd
            def _(pool):
                pool.memset(raw_r[:, :, E:RW], 0.0).then_inc(pad_done, 1)
                for i in range(3):
                    pool.wait_ge(hi_done, i + 1)
                    pool.tensor_tensor(kept["w_qkv"][:, 1, i], raw[:, i], as_f32(kept["w_qkv"][:, 0, i]),
                                       ALU.subtract).then_inc(lo_done, 1)
                pool.wait_ge(hi_done, 4)
                pool.tensor_tensor(kept["w_r"][:, 1], raw_r[:, :, :], as_f32(kept["w_r"][:, 0]),
                                   ALU.subtract).then_inc(lo_done, 1)

            @block.vector
            def _(dve):
                dve.memset(tmp[:, :], 0.0).then_inc(mv_copied, 1)
                with dve.Fori(0, NB // 2) as it:
                    for s in range(2):
                        dve.wait_ge(x_loaded[s], 16 * it + 16)
                        for k in range(TB):
                            dve.bn_stats(six[:, s * TB + k], x_in[:, s, k]).then_inc(six_done, 1)
                    dve.wait_ge(six_done, it * PER + PER)
                    dve.sem_inc(passed, 1)
                    for k in range(PER):
                        dve.bn_aggr(mean_var[:, k], six[:, k]).then_inc(mv_done, 1)
                    dve.wait_ge(mv_done, it * PER + PER)
                    dve.tensor_copy(mv_all[:, bass.ds(it * PER, PER)], mean_var[:, :]).then_inc(mv_copied, 1)
                    dve.wait_ge(mv_copied, it + 2)
                var = mv_all[:, :, 1]
                n = [0]

                def link(ins):
                    n[0] += 1
                    ins.then_inc(chain, 1)
                    dve.wait_ge(chain, n[0])

                def newton(rstd, a):
                    link(dve.reciprocal(rstd, root[:, :]))
                    link(dve.tensor_tensor(tmp[:, :], rstd, rstd, ALU.mult))
                    link(dve.tensor_tensor(tmp[:, :], tmp[:, :], a, ALU.mult))
                    link(dve.tensor_scalar(tmp[:, :], tmp[:, :], -0.5, 1.5, ALU.mult, ALU.add))
                    link(dve.tensor_tensor(rstd, rstd, tmp[:, :], ALU.mult))

                link(dve.tensor_scalar(a1[:, :], var, LN_EPS, None, ALU.add))
                dve.wait_ge(root_done, 1)
                newton(kept["stat"][:, 1], a1[:, :])
                link(dve.tensor_tensor(tmp[:, :], kept["stat"][:, 1], kept["stat"][:, 1], ALU.mult))
                link(dve.tensor_tensor(tmp[:, :], tmp[:, :], var, ALU.mult))
                link(dve.tensor_scalar(a2[:, :], tmp[:, :], RMS_EPS, None, ALU.add))
                assert n[0] == 9
                dve.wait_ge(root_done, 2)
                newton(kept["stat"][:, 2], a2[:, :])
                link(dve.tensor_copy(kept["stat"][:, 0], mv_all[:, :, 0]))


def project_phase(nc, t, kept):
    ctx, sb, ps, sem = open_scope(nc)
    MQK = 2 * KC
    with ctx:
        x_in = sb("pr_x", [P, TB, D])
        xn = sb("pr_xn", [P, TB, D])
        xf = sb("pr_xf", [P, TB, D])
        base = sb("pr_base", [P, TB, D])
        base0 = sb("pr_base0", [P, TB, D])
        stat = sb("pr_stat", [P, 3, TB])
        xT = sb("pr_xT", [P, 2, KC, BLK], F32R)
        fT = sb("pr_fT", [P, 2, KC, BLK], F32R)
        qk = sb("pr_qk", [P, 2, BLK])
        qk_part = sb("pr_qk_part", [P, 2, MQK, BLK], F32R)
        v = sb("pr_v", [P, 2, D])
        v_part = sb("pr_v_part", [P, TB, H, 2, HD], F32R)
        ps_t = [ps(f"pr_ps_t{i}", [P, KC, P]) for i in range(2)]
        ps_m = [ps(f"pr_ps_m{i}", [P, BLK]) for i in range(3)]
        ps_r = ps("pr_ps_r", [P, TB, RW])

        x_loaded = sem("pr_x_loaded")
        x_used = sem("pr_x_used")
        x_used_pool = sem("pr_x_used_pool")
        stat_set = sem("pr_stat_set")
        xn_done = sem("pr_xn_done")
        xf_done = sem("pr_xf_done")
        sum_done = sem("pr_sum_done")
        base_done = sem("pr_base_done")
        turned = sem("pr_turned")
        turned_hi = sem("pr_turned_hi")
        turned_lo = sem("pr_turned_lo")
        r_done = sem("pr_r_done")
        r_copied = sem("pr_r_copied")
        m_done = sem("pr_m_done")
        m_copied = sem("pr_m_copied")
        m_hi = sem("pr_m_hi")
        m_lo = sem("pr_m_lo")
        rows_stored = sem("pr_rows_stored")
        qkv_stored = sem("pr_qkv_stored")
        passed = sem("pr_passed")
        x_rows = t["x"].rearrange("a (b t p) d -> (a b) p t d", p=P, t=TB)
        base_rows = t["base"].rearrange("(b t p) d -> b p t d", p=P, t=TB)
        xf_rows = t["xf"].rearrange("(b t p) d -> b p t d", p=P, t=TB)
        v_rows = t["v_part"].rearrange("(b t p) n -> b p t n", p=P, t=TB)
        NM = MQK + TB
        NTR = 2 * TB
        STORES = 16 * (2 * MQK + 1)

        with nc.Block() as block:
            @block.sync
            def _(sp):
                sp.sem_inc(rows_stored, 48)
                sp.sem_inc(qkv_stored, STORES)
                with sp.Fori(0, NB) as b:
                    sp.wait_ge(xf_done, b * TB + TB)
                    sp.dma_start(xf_rows[b], xf[:, :]).then_inc(rows_stored, 16)
                    sp.wait_ge(base_done, b * TB + TB)
                    sp.dma_start(base_rows[b], base[:, :]).then_inc(rows_stored, 16)
                    sp.wait_ge(turned_lo, b * NTR + NTR + 2)
                    sp.dma_start(t["fT_part"][b], as_f32(fT[:, :])).then_inc(rows_stored, 16)
                    sp.wait_ge(m_hi, b * NM + NM)
                    sp.wait_ge(m_lo, b * NM + NM)
                    for part in range(2):
                        for m in range(MQK):
                            name, c = ("q_part", m) if m < KC else ("k_part", m - KC)
                            dst = t[name][part, c * P:(c + 1) * P, bass.ds(b * BLK, BLK)]
                            sp.dma_start(dst, as_f32(qk_part[:, part, m])).then_inc(qkv_stored, 16)
                    sp.dma_start(v_rows[b], as_f32(v_part[:, :]).rearrange("p t h a d -> p t (h a d)")).then_inc(qkv_stored, 16)
                sp.wait_ge(rows_stored, 48 * NB + 48)
                sp.wait_ge(qkv_stored, STORES * NB + STORES)

            @block.gpsimd
            def _(pool):
                pool.sem_inc(x_used_pool, 1)
                with pool.Fori(0, NB) as b:
                    pool.wait_ge(x_loaded, 16 * b + 16)
                    for k in range(TB):
                        pool.wait_ge(xn_done, b * TB + k + 1)
                        pool.tensor_tensor(base0[:, k], x_in[:, k], xn[:, k], ALU.add).then_inc(x_used_pool, 1)
                        pool.wait_ge(x_used_pool, b * TB + k + 2)
                        if k == 0:
                            pool.wait_ge(rows_stored, b * 48 + 48)
                        pool.tensor_tensor(base[:, k], base0[:, k], kept["bo"][:, :], ALU.add).then_inc(base_done, 1)
                        pool.wait_ge(base_done, b * TB + k + 1)
                    for m in range(NM):
                        pool.wait_ge(m_copied, b * NM + m + 1)
                        if m == 0:
                            pool.wait_ge(qkv_stored, b * STORES + STORES)
                        if m < MQK:
                            src, dst = qk[:, m % 2], qk_part[:, 0, m]
                        else:
                            src = v[:, m % 2].rearrange("p (h d) -> p h d", h=H)
                            dst = v_part[:, m - MQK, :, 0, :]
                        pool.sem_inc(passed, 1)
                        pool.tensor_scalar(dst, src, 1.0, 1.0, ALU.mult, ALU.mult).then_inc(m_hi, 1)

            @block.scalar
            def _(act):
                with act.Fori(0, NB) as b:
                    act.wait_ge(x_used, b * TB + 1)
                    act.wait_ge(x_used_pool, b * TB + 1)
                    act.dma_start(x_in[:, :], x_rows[b]).then_inc(x_loaded, 16)
                    act.wait_ge(m_done, b * NM + NM)
                    act.wait_ge(rows_stored, b * 48 + 48)
                    for i in range(NTR):
                        k = i // 2
                        dst = (xT, fT)[i % 2]
                        act.wait_ge(turned, b * NTR + NTR + i + 1)
                        act.activation(dst[:, 0, :, k * P:(k + 1) * P], ps_t[i % 2][:, :, :], ACT.Copy).then_inc(turned_hi, 1)
                    act.wait_ge(r_done, b + 1)
                    act.activation(kept["logits"][:, bass.ds(b * TB, TB)], ps_r[:, :, :], ACT.Copy).then_inc(r_copied, 1)

            @block.vector
            def _(dve):
                dve.sem_inc(x_used, 1)
                dve.sem_inc(turned_lo, 2)
                with dve.Fori(0, NB) as b:
                    dve.wait_ge(x_used, b * TB + 1)
                    dve.tensor_copy(stat[:, :, :], kept["stat"][:, :, bass.ds(b * TB, TB)]).then_inc(stat_set, 1)
                    dve.wait_ge(stat_set, b + 1)
                    dve.wait_ge(x_loaded, 16 * b + 16)
                    for k in range(TB):
                        if k == 0:
                            dve.wait_ge(turned, b * NTR + NTR)
                            dve.wait_ge(x_used_pool, b * TB + 1)
                            dve.wait_ge(rows_stored, b * 48 + 48)
                        dve.tensor_scalar(xn[:, k], x_in[:, k], stat[:, 0, k:k + 1], stat[:, 1, k:k + 1],
                                          ALU.subtract, ALU.mult).then_inc(xn_done, 1)
                        dve.wait_ge(xn_done, b * TB + k + 1)
                        dve.scalar_tensor_tensor(out=xf[:, k], in0=xn[:, k], scalar=stat[:, 2, k:k + 1],
                                                 in1=kept["w_norm"][:, :], op0=ALU.mult, op1=ALU.mult).then_inc(xf_done, 1)
                        dve.wait_ge(xf_done, b * TB + k + 1)
                        dve.sem_inc(x_used, 1)
                    for i in range(NTR):
                        k = i // 2
                        dst = (xT, fT)[i % 2]
                        dve.wait_ge(turned_hi, b * NTR + i + 1)
                        dve.tensor_tensor(dst[:, 1, :, k * P:(k + 1) * P], ps_t[i % 2][:, :, :],
                                          as_f32(dst[:, 0, :, k * P:(k + 1) * P]), ALU.subtract).then_inc(turned_lo, 1)

                    def low(m):
                        dve.wait_ge(m_hi, b * NM + m + 1)
                        if m < MQK:
                            dve.tensor_tensor(qk_part[:, 1, m], qk[:, m % 2], as_f32(qk_part[:, 0, m]),
                                              ALU.subtract).then_inc(m_lo, 1)
                        else:
                            dve.tensor_tensor(v_part[:, m - MQK, :, 1, :], v[:, m % 2].rearrange("p (h d) -> p h d", h=H),
                                              as_f32(v_part[:, m - MQK, :, 0, :]), ALU.subtract).then_inc(m_lo, 1)

                    for m in range(NM):
                        dve.wait_ge(m_done, b * NM + NM + m + 1)
                        if m >= 2:
                            dve.wait_ge(m_lo, b * NM + m - 1)
                        if m < KC:
                            dve.tensor_scalar(qk[:, m % 2], ps_m[m % 3][:, :], kept["bqk"][:, m:m + 1], Q_SCALE,
                                              ALU.add, ALU.mult).then_inc(m_copied, 1)
                        elif m < MQK:
                            dve.tensor_scalar(qk[:, m % 2], ps_m[m % 3][:, :], kept["bqk"][:, m:m + 1], None,
                                              ALU.add).then_inc(m_copied, 1)
                        else:
                            dve.tensor_tensor(v[:, m % 2], ps_m[m % 3][:, :], kept["bv"][:, :], ALU.add).then_inc(m_copied, 1)
                        if m >= 1:
                            low(m - 1)
                    low(NM - 1)
                    dve.wait_ge(m_lo, b * NM + NM)

            @block.tensor
            def _(pe):
                pe.sem_inc(turned, NTR)
                pe.sem_inc(m_done, NM)
                with pe.Fori(0, NB) as b:
                    for i in range(NTR):
                        k = i // 2
                        src, ready = ((xn, xn_done), (xf, xf_done))[i % 2]
                        pe.wait_ge(ready, b * TB + k + 1)
                        pe.wait_ge(turned_lo, b * NTR + i + 1)
                        for c in range(KC):
                            mm = pe.transpose(ps_t[i % 2][:, c], src[:, k, c * P:(c + 1) * P], kept["ident"][:, :])
                        mm.then_inc(turned, 1)
                    pe.wait_ge(turned_lo, b * NTR + NTR + 2)
                    for k in range(TB):
                        for c in range(KC):
                            for n, (i, j) in enumerate(THREE):
                                mm = pe.matmul(ps_r[:, k], fT[:, i, c, k * P:(k + 1) * P], kept["w_r"][:, j, c],
                                               start=(c == 0 and n == 0), stop=(c == KC - 1 and n == 2))
                    mm.then_inc(r_done, 1)
                    for m in range(NM):
                        if m >= 3:
                            pe.wait_ge(m_copied, b * NM + m - 2)
                        for c in range(KC):
                            for n, (i, j) in enumerate(THREE):
                                if m < MQK:
                                    w = kept["w_qkv"][:, j, m // KC, c, (m % KC) * P:(m % KC + 1) * P]
                                    args = (w, xT[:, i, c])
                                else:
                                    k = m - MQK
                                    args = (xT[:, i, c, k * P:(k + 1) * P], kept["w_qkv"][:, j, 2, c])
                                mm = pe.matmul(ps_m[m % 3][:, :], *args, start=(c == 0 and n == 0),
                                               stop=(c == KC - 1 and n == 2))
                        mm.then_inc(m_done, 1)
                    pe.wait_ge(m_copied, b * NM + NM)
                    pe.wait_ge(r_copied, b + 1)


MAXW = 1024
WRAP = 4
TURN_LEAD = 3
LOW_LAG = 2
LAG = 4
P_SLOTS = 6
POOL_LOWS = (2, 5)
ACT_HIGHS = (1, 4)


def high_by(pair):
    return int(pair % P_SLOTS in ACT_HIGHS)


def low_by(pair):
    return int(pair % P_SLOTS in POOL_LOWS)


def pairs_before(pair, maker, by):
    return sum(maker(p) == by for p in range(pair))


def attention_plan():
    n_u, stream, turn = 2 * NB, [], None
    for u in range(n_u):
        j = u % NB
        for i in range(TB * j, TB * j + TB):
            for k0 in range(0, P * (i + 1), MAXW):
                stream.append(["max", u, 0, i, k0, min(MAXW, P * (i + 1) - k0)])
                if turn:
                    stream.append(turn)
                    turn = None
        turn = ["turn", u, 0]
        if u in (WRAP - 1, n_u - 1):
            stream.append(turn)
            turn = None
    for a, step in enumerate(stream):
        step[2] = a
    N_A = len(stream)
    ahead = 1 + [s[:2] for s in stream].index(["turn", WRAP - 1])
    before = [("load", 0, 0)] + [tuple(s) for s in stream[:ahead]]
    queue = [tuple(s) for s in stream[ahead:]]
    queue += [(s[0], s[1] + n_u, s[2] + N_A, *s[3:]) for s in stream[:ahead]]
    cost = sum(s[5] + 64 for s in stream if s[0] == "max")
    starts, n = [], 0
    for u in range(n_u):
        starts.append(n)
        n += 2 * (u % NB) + 2
    N_P = n

    plan = [("load", 1, 0)]
    done = 0

    def maxima(pair, half):
        nonlocal done
        while queue:
            u = queue[0][1]
            due = u < n_u and starts[u] - TURN_LEAD <= pair
            if done > cost * (pair + 0.5 * half) / (N_P + LAG) and not due:
                break
            step = queue.pop(0)
            plan.append(step)
            if step[0] == "max":
                done += step[5] + 64

    b = pair = 0
    lows, values = [], []

    def value():
        plan.append(values.pop(0))
        if plan[-1][6] and plan[-1][1] == NB - 1:
            plan.append(("load", 0, 1))

    for u in range(n_u):
        pairs = 2 * (u % NB) + 2
        for p in range(pairs):
            c0 = 2 * P if p == pairs - 1 else 0
            for half in range(2):
                maxima(pair, half)
                plan.append(("score", u, b, 2 * p + half, c0))
                b += 1
            lows.append(("low", u, pair, c0))
            values.append(("value", u, pair, c0, 2 * p, p == 0, p == pairs - 1))
            pair += 1
            if len(lows) > LOW_LAG:
                plan.append(lows.pop(0))
            if len(values) > LAG:
                value()
    plan += lows
    while values:
        maxima(pair, 0)
        value()
        pair += 1
    maxima(2 * pair, 0)
    last = [s for s in plan if s[1] < n_u and s != ("load", 0, 1)]
    return before, plan, last, N_A, b, N_P


def attention_phase(nc, t, kept):
    ctx, sb, ps, sem = open_scope(nc)
    before, plan, last_plan, N_A, N_B, N_P = attention_plan()
    N_U = 2 * NB
    R_MAX = 3 * HD + 2
    R_ALL = R_MAX + 2
    with ctx:
        q = [sb(f"at_q{i}", [R_ALL, S], F32R) for i in range(2)]
        k = [sb(f"at_k{i}", [R_ALL, S], F32R) for i in range(2)]
        v = [sb(f"at_v{i}", [P, NT, 3 * HD], F32R) for i in range(2)]
        ex = sb("at_ex", [P, P_SLOTS, 2, BLK])
        ex_hi = sb("at_ex_hi", [P, P_SLOTS, 2, BLK], F32R)
        ex_lo = sb("at_ex_lo", [P, P_SLOTS, 2, BLK], F32R)
        part_max = sb("at_part_max", [P, TB, S // MAXW])
        neg_max = sb("at_neg_max", [P, TB])
        max_row = sb("at_max_row", [TB, 2, 2, P], F32R)
        out_sb = sb("at_out", [3 * HD, 2, BLK])
        mask_q = sb("at_mask_q", [P, P], BF16)
        mask_k = sb("at_mask_k", [P, 2 * P], BF16)
        ident_b = sb("at_ident_b", [P, P], BF16)
        mask_f = sb("at_mask_f", [P, 3 * P])
        ps_a = [ps(f"at_ps_a{i}", [P, MAXW]) for i in range(2)]
        ps_b = [ps(f"at_ps_b{i}", [P, BLK]) for i in range(3)]
        ps_o = ps("at_ps_o", [P, BLK])

        masks_loaded = sem("at_masks_loaded")
        consts_done = sem("at_consts_done")
        ones_done = sem("at_ones_done")
        loaded = [sem(f"at_loaded{i}") for i in range(2)]
        head_done = [sem(f"at_head_done{i}") for i in range(2)]
        a_done = sem("at_a_done")
        a_free = sem("at_a_free")
        neg_done = sem("at_neg_done")
        row_done = sem("at_row_done")
        row_loaded = [sem(f"at_row_loaded{i}") for i in range(2)]
        b_done = sem("at_b_done")
        b_free = sem("at_b_free")
        hi_done = (sem("at_hi_done_pool"), sem("at_hi_done_act"))
        lo_done = (sem("at_lo_done"), sem("at_lo_done_pool"))
        v_done = sem("at_v_done")
        o_free = sem("at_o_free")
        o_stored = [sem(f"at_o_stored{i}") for i in range(2)]
        passed = sem("at_passed")

        ao = t["att_out"]
        LO_CREDIT = [sum(low_by(p) == by for p in range(P_SLOTS)) for by in range(2)]

        def wait_high(eng, it, pair):
            by = high_by(pair)
            eng.wait_ge(hi_done[by], it * pairs_before(N_P, high_by, by) + pairs_before(pair, high_by, by) + 1)

        def wait_low(eng, it, pair, behind):
            by = low_by(pair)
            eng.wait_ge(lo_done[by], it * pairs_before(N_P, low_by, by) + pairs_before(pair, low_by, by) + 1
                        + (0 if behind else LO_CREDIT[by]))

        def wait_taken(eng, it, pair):
            eng.wait_ge(v_done, it * N_P + pair + 1)

        def exponentials(eng, it, pair):
            eng.wait_ge(b_free, it * N_B + 2 * pair + 2 + 3)

        v_src = t["v_part"].rearrange("(t p) (h n) -> h p t n", p=P, h=H)

        ITS = H // 2 - 1

        with nc.Block() as block:
            @block.scalar
            def _(act):
                act.dma_start(mask_f[:, :], t["masks"]).then_inc(masks_loaded, 16)
                act.sem_inc(b_free, 3)
                act.sem_inc(o_free, 1)

                def work(it, steps):
                    for step in steps:
                        if step[0] == "score":
                            _, u, b, kt, c0 = step
                            pair = b // 2
                            act.wait_ge(b_done, it * N_B + b + 1)
                            if b % 2 == 0:
                                wait_low(act, it, pair, behind=True)
                            act.activation(ex[:, pair % P_SLOTS, b % 2, c0:], ps_b[b % 3][:, c0:],
                                           ACT.Exp).then_inc(b_free, 1)
                        if step[0] == "low" and high_by(step[2]) == 1:
                            _, u, pair, c0 = step
                            s = pair % P_SLOTS
                            exponentials(act, it, pair)
                            wait_taken(act, it, pair)
                            act.activation(ex_hi[:, s, :, c0:], ex[:, s, :, c0:], ACT.Copy).then_inc(hi_done[1], 1)
                        if step[0] == "value" and step[6]:
                            _, u, pair, c0, kt, first, last = step
                            act.wait_ge(v_done, it * N_P + pair + P_SLOTS + 1)
                            act.wait_ge(o_stored[u % 2], it * 16 * NB + 16 * (u // 2) + 16)
                            act.activation(out_sb[:, u % 2], ps_o[0:3 * HD, :], ACT.Copy).then_inc(o_free, 1)

                with act.Fori(0, ITS) as it:
                    work(it, plan)
                work(ITS, last_plan)

            @block.gpsimd
            def _(pool):
                ones = [x for i in range(2) for x in (q[i][3 * HD:R_ALL, :], k[i][3 * HD:R_ALL, :], v[i][:, :, 2 * HD:])]
                for n, x in enumerate(ones):
                    pool.memset(as_f32(x), 1.0).then_inc(ones_done, 1)
                    pool.wait_ge(ones_done, n + 1)
                pool.sem_inc(lo_done[1], LO_CREDIT[1])

                def work(it, steps):
                    for step in steps:
                        if step[0] != "low":
                            continue
                        _, u, pair, c0 = step
                        s = pair % P_SLOTS
                        if high_by(pair) == 0:
                            exponentials(pool, it, pair)
                            wait_taken(pool, it, pair)
                            pool.sem_inc(passed, 1)
                            pool.tensor_scalar(ex_hi[:, s, :, c0:], ex[:, s, :, c0:], 1.0, 1.0,
                                               ALU.mult, ALU.mult).then_inc(hi_done[0], 1)
                        if low_by(pair) == 1:
                            wait_high(pool, it, pair)
                            pool.tensor_tensor(ex_lo[:, s, :, c0:], ex[:, s, :, c0:], as_f32(ex_hi[:, s, :, c0:]),
                                               ALU.subtract).then_inc(lo_done[1], 1)

                with pool.Fori(0, ITS) as it:
                    work(it, plan)
                work(ITS, last_plan)

            @block.vector
            def _(dve):
                dve.wait_ge(masks_loaded, 16)
                dve.tensor_copy(mask_q[:, :], mask_f[:, 0:P]).then_inc(consts_done, 1)
                dve.tensor_copy(mask_k[:, :], mask_f[:, P:]).then_inc(consts_done, 1)
                dve.tensor_copy(ident_b[:, :], kept["ident"][:, :]).then_inc(consts_done, 1)
                dve.sem_inc(a_free, 2)
                dve.sem_inc(lo_done[0], LO_CREDIT[0])
                for i in range(2):
                    dve.sem_inc(row_loaded[i], 32)

                def work(it, steps):
                    for step in steps:
                        if step[0] == "max":
                            _, u, a, i, k0, width = step
                            dve.wait_ge(a_done, it * N_A + a + 1)
                            if k0 == 0 and i % TB == 0:
                                dve.wait_ge(neg_done, it * N_U + u + 1)
                            dve.reduce_max(part_max[:, i % TB, k0 // MAXW:k0 // MAXW + 1], ps_a[a % 2][:, 0:width],
                                           AX.X).then_inc(a_free, 1)
                            if k0 + width == P * (i + 1) and i % TB == TB - 1:
                                dve.wait_ge(a_free, it * N_A + a + 2 + 1)
                                chunks = k0 // MAXW + 1
                                dve.tensor_reduce(neg_max[:, :], part_max[:, :, 0:chunks], AX.X, ALU.max,
                                                  negate=True).then_inc(neg_done, 1)
                        if step[0] == "turn":
                            _, u, a = step
                            dve.wait_ge(a_done, it * N_A + a + 1)
                            dve.wait_ge(row_loaded[u % 2], it * 32 * NB + 32 * (u // 2) + 32)
                            dve.tensor_copy(max_row[:, u % 2, 0], ps_a[a % 2][0:TB, 0:P]).then_inc(row_done, 1)
                            dve.wait_ge(row_done, it * N_U + u + 1)
                            dve.tensor_tensor(max_row[:, u % 2, 1], ps_a[a % 2][0:TB, 0:P],
                                              as_f32(max_row[:, u % 2, 0]), ALU.subtract).then_inc(a_free, 1)
                        if step[0] == "low" and low_by(step[2]) == 0:
                            _, u, pair, c0 = step
                            s = pair % P_SLOTS
                            wait_high(dve, it, pair)
                            dve.tensor_tensor(ex_lo[:, s, :, c0:], ex[:, s, :, c0:], as_f32(ex_hi[:, s, :, c0:]),
                                              ALU.subtract).then_inc(lo_done[0], 1)

                work(0, before)
                with dve.Fori(0, ITS) as it:
                    work(it, plan)
                work(ITS, last_plan)

            @block.sync
            def _(sp):
                for i in range(2):
                    sp.sem_inc(o_stored[i], 16)

                def work(it, steps, first=False):
                    for step in steps:
                        if step[0] == "load":
                            _, i, ahead = step
                            if first:
                                sp.wait_ge(ones_done, 3)
                            else:
                                sp.wait_ge(head_done[i], it + 1)
                            h = 2 * it + 2 * ahead + i
                            for dst, src, order in ((q[i], "q_part", (0, 1, 0)), (k[i], "k_part", (0, 0, 1))):
                                for r, part in enumerate(order):
                                    sp.dma_start(as_f32(dst[r * HD:(r + 1) * HD, :]),
                                                 t[src][part, bass.ds(h * HD, HD), :]).then_inc(loaded[i], 16)
                            sp.dma_start(as_f32(k[i][3 * HD:3 * HD + 2, :]), t["alibi_s"][h]).then_inc(loaded[i], 16)
                            sp.dma_start(as_f32(v[i][:, :, 0:2 * HD]), v_src[h]).then_inc(loaded[i], 16)
                        if step[0] == "turn":
                            _, u, a = step
                            sp.wait_ge(a_free, it * N_A + a + 2 + 1)
                            g, j = u // NB % 2, u % NB
                            for part in range(2):
                                sp.dma_start(as_f32(q[g][R_MAX + part:R_MAX + part + 1, j * BLK:(j + 1) * BLK]),
                                             as_f32(max_row[:, u % 2, part])).then_inc(row_loaded[u % 2], 16)
                        if step[0] == "value" and step[6]:
                            _, u, pair, c0, kt, first_pair, last_pair = step
                            sp.wait_ge(o_free, it * N_U + u + 2)
                            j = u % NB
                            sp.dma_start(ao[2 * it + u // NB, :, j * BLK:(j + 1) * BLK], out_sb[:, u % 2]).then_inc(o_stored[u % 2], 16)

                work(0, before, first=True)
                sp.wait_ge(ones_done, 6)
                with sp.Fori(0, ITS) as it:
                    work(it, plan)
                work(ITS, last_plan)
                for i in range(2):
                    sp.wait_ge(o_stored[i], 16 * NB * (H // 2) + 16)

            @block.tensor
            def _(pe):
                pe.sem_inc(head_done[1], 1)
                pe.sem_inc(v_done, P_SLOTS)
                pe.sem_inc(neg_done, 1)
                pe.wait_ge(ones_done, 6)
                pe.wait_ge(consts_done, 3)
                LOADS = 16 * 8

                def work(it, steps):
                    for step in steps:
                        if step[0] == "max":
                            _, u, a, i, k0, width = step
                            g = u // NB % 2
                            if i == 0:
                                pe.wait_ge(loaded[g], (it + u // N_U) * LOADS + LOADS)
                            pe.wait_ge(a_free, it * N_A + a + 1)
                            for w0 in range(0, width, BLK):
                                w = min(BLK, width - w0)
                                diagonal = k0 + w0 + w == P * (i + 1)
                                mm = pe.matmul(ps_a[a % 2][:, w0:w0 + w], q[g][0:R_MAX, i * P:(i + 1) * P],
                                               k[g][0:R_MAX, k0 + w0:k0 + w0 + w], start=True, stop=not diagonal)
                                if diagonal:
                                    mm = pe.matmul(ps_a[a % 2][:, w0 + w - P:w0 + w], ident_b[:, :], mask_q[:, :],
                                                   start=False, stop=True)
                            mm.then_inc(a_done, 1)
                        if step[0] == "turn":
                            _, u, a = step
                            pe.wait_ge(neg_done, it * N_U + u + 2)
                            pe.wait_ge(a_free, it * N_A + a + 1)
                            pe.transpose(ps_a[a % 2][0:TB, 0:P], neg_max[:, :], kept["ident"][:, :]).then_inc(a_done, 1)
                        if step[0] == "score":
                            _, u, b, kt, c0 = step
                            g, j = u // NB, u % NB
                            if kt == 0:
                                pe.wait_ge(row_loaded[u % 2], it * 32 * NB + 32 * (u // 2) + 64)
                            pe.wait_ge(b_free, it * N_B + b + 1)
                            r = kt - TB * j
                            mm = pe.matmul(ps_b[b % 3][:, c0:], k[g][0:R_ALL, kt * P:(kt + 1) * P],
                                           q[g][0:R_ALL, j * BLK + c0:(j + 1) * BLK], start=True, stop=r < 0)
                            if r >= 0:
                                w = P * (1 + r % 2)
                                mm = pe.matmul(ps_b[b % 3][:, c0:c0 + w], ident_b[:, :], mask_k[:, 2 * P - w:],
                                               start=False, stop=True)
                            mm.then_inc(b_done, 1)
                        if step[0] == "value":
                            _, u, pair, c0, kt, first, last = step
                            g, s = u // NB, pair % P_SLOTS
                            wait_low(pe, it, pair, behind=False)
                            if first:
                                pe.wait_ge(o_free, it * N_U + u + 1)
                            for half in range(2):
                                for x, part in enumerate((ex_hi, ex_lo)):
                                    mm = pe.matmul(ps_o[0:3 * HD, c0:], v[g][:, kt + half, :], part[:, s, half, c0:],
                                                   start=first and half == 0 and x == 0, stop=last and half == 1 and x == 1)
                            mm.then_inc(v_done, 1)
                            if last and u % NB == NB - 1:
                                pe.wait_ge(v_done, it * N_P + pair + P_SLOTS + 1)
                                pe.sem_inc(head_done[g], 1)

                work(0, before)
                with pe.Fori(0, ITS) as it:
                    work(it, plan)
                work(ITS, last_plan)


def routing_phase(nc, t, kept):
    ctx, sb, ps, sem = open_scope(nc)
    WHOLE = [P, NT, E]
    with ctx:
        logits = kept["logits"][:, :, 0:E]
        probs = sb("ro_probs", WHOLE)
        work = sb("ro_work", WHOLE)
        chosen = [sb(f"ro_chosen{k}", WHOLE) for k in range(TOPK)]
        mask = sb("ro_mask", WHOLE)
        before = [sb(f"ro_before{i}", WHOLE) for i in range(2)]
        mask_b = sb("ro_mask_b", WHOLE, BF16)
        before_b = sb("ro_before_b", WHOLE, BF16)
        experts = sb("ro_experts", [P, E])
        upper_f = sb("ro_upper_f", [P, P])
        upper = sb("ro_upper", [P, P], BF16)
        ones_b = sb("ro_ones", [P, P], BF16)
        best = sb("ro_best", [P, NT, 8])
        best_at = sb("ro_best_at", [P, NT, 8], U32)
        at_f = sb("ro_at_f", [P, NT, 8])
        one = sb("ro_one", [P, NT])
        place = sb("ro_place", [P, TOPK, NT])
        late = sb("ro_late", [P, TOPK, NT])
        slot = sb("ro_slot", [P, TOPK, NT])
        first = sb("ro_first", [P, TOPK, NT])
        zeros = sb("ro_zeros", [P, E * CAP // P], I32)
        ps_place = ps("ro_ps_place", [P, NT, E])
        consts = sem("ro_consts")
        chain = sem("ro_chain")
        exp_done = sem("ro_exp_done")
        place_done = sem("ro_place_done")
        zeros_done = sem("ro_zeros_done")
        table_clear = sem("ro_table_clear")
        iotas = sem("ro_iotas")
        counts_ready = sem("ro_counts_ready")
        probs_ready = sem("ro_probs_ready")

        def per_tile(x):
            return x.unsqueeze(2).to_broadcast(WHOLE)

        with nc.Block() as block:
            @block.sync
            def _(sp):
                sp.dma_start(experts[:, :], t["experts"].partition_broadcast(P)).then_inc(consts, 16)
                sp.dma_start(upper_f[:, :], t["upper"]).then_inc(consts, 16)
                sp.wait_ge(zeros_done, 1)
                sp.dma_start(t["slot_token"].rearrange("(p n) a -> p (n a)", p=P), zeros[:, :]).then_inc(table_clear, 16)
                sp.wait_ge(table_clear, 16)

            @block.gpsimd
            def _(pool):
                pool.memset(zeros[:, :], 0).then_inc(zeros_done, 1)
                pool.iota(kept["token"][:, :], pattern=[[P, NT]], base=0, channel_multiplier=1).then_inc(iotas, 1)

            @block.scalar
            def _(act):
                act.wait_ge(probs_ready, 1)
                act.activation(probs[:, :, :], work[:, :, :], ACT.Exp).then_inc(exp_done, 1)
                act.activation(kept["shared_gate"][:, :], kept["logits"][:, :, E], ACT.Sigmoid).then_inc(exp_done, 1)

            @block.tensor
            def _(pe):
                pe.wait_ge(counts_ready, 1)
                half = NT // 2
                for i in range(2):
                    pe.matmul(ps_place[:, i * half:(i + 1) * half], upper[:, :], mask_b[:, i * half:(i + 1) * half],
                              start=True, stop=False)
                    pe.matmul(ps_place[:, i * half:(i + 1) * half], ones_b[:, :], before_b[:, i * half:(i + 1) * half],
                              start=False, stop=True).then_inc(place_done, 1)

            @block.vector
            def _(dve):
                n = [0]

                def link(ins):
                    n[0] += 1
                    ins.then_inc(chain, 1)
                    dve.wait_ge(chain, n[0])

                dve.wait_ge(consts, 32)
                link(dve.tensor_copy(upper[:, :], upper_f[:, :]))
                link(dve.memset(ones_b[:, :], 1.0))
                link(dve.tensor_reduce(one[:, :], logits, AX.X, ALU.max))
                dve.tensor_tensor(work[:, :, :], logits, per_tile(one[:, :]), ALU.subtract).then_inc(probs_ready, 1)
                dve.wait_ge(exp_done, 1)
                link(dve.tensor_reduce(one[:, :], probs[:, :, :], AX.X, ALU.add))
                link(dve.reciprocal(one[:, :], one[:, :]))
                link(dve.tensor_tensor(probs[:, :, :], probs[:, :, :], per_tile(one[:, :]), ALU.mult))
                for i in range(NT):
                    link(dve.max(best[:, i], probs[:, i]))
                    dve.max_index(best_at[:, i], best[:, i], probs[:, i]).then_inc(iotas, 1)
                dve.wait_ge(iotas, NT + 1)
                link(dve.tensor_copy(at_f[:, :, :], best_at[:, :, :]))
                for k in range(TOPK):
                    link(dve.tensor_tensor(chosen[k][:, :, :], experts[:, :].unsqueeze(1).to_broadcast(WHOLE),
                                           per_tile(at_f[:, :, k]), ALU.is_equal))
                link(dve.tensor_tensor(mask[:, :, :], chosen[0][:, :, :], chosen[1][:, :, :], ALU.add))
                link(dve.tensor_tensor(work[:, :, :], chosen[2][:, :, :], chosen[3][:, :, :], ALU.add))
                link(dve.tensor_tensor(mask[:, :, :], mask[:, :, :], work[:, :, :], ALU.add))
                link(dve.tensor_copy(mask_b[:, :, :], mask[:, :, :]))
                link(dve.memset(before[0][:, 0:1], 0.0))
                link(dve.tensor_copy(before[0][:, 1:], mask[:, 0:NT - 1]))
                d, src = 1, 0
                while d < NT:
                    a, b = before[src], before[1 - src]
                    link(dve.tensor_copy(b[:, 0:d], a[:, 0:d]))
                    link(dve.tensor_tensor(b[:, d:], a[:, d:], a[:, 0:NT - d], ALU.add))
                    d, src = 2 * d, 1 - src
                dve.tensor_copy(before_b[:, :, :], before[src][:, :, :]).then_inc(counts_ready, 1)
                dve.wait_ge(place_done, 2)
                for k in range(TOPK):
                    link(dve.tensor_tensor(work[:, :, :], ps_place[:, :, :], chosen[k][:, :, :], ALU.mult))
                    link(dve.tensor_reduce(place[:, k], work[:, :, :], AX.X, ALU.add))
                    link(dve.tensor_scalar(first[:, k], at_f[:, :, k], float(CAP), None, ALU.mult))
                link(dve.tensor_scalar(late[:, :, :], place[:, :, :], float(CAP), None, ALU.is_ge))
                link(dve.tensor_scalar(slot[:, :, :], late[:, :, :], float(1 << 20), None, ALU.mult))
                link(dve.tensor_tensor(slot[:, :, :], slot[:, :, :], place[:, :, :], ALU.add))
                link(dve.tensor_tensor(slot[:, :, :], slot[:, :, :], first[:, :, :], ALU.add))
                link(dve.tensor_copy(kept["scatter_to"][:, :, :], slot[:, :, :]))
                link(dve.tensor_scalar(slot[:, :, :], place[:, :, :], float(CAP - 1), None, ALU.min))
                link(dve.tensor_tensor(slot[:, :, :], slot[:, :, :], first[:, :, :], ALU.add))
                link(dve.tensor_copy(kept["gather_from"][:, :, :], slot[:, :, :]))
                link(dve.tensor_scalar(late[:, :, :], late[:, :, :], -1.0, 1.0, ALU.mult, ALU.add))
                for k in range(TOPK):
                    link(dve.tensor_tensor(kept["weight"][:, k], late[:, k], best[:, :, k], ALU.mult))


def shared_phase(nc, t, kept):
    ctx, sb, ps, sem = open_scope(nc)
    FC = FS // P
    with ctx:
        w_in = sb("sh_w_in", [P, 2, 2, KC, FS], F32R)
        w_out = sb("sh_w_out", [P, 2, FC, D], F32R)
        raw = sb("sh_raw", [P, 2, FS])
        fT = sb("sh_fT", [P, 2, 2, KC, BLK], F32R)
        gate = sb("sh_gate", [P, BLK])
        hid = sb("sh_hid", [P, BLK])
        hid_part = sb("sh_hid_part", [P, 2, 2, BLK], F32R)
        base = sb("sh_base", [P, TB, D])
        idx = [sb(f"sh_idx{k}", [P, 1], U32) for k in range(TOPK)]
        tok = [sb(f"sh_tok{k}", [P, 1], I32) for k in range(TOPK)]
        ps_h = [ps(f"sh_ps_h{i}", [P, 2, BLK]) for i in range(2)]
        ps_y = ps("sh_ps_y", [P, TB, D])
        raw_loaded = [sem(f"sh_raw_loaded{i}") for i in range(2)]
        raw_hi = sem("sh_raw_hi")
        raw_lo = sem("sh_raw_lo")
        f_loaded = [sem(f"sh_f_loaded{i}") for i in range(2)]
        base_loaded = sem("sh_base_loaded")
        h_done = sem("sh_h_done")
        gate_done = sem("sh_gate_done")
        hid_done = sem("sh_hid_done")
        hid_hi = sem("sh_hid_hi")
        hid_lo = sem("sh_hid_lo")
        y_chunk = sem("sh_y_chunk")
        y_taken = sem("sh_y_taken")
        stored = sem("sh_stored")
        idx_set = sem("sh_idx_set")
        scattered = [sem(f"sh_scattered{k}") for k in range(TOPK)]
        base_rows = t["base"].rearrange("(b t p) d -> b p t d", p=P, t=TB)
        pieces = [(raw_s, w_in[:, :, i, c], t[name][c * P:(c + 1) * P, :], FS) for c in range(KC)
                  for i, (name, raw_s) in enumerate((("sw_gate", 0), ("sw_up", 1)))]
        w_down = t["sw_down"].rearrange("(c p) n -> p c n", p=P)
        for c in range(0, FC, 2):
            m = min(2, FC - c)
            pieces.append((c // 2 % 2, w_out[:, :, c:c + m].rearrange("p a c n -> p a (c n)"),
                           w_down[:, c:c + m, :], m * D))
        NPC = len(pieces)

        with nc.Block() as block:
            @block.sync
            def _(sp):
                for n, (s, _, src, width) in enumerate(pieces):
                    if n >= 2:
                        sp.wait_ge(raw_lo, n - 1)
                    dst = raw[:, s, 0:width]
                    if len(src.shape) == 3:
                        dst = dst.rearrange("p (c n) -> p c n", n=D)
                    sp.dma_start(dst, src).then_inc(raw_loaded[s], 16)
                sp.sem_inc(stored, 16)
                with sp.Fori(0, NB // 2) as it:
                    for s in range(2):
                        b = 2 * it + s
                        sp.wait_ge(h_done, it * 2 * FC + s * FC + 1)
                        sp.dma_start(as_f32(fT[:, s]), t["fT_part"][b]).then_inc(f_loaded[s], 16)
                        sp.wait_ge(stored, b * 16 + 16)
                        sp.dma_start(base[:, :], base_rows[b]).then_inc(base_loaded, 16)
                        sp.wait_ge(y_taken, b * TB + TB + TB)
                        sp.dma_start(base_rows[b], base[:, :]).then_inc(stored, 16)
                sp.wait_ge(stored, 16 * NB + 16)

            @block.gpsimd
            def _(pool):
                with pool.Fori(0, NT) as i:
                    for k in range(TOPK):
                        pool.tensor_copy(idx[k][:, :], kept["scatter_to"][:, k, bass.ds(i, 1)]).then_inc(idx_set, 1)
                        pool.tensor_copy(tok[k][:, :], kept["token"][:, bass.ds(i, 1)]).then_inc(idx_set, 1)
                    pool.wait_ge(idx_set, i * 2 * TOPK + 2 * TOPK)
                    pool.sem_inc(kept["passed"], 1)
                    for k in range(TOPK):
                        pool.indirect_dma_start(
                            out=t["slot_token"][:, :], out_offset=bass.IndirectOffsetOnAxis(ap=idx[k][:, 0:1], axis=0),
                            in_=tok[k][:, :], in_offset=None, bounds_check=E * CAP - 1, oob_is_err=False,
                        ).then_inc(scattered[k], 16)
                    for k in range(TOPK):
                        pool.wait_ge(scattered[k], i * 16 + 16)
                    pool.sem_inc(kept["passed"], 1)

            @block.scalar
            def _(act):
                for n, (s, dst, src, width) in enumerate(pieces):
                    act.wait_ge(raw_loaded[s], 16 * (1 + sum(x[0] == s for x in pieces[:n])))
                    act.activation(dst[:, 0], raw[:, s, 0:width], ACT.Copy).then_inc(raw_hi, 1)
                with act.Fori(0, NB // 2) as it:
                    for s in range(2):
                        for f in range(FC):
                            n = s * FC + f
                            act.wait_ge(h_done, it * 2 * FC + n + FC + 1)
                            act.wait_ge(hid_done, it * 2 * FC + n + 1)
                            act.activation(gate[:, :], ps_h[f % 2][:, 0], ACT.Silu).then_inc(gate_done, 1)
                            act.wait_ge(hid_done, it * 2 * FC + n + 2)
                            act.wait_ge(y_chunk, it * 2 * FC + n + 1)
                            act.activation(hid_part[:, n % 2, 0], hid[:, :], ACT.Copy).then_inc(hid_hi, 1)

            @block.vector
            def _(dve):
                for n, (s, dst, src, width) in enumerate(pieces):
                    dve.wait_ge(raw_hi, n + 1)
                    dve.tensor_tensor(dst[:, 1], raw[:, s, 0:width], as_f32(dst[:, 0]), ALU.subtract).then_inc(raw_lo, 1)
                dve.sem_inc(hid_done, 1)
                dve.sem_inc(hid_lo, 1)
                dve.sem_inc(y_taken, TB)
                with dve.Fori(0, NB // 2) as it:
                    for s in range(2):
                        for f in range(FC):
                            n = s * FC + f
                            dve.wait_ge(gate_done, it * 2 * FC + n + 1)
                            dve.wait_ge(hid_lo, it * 2 * FC + n + 1)
                            dve.tensor_tensor(hid[:, :], ps_h[f % 2][:, 1], gate[:, :], ALU.mult).then_inc(hid_done, 1)
                            dve.wait_ge(hid_hi, it * 2 * FC + n + 1)
                            dve.tensor_tensor(hid_part[:, n % 2, 1], hid[:, :], as_f32(hid_part[:, n % 2, 0]),
                                              ALU.subtract).then_inc(hid_lo, 1)
                        b = 2 * it + s
                        dve.wait_ge(base_loaded, b * 16 + 16)
                        dve.wait_ge(y_chunk, it * 2 * FC + s * FC + FC + 2)
                        for k in range(TB):
                            dve.scalar_tensor_tensor(out=base[:, k], in0=ps_y[:, k],
                                                     scalar=kept["shared_gate"][:, bass.ds(b * TB + k, 1)],
                                                     in1=base[:, k], op0=ALU.mult, op1=ALU.add).then_inc(y_taken, 1)

            @block.tensor
            def _(pe):
                pe.wait_ge(raw_lo, NPC)
                pe.sem_inc(h_done, FC)
                pe.sem_inc(y_chunk, 2)

                def down(it, s, f):
                    n = s * FC + f
                    pe.wait_ge(hid_lo, it * 2 * FC + n + 2)
                    if f == 0:
                        pe.wait_ge(y_taken, (2 * it + s) * TB + TB)
                    for k in range(TB):
                        for x, (i, j) in enumerate(THREE):
                            mm = pe.matmul(ps_y[:, k], hid_part[:, n % 2, i, k * P:(k + 1) * P], w_out[:, j, f],
                                           start=f == 0 and x == 0, stop=f == FC - 1 and x == 2)
                    mm.then_inc(y_chunk, 1)

                with pe.Fori(0, NB // 2) as it:
                    for s in range(2):
                        pe.wait_ge(f_loaded[s], 16 * it + 16)
                        for f in range(FC):
                            n = s * FC + f
                            if f >= 2:
                                pe.wait_ge(hid_done, it * 2 * FC + n)
                            for g in range(2):
                                for c in range(KC):
                                    for x, (i, j) in enumerate(THREE):
                                        mm = pe.matmul(ps_h[f % 2][:, g], w_in[:, j, g, c, f * P:(f + 1) * P],
                                                       fT[:, s, i, c], start=c == 0 and x == 0, stop=c == KC - 1 and x == 2)
                            mm.then_inc(h_done, 1)
                            if f >= 1:
                                down(it, s, f - 1)
                        down(it, s, FC - 1)


def expert_phase(nc, t, kept):
    ctx, sb, ps, sem = open_scope(nc)
    SC = CAP // P
    FP = [min(P, F - c) for c in range(0, F, P)]
    FC = len(FP)
    with ctx:
        raw_in = sb("ex_raw_in", [P, 2, KC, F])
        raw_out = sb("ex_raw_out", [P, FC, D])
        w_in = sb("ex_w_in", [P, 2, 2, 2, KC, F], F32R)
        w_out = sb("ex_w_out", [P, 2, 2, FC, D], F32R)
        table = sb("ex_table", [P, E, SC], U32)
        idx = [sb(f"ex_idx{i}", [P, 1], U32) for i in range(2 * SC)]
        x = [sb(f"ex_x{i}", [P, D]) for i in range(2 * SC)]
        xT = sb("ex_xT", [P, 2, KC, CAP], F32R)
        gate = sb("ex_gate", [P, CAP])
        hid = sb("ex_hid", [P, CAP])
        hid_part = sb("ex_hid_part", [P, 2, FC, CAP], F32R)
        y = sb("ex_y", [P, 2, SC, D])
        ps_t = [ps(f"ex_ps_t{i}", [P, KC, P]) for i in range(2)]
        ps_h = [ps(f"ex_ps_h{i}", [P, 2, CAP]) for i in range(2)]
        ps_y = ps("ex_ps_y", [P, SC, D])
        table_loaded = sem("ex_table_loaded")
        in_loaded = sem("ex_in_loaded")
        out_loaded = sem("ex_out_loaded")
        w_hi = sem("ex_w_hi")
        in_lo = sem("ex_in_lo")
        out_lo = sem("ex_out_lo")
        idx_set = sem("ex_idx_set")
        x_loaded = [sem(f"ex_x_loaded{i}") for i in range(2 * SC)]
        turned = sem("ex_turned")
        x_hi = sem("ex_x_hi")
        x_lo = sem("ex_x_lo")
        h_done = sem("ex_h_done")
        gate_done = sem("ex_gate_done")
        hid_done = sem("ex_hid_done")
        hid_hi = sem("ex_hid_hi")
        hid_lo = sem("ex_hid_lo")
        y_done = sem("ex_y_done")
        y_taken = sem("ex_y_taken")
        y_stored = [sem(f"ex_y_stored{i}") for i in range(2)]
        passed = sem("ex_passed")
        y_rows = t["expert_out"].rearrange("(e p c) d -> e p c d", e=E, c=SC)
        w_src = [t[name].rearrange("e (c p) f -> e p c f", p=P) for name in ("w_gate", "w_up")]

        with nc.Block() as block:
            @block.sync
            def _(sp):
                with nc.allow_non_contiguous_dma(reason="32 KB, once"):
                    sp.dma_start(table[:, :, :], t["slot_token"].bitcast(U32).rearrange("(e p c) a -> p e (c a)", e=E, c=SC)).then_inc(table_loaded, 16)
                with sp.Fori(0, E) as e:
                    sp.wait_ge(in_lo, e + 1)
                    sp.wait_ge(w_hi, 2 * e + 2)
                    sp.sem_inc(passed, 1)
                    for g in range(2):
                        sp.dma_start(raw_in[:, g], w_src[g][e]).then_inc(in_loaded, 16)
                    sp.wait_ge(out_lo, e + 1)
                    sp.dma_start(raw_out[:, 0:FC - 1], t["w_down"][e, 0:(FC - 1) * P, :].rearrange("(c p) n -> p c n", p=P)).then_inc(out_loaded, 16)
                    sp.dma_start(raw_out[0:FP[-1], FC - 1], t["w_down"][e, (FC - 1) * P:F, :]).then_inc(out_loaded, 16)

            @block.gpsimd
            def _(pool):
                pool.wait_ge(table_loaded, 16)
                pool.sem_inc(in_lo, 1)
                with pool.Fori(0, E // 2) as it:
                    for i in range(2):
                        e = 2 * it + i
                        for c in range(SC):
                            pool.wait_ge(turned, e * SC + c + 1)
                            pool.tensor_copy(idx[i * SC + c][:, :], table[:, bass.ds(e, 1), c]).then_inc(idx_set, 1)
                            pool.wait_ge(idx_set, e * SC + c + 1)
                            pool.sem_inc(passed, 1)
                            pool.indirect_dma_start(
                                out=x[i * SC + c][:, :], out_offset=None, in_=t["xf"][:, :],
                                in_offset=bass.IndirectOffsetOnAxis(ap=idx[i * SC + c][:, 0:1], axis=0),
                                bounds_check=S - 1, oob_is_err=False,
                            ).then_inc(x_loaded[i * SC + c], 16)
                        pool.wait_ge(w_hi, 2 * e + 3)
                        pool.tensor_tensor(w_in[:, i, 1].rearrange("p g c f -> p (g c f)"),
                                           raw_in[:, :].rearrange("p g c f -> p (g c f)"),
                                           as_f32(w_in[:, i, 0]).rearrange("p g c f -> p (g c f)"),
                                           ALU.subtract).then_inc(in_lo, 1)

            @block.scalar
            def _(act):
                act.sem_inc(w_hi, 2)
                act.sem_inc(y_taken, 1)
                for i in range(2):
                    act.sem_inc(y_stored[i], 16)

                def parts(it, i):
                    e = 2 * it + i
                    act.wait_ge(in_loaded, 32 * e + 32)
                    act.wait_ge(y_done, e + 1)
                    act.activation(w_in[:, i, 0], raw_in[:, :], ACT.Copy).then_inc(w_hi, 1)
                    act.wait_ge(out_loaded, 32 * e + 32)
                    act.activation(w_out[:, i, 0, 0:FC - 1], raw_out[:, 0:FC - 1], ACT.Copy)
                    act.activation(w_out[0:FP[-1], i, 0, FC - 1], raw_out[0:FP[-1], FC - 1], ACT.Copy).then_inc(w_hi, 1)

                with act.Fori(0, E // 2) as it:
                    for i in range(2):
                        e = 2 * it + i
                        parts(it, i)
                        for c in range(SC):
                            act.wait_ge(turned, e * SC + c + 2 * SC + 1)
                            act.wait_ge(h_done, e * FC + FC)
                            act.activation(xT[:, 0, :, c * P:(c + 1) * P], ps_t[c % 2][:, :, :], ACT.Copy).then_inc(x_hi, 1)
                        for f in range(FC):
                            n = i * FC + f
                            act.wait_ge(h_done, it * 2 * FC + n + FC + 1)
                            act.wait_ge(hid_done, it * 2 * FC + n + 1)
                            act.activation(gate[0:FP[f], :], ps_h[n % 2][0:FP[f], 0], ACT.Silu).then_inc(gate_done, 1)
                            act.wait_ge(hid_done, it * 2 * FC + n + 2)
                            act.wait_ge(y_done, e + 2)
                            act.activation(hid_part[0:FP[f], 0, f], hid[0:FP[f], :], ACT.Copy).then_inc(hid_hi, 1)
                        act.wait_ge(y_done, e + 3)
                        act.wait_ge(y_stored[i], 16 * it + 16)
                        act.activation(y[:, i], ps_y[:, :, :], ACT.Copy).then_inc(y_taken, 1)
                        act.wait_ge(y_taken, e + 2)
                        act.dma_start(y_rows[e], y[:, i]).then_inc(y_stored[i], 16)
                for i in range(2):
                    act.wait_ge(y_stored[i], 16 * (E // 2) + 16)

            @block.vector
            def _(dve):
                dve.sem_inc(out_lo, 1)
                dve.sem_inc(hid_done, 1)
                dve.sem_inc(hid_lo, 1)
                dve.sem_inc(x_lo, 2)
                with dve.Fori(0, E // 2) as it:
                    for i in range(2):
                        e = 2 * it + i
                        dve.wait_ge(w_hi, 2 * e + 4)
                        dve.tensor_tensor(w_out[:, i, 1, 0:FC - 1], raw_out[:, 0:FC - 1], as_f32(w_out[:, i, 0, 0:FC - 1]),
                                          ALU.subtract)
                        last = slice(0, FP[-1])
                        dve.tensor_tensor(w_out[last, i, 1, FC - 1], raw_out[last, FC - 1], as_f32(w_out[last, i, 0, FC - 1]),
                                          ALU.subtract).then_inc(out_lo, 1)
                        for c in range(SC):
                            dve.wait_ge(x_hi, e * SC + c + 1)
                            dve.tensor_tensor(xT[:, 1, :, c * P:(c + 1) * P], ps_t[c % 2][:, :, :],
                                              as_f32(xT[:, 0, :, c * P:(c + 1) * P]), ALU.subtract).then_inc(x_lo, 1)
                        for f in range(FC):
                            n = i * FC + f
                            rows = slice(0, FP[f])
                            dve.wait_ge(gate_done, it * 2 * FC + n + 1)
                            dve.wait_ge(hid_lo, it * 2 * FC + n + 1)
                            dve.tensor_tensor(hid[rows, :], ps_h[n % 2][rows, 1], gate[rows, :], ALU.mult).then_inc(hid_done, 1)
                            dve.wait_ge(hid_hi, it * 2 * FC + n + 1)
                            dve.tensor_tensor(hid_part[rows, 1, f], hid[rows, :], as_f32(hid_part[rows, 0, f]),
                                              ALU.subtract).then_inc(hid_lo, 1)

            @block.tensor
            def _(pe):
                pe.sem_inc(turned, 2 * SC)
                pe.sem_inc(h_done, FC)
                pe.sem_inc(y_done, 2)
                with pe.Fori(0, E // 2) as it:
                    for i in range(2):
                        e = 2 * it + i
                        for c in range(SC):
                            pe.wait_ge(x_loaded[i * SC + c], 16 * it + 16)
                            pe.wait_ge(x_lo, e * SC + c + 1)
                            for m in range(KC):
                                mm = pe.transpose(ps_t[c % 2][:, m], x[i * SC + c][:, m * P:(m + 1) * P], kept["ident"][:, :])
                            mm.then_inc(turned, 1)
                        pe.wait_ge(in_lo, e + 2)
                        pe.wait_ge(x_lo, e * SC + SC + 2)
                        for f in range(FC):
                            n = i * FC + f
                            pe.wait_ge(hid_done, it * 2 * FC + max(n, 1))
                            for g in range(2):
                                for c in range(KC):
                                    for m, (a, b) in enumerate(THREE):
                                        mm = pe.matmul(ps_h[n % 2][0:FP[f], g], w_in[:, i, b, g, c, f * P:f * P + FP[f]],
                                                       xT[:, a, c], start=c == 0 and m == 0, stop=c == KC - 1 and m == 2)
                            mm.then_inc(h_done, 1)
                        pe.wait_ge(out_lo, e + 2)
                        pe.wait_ge(hid_lo, it * 2 * FC + i * FC + FC + 1)
                        pe.wait_ge(y_taken, e + 1)
                        for s in range(SC):
                            for f in range(FC):
                                for m, (a, b) in enumerate(THREE):
                                    mm = pe.matmul(ps_y[:, s], hid_part[0:FP[f], a, f, s * P:(s + 1) * P],
                                                   w_out[0:FP[f], i, b, f], start=f == 0 and m == 0,
                                                   stop=f == FC - 1 and m == 2)
                        mm.then_inc(y_done, 1)


def output_phase(nc, t, kept):
    ctx, sb, ps, sem = open_scope(nc)
    with ctx:
        raw = sb("ou_raw", [P, KC, D])
        w = sb("ou_w", [P, 2, KC, D], F32R)
        att = sb("ou_att", [P, 2, 3, BLK])
        z = sb("ou_z", [P, 2, BLK])
        z_part = sb("ou_z_part", [P, 2, KC, BLK], F32R)
        acc = sb("ou_acc", [P, TB, D])
        idx = [sb(f"ou_idx{k}", [P, 1], U32) for k in range(TOPK)]
        ey = [sb(f"ou_ey{k}", [P, D]) for k in range(TOPK)]
        weight = sb("ou_weight", [P, TOPK, TB])
        ps_z = [ps(f"ou_ps{i}", [P, D]) for i in range(2)]
        w_loaded = sem("ou_w_loaded")
        w_hi = sem("ou_w_hi")
        w_lo = sem("ou_w_lo")
        att_loaded = [sem(f"ou_att_loaded{i}") for i in range(2)]
        z_made = sem("ou_z_made")
        chain = sem("ou_chain")
        z_hi = sem("ou_z_hi")
        z_lo = sem("ou_z_lo")
        base_loaded = sem("ou_base_loaded")
        idx_set = sem("ou_idx_set")
        gathered = [sem(f"ou_gathered{k}") for k in range(TOPK)]
        o_done = sem("ou_o_done")
        added = sem("ou_added")
        weight_set = sem("ou_weight_set")
        stored = sem("ou_stored")
        passed = sem("ou_passed")
        base_rows = t["base"].rearrange("(b t p) d -> b p t d", p=P, t=TB)
        out_rows = t["out"].rearrange("a (b t p) d -> (a b) p t d", p=P, t=TB)
        PER = 1 + TOPK

        with nc.Block() as block:
            @block.sync
            def _(sp):
                sp.dma_start(raw[:, :, :], t["wo"].rearrange("(c p) n -> p c n", p=P)).then_inc(w_loaded, 16)
                sp.sem_inc(stored, 16)
                with sp.Fori(0, NB) as b:
                    for c in range(KC):
                        sp.wait_ge(z_made, b * KC + c + 1)
                        for part in range(3):
                            for g in range(HPC):
                                sp.dma_start(att[g * HD:(g + 1) * HD, c % 2, part],
                                             t["att_out"][c * HPC + g, part * HD:(part + 1) * HD, bass.ds(b * BLK, BLK)]).then_inc(att_loaded[c % 2], 16)

            @block.gpsimd
            def _(pool):
                with pool.Fori(0, NT) as i:
                    for k in range(TOPK):
                        pool.wait_ge(added, i * PER + k + 2)
                        pool.tensor_copy(idx[k][:, :], kept["gather_from"][:, k, bass.ds(i, 1)]).then_inc(idx_set, 1)
                        pool.wait_ge(idx_set, i * TOPK + k + 1)
                        pool.sem_inc(passed, 1)
                        pool.indirect_dma_start(
                            out=ey[k][:, :], out_offset=None, in_=t["expert_out"][:, :],
                            in_offset=bass.IndirectOffsetOnAxis(ap=idx[k][:, 0:1], axis=0),
                            bounds_check=E * CAP - 1, oob_is_err=False,
                        ).then_inc(gathered[k], 16)

            @block.scalar
            def _(act):
                act.wait_ge(w_loaded, 16)
                act.activation(w[:, 0], raw[:, :, :], ACT.Copy).then_inc(w_hi, 1)
                with act.Fori(0, NB) as b:
                    act.wait_ge(stored, 16 * b + 16)
                    act.dma_start(acc[:, :], base_rows[b]).then_inc(base_loaded, 16)
                    for c in range(KC):
                        act.wait_ge(z_made, b * KC + c + 3)
                        act.wait_ge(o_done, b * TB + TB)
                        act.activation(z_part[:, 0, c], z[:, c % 2], ACT.Copy).then_inc(z_hi, 1)
                    act.wait_ge(added, (b + 1) * TB * PER + PER)
                    act.dma_start(out_rows[b], acc[:, :]).then_inc(stored, 16)
                act.wait_ge(stored, 16 * NB + 16)

            @block.vector
            def _(dve):
                dve.wait_ge(w_hi, 1)
                dve.tensor_tensor(w[:, 1], raw[:, :, :], as_f32(w[:, 0]), ALU.subtract).then_inc(w_lo, 1)
                dve.sem_inc(z_made, 2)
                dve.sem_inc(z_lo, 2)
                dve.sem_inc(added, PER)
                with dve.Fori(0, NB) as b:
                    def low(c):
                        dve.wait_ge(z_hi, b * KC + c + 1)
                        dve.tensor_tensor(z_part[:, 1, c], z[:, c % 2], as_f32(z_part[:, 0, c]), ALU.subtract).then_inc(z_lo, 1)

                    dve.wait_ge(added, b * TB * PER + PER)
                    dve.tensor_copy(weight[:, :, :], kept["weight"][:, :, bass.ds(b * TB, TB)]).then_inc(weight_set, 1)
                    for c in range(KC):
                        s = c % 2
                        n = b * 3 * KC + 3 * c
                        dve.wait_ge(att_loaded[s], (b * KC // 2 + c // 2 + 1) * 16 * 3 * HPC)
                        dve.reciprocal(att[:, s, 2], att[:, s, 2]).then_inc(chain, 1)
                        dve.tensor_tensor(att[:, s, 0], att[:, s, 0], att[:, s, 1], ALU.add).then_inc(chain, 1)
                        dve.wait_ge(chain, b * 2 * KC + 2 * c + 2)
                        dve.wait_ge(z_lo, b * KC + c + 1)
                        dve.tensor_tensor(z[:, s], att[:, s, 0], att[:, s, 2], ALU.mult).then_inc(z_made, 1)
                        if c >= 1:
                            low(c - 1)
                    low(KC - 1)
                    dve.wait_ge(base_loaded, 16 * b + 16)
                    dve.wait_ge(weight_set, b + 1)
                    for k in range(TB):
                        n = b * TB * PER + k * PER + PER
                        dve.wait_ge(o_done, b * TB + k + TB + 1)
                        dve.tensor_tensor(acc[:, k], ps_z[k % 2][:, :], acc[:, k], ALU.add).then_inc(added, 1)
                        for j in range(TOPK):
                            dve.wait_ge(added, n + j + 1)
                            dve.wait_ge(gathered[j], (b * TB + k + 1) * 16)
                            dve.scalar_tensor_tensor(out=acc[:, k], in0=ey[j][:, :], scalar=weight[:, j, k:k + 1],
                                                     in1=acc[:, k], op0=ALU.mult, op1=ALU.add).then_inc(added, 1)

            @block.tensor
            def _(pe):
                pe.wait_ge(w_lo, 1)
                pe.sem_inc(o_done, TB)
                with pe.Fori(0, NB) as b:
                    pe.wait_ge(z_lo, b * KC + KC + 2)
                    for k in range(TB):
                        pe.wait_ge(added, (b * TB + k) * PER + 1 if k else b * TB * PER + PER)
                        for c in range(KC):
                            for n, (i, j) in enumerate(THREE):
                                mm = pe.matmul(ps_z[k % 2][:, :], z_part[:, i, c, k * P:(k + 1) * P], w[:, j, c],
                                               start=c == 0 and n == 0, stop=c == KC - 1 and n == 2)
                        mm.then_inc(o_done, 1)


def host_constants():
    start = 2.0 ** (-8.0 / H_ALL)
    slopes = np.array([start * start ** i for i in range(H_ALL)], np.float32).astype(np.float64)
    bias = slopes[:, None] * (np.arange(S) - S // 2)[None, :]

    def twelve_bits(x):
        m, e = np.frexp(x)
        return np.ldexp(np.rint(m * 4096) / 4096, e)

    hi = twelve_bits(bias)
    alibi = np.stack([hi, twelve_bits(bias - hi)], axis=1).astype(np.float32)
    row, col = np.arange(P)[:, None], np.arange(P)[None, :]
    masks = np.zeros((P, 3 * P), np.float32)
    masks[:, 0:P][col > row] = MASKED
    masks[:, P:2 * P] = MASKED
    masks[:, 2 * P:][row > col] = MASKED
    return alibi, masks


KEPT = (
    ("ident", [P, P], F32), ("token", [P, NT], I32), ("shared_gate", [P, NT], F32),
    ("scatter_to", [P, TOPK, NT], U32), ("gather_from", [P, TOPK, NT], U32), ("weight", [P, TOPK, NT], F32),
)
PROJECTION = (
    ("w_norm", [P, D], F32), ("bv", [P, D], F32), ("bo", [P, D], F32), ("bqk", [P, 2 * KC], F32),
    ("w_qkv", [P, 2, 3, KC, D], F32R), ("w_r", [P, 2, KC, RW], F32R), ("stat", [P, 3, NT], F32),
)
SCRATCH = (
    ("base", [S, D], F32), ("xf", [S, D], F32), ("fT_part", [NB, P, 2, KC, BLK], F32),
    ("q_part", [2, D, S], F32), ("k_part", [2, D, S], F32), ("v_part", [S, H * 2 * HD], F32),
    ("att_out", [H, 3 * HD, S], F32), ("slot_token", [E * CAP, 1], I32), ("expert_out", [E * CAP, D], F32),
    ("alibi_s", [H, 2, S], F32),
)


def build(nc, t):
    for name, shape, dt in SCRATCH:
        if name not in t:
            t[name] = nc.dram_tensor("scratch_" + name, shape, dt, kind="Internal").ap()
    with ExitStack() as whole:
        kept = {n: whole.enter_context(nc.sbuf_tensor("kept_" + n, shape, dt)) for n, shape, dt in KEPT}
        kept["passed"] = whole.enter_context(nc.semaphore("kept_passed"))
        with ExitStack() as front:
            kept["logits"] = front.enter_context(nc.sbuf_tensor("kept_logits", [P, NT, RW], F32))
            with ExitStack() as projection:
                for n, shape, dt in PROJECTION:
                    kept[n] = projection.enter_context(nc.sbuf_tensor("kept_" + n, shape, dt))
                statistics_phase(nc, t, kept)
                project_phase(nc, t, kept)
            routing_phase(nc, t, kept)
        shared_phase(nc, t, kept)
        attention_phase(nc, t, kept)
        expert_phase(nc, t, kept)
        output_phase(nc, t, kept)


_INS = {
    "L0_attn_x": "x", "L0_attn_wq": "wq", "L0_attn_bq": "bq", "L0_attn_wk": "wk", "L0_attn_bk": "bk",
    "L0_attn_wv": "wv", "L0_attn_bv": "bv", "L0_attn_wo": "wo", "L0_attn_bo": "bo", "L0_ffn_w_norm": "w_norm",
    "L0_ffn_w_router": "w_router", "L0_ffn_w_gate": "w_gate", "L0_ffn_w_up": "w_up", "L0_ffn_w_down": "w_down",
    "L0_ffn_sw_gate": "sw_gate", "L0_ffn_sw_up": "sw_up", "L0_ffn_sw_down": "sw_down",
    "L0_ffn_w_shared_gate": "w_sgate",
}


def kernel(**inputs):
    import numpy as _np
    import concourse.bacc as _bacc
    from concourse.bass_utils import run_bass_kernel_spmd as _run

    nc = _bacc.Bacc("TRN2", target_bir_lowering=False, num_devices=1)
    alibi, masks = host_constants()
    arrays = {name: _np.ascontiguousarray(inputs[long]) for long, name in _INS.items()}
    arrays |= {
        "alibi": alibi, "masks": masks, "ident": _np.eye(P, dtype=_np.float32),
        "upper": _np.triu(_np.ones((P, P), _np.float32), 1), "experts": _np.arange(E, dtype=_np.float32),
    }
    t = {n: nc.dram_tensor(f"in_{n}", a.shape, mybir.dt.from_np(a.dtype), kind="ExternalInput").ap() for n, a in arrays.items()}
    t["out"] = nc.dram_tensor("out_x", (1, S, D), F32, kind="ExternalOutput").ap()
    build(nc, t)
    r = _run(nc, [{f"in_{n}": a for n, a in arrays.items()}], core_ids=[0])
    return r.results[0]["out_x"]
```

```python
from contextlib import ExitStack

import concourse.bass as bass
import numpy as np
from concourse import mybir

ALU = mybir.AluOpType
ACT = mybir.ActivationFunctionType
AX = mybir.AxisListType
F32 = mybir.dt.float32
F32R = mybir.dt.float32r
BF16 = mybir.dt.bfloat16
I32 = mybir.dt.int32
U32 = mybir.dt.uint32

P = 128
S = 4096
D = 512
KC = D // P
H = H_ALL = 16
HD = D // H
E = 32
TOPK = 4
CAP = 256
F = 352
FS = 1408
BLK = 512
NB = S // BLK
TB = BLK // P
NT = S // P
RW = E + 2
HPC = P // HD
LN_EPS = 1e-5
RMS_EPS = 1e-6
Q_SCALE = float(1.0 / np.sqrt(np.float32(HD)))
MASKED = -1e30


THREE = ((0, 0), (0, 1), (1, 0))


def as_f32(ap):
    return ap.bitcast(F32)


def open_scope(nc):
    ctx = ExitStack()

    def sb(name, shape, dt=F32):
        return ctx.enter_context(nc.sbuf_tensor(name, shape, dt))

    def ps(name, shape, dt=F32):
        return ctx.enter_context(nc.psum_tensor(name, shape, dt))

    def sem(name):
        return ctx.enter_context(nc.semaphore(name))

    return ctx, sb, ps, sem


def statistics_phase(nc, t, kept):
    ctx, sb, ps, sem = open_scope(nc)
    PER = 2 * TB
    with ctx:
        x_in = sb("st_x", [P, 2, TB, D])
        six = sb("st_six", [P, PER, 6])
        mean_var = sb("st_mv", [P, PER, 2])
        mv_all = sb("st_mv_all", [P, NT, 2])
        a1 = sb("st_a1", [P, NT])
        a2 = sb("st_a2", [P, NT])
        root = sb("st_root", [P, NT])
        tmp = sb("st_tmp", [P, NT])
        raw = sb("st_raw", [P, 3, KC, D])
        raw_r = sb("st_raw_r", [P, KC, RW])
        x_loaded = [sem("st_x_loaded0"), sem("st_x_loaded1")]
        w_loaded = [sem(f"st_w_loaded{i}") for i in range(4)]
        consts_loaded = sem("st_consts_loaded")
        six_done = sem("st_six_done")
        mv_done = sem("st_mv_done")
        mv_copied = sem("st_mv_copied")
        chain = sem("st_chain")
        root_done = sem("st_root_done")
        hi_done = sem("st_hi_done")
        lo_done = sem("st_lo_done")
        pad_done = sem("st_pad_done")
        passed = sem("st_passed")
        x_rows = t["x"].rearrange("a (b t p) d -> (a b) p t d", p=P, t=TB)

        with nc.Block() as block:
            @block.sync
            def _(sp):
                with sp.Fori(0, NB // 2) as it:
                    for s in range(2):
                        sp.wait_ge(mv_copied, it + 1)
                        sp.dma_start(x_in[:, s], x_rows[2 * it + s]).then_inc(x_loaded[s], 16)

            @block.scalar
            def _(act):
                for i, name in enumerate(("wq", "wk", "wv")):
                    act.dma_start(raw[:, i], t[name].rearrange("(c p) n -> p c n", p=P)).then_inc(w_loaded[i], 16)
                act.wait_ge(pad_done, 1)
                act.dma_start(raw_r[:, :, 0:E], t["w_router"].rearrange("(c p) n -> p c n", p=P)).then_inc(w_loaded[3], 16)
                with nc.allow_non_contiguous_dma(reason="one column, once"):
                    act.dma_start(raw_r[:, :, E:E + 1], t["w_sgate"].rearrange("(c p) n -> p c n", p=P)).then_inc(w_loaded[3], 16)
                act.dma_start(kept["w_norm"][:, :], t["w_norm"].partition_broadcast(P)).then_inc(consts_loaded, 16)
                act.dma_start(kept["bv"][:, :], t["bv"].partition_broadcast(P)).then_inc(consts_loaded, 16)
                act.dma_start(kept["bo"][:, :], t["bo"].partition_broadcast(P)).then_inc(consts_loaded, 16)
                with nc.allow_non_contiguous_dma(reason="2 KB, once"):
                    act.dma_start(kept["bqk"][:, 0:KC], t["bq"].rearrange("(c p) -> p c", p=P)).then_inc(consts_loaded, 16)
                    act.dma_start(kept["bqk"][:, KC:2 * KC], t["bk"].rearrange("(c p) -> p c", p=P)).then_inc(consts_loaded, 16)
                act.dma_start(kept["ident"][:, :], t["ident"]).then_inc(consts_loaded, 16)
                act.wait_ge(chain, 1)
                act.activation(root[:, :], a1[:, :], ACT.Sqrt).then_inc(root_done, 1)
                act.wait_ge(chain, 9)
                act.activation(root[:, :], a2[:, :], ACT.Sqrt).then_inc(root_done, 1)
                for i in range(3):
                    act.wait_ge(w_loaded[i], 16)
                    act.activation(kept["w_qkv"][:, 0, i], raw[:, i], ACT.Copy).then_inc(hi_done, 1)
                act.wait_ge(w_loaded[3], 32)
                act.activation(kept["w_r"][:, 0], raw_r[:, :, :], ACT.Copy).then_inc(hi_done, 1)
                act.dma_start(t["alibi_s"], t["alibi"]).then_inc(consts_loaded, 16)
                act.wait_ge(consts_loaded, 16 * 7)

            @block.gpsimd
            def _(pool):
                pool.memset(raw_r[:, :, E:RW], 0.0).then_inc(pad_done, 1)
                for i in range(3):
                    pool.wait_ge(hi_done, i + 1)
                    pool.tensor_tensor(kept["w_qkv"][:, 1, i], raw[:, i], as_f32(kept["w_qkv"][:, 0, i]),
                                       ALU.subtract).then_inc(lo_done, 1)
                pool.wait_ge(hi_done, 4)
                pool.tensor_tensor(kept["w_r"][:, 1], raw_r[:, :, :], as_f32(kept["w_r"][:, 0]),
                                   ALU.subtract).then_inc(lo_done, 1)

            @block.vector
            def _(dve):
                dve.memset(tmp[:, :], 0.0).then_inc(mv_copied, 1)
                with dve.Fori(0, NB // 2) as it:
                    for s in range(2):
                        dve.wait_ge(x_loaded[s], 16 * it + 16)
                        for k in range(TB):
                            dve.bn_stats(six[:, s * TB + k], x_in[:, s, k]).then_inc(six_done, 1)
                    dve.wait_ge(six_done, it * PER + PER)
                    dve.sem_inc(passed, 1)
                    for k in range(PER):
                        dve.bn_aggr(mean_var[:, k], six[:, k]).then_inc(mv_done, 1)
                    dve.wait_ge(mv_done, it * PER + PER)
                    dve.tensor_copy(mv_all[:, bass.ds(it * PER, PER)], mean_var[:, :]).then_inc(mv_copied, 1)
                    dve.wait_ge(mv_copied, it + 2)
                var = mv_all[:, :, 1]
                n = [0]

                def link(ins):
                    n[0] += 1
                    ins.then_inc(chain, 1)
                    dve.wait_ge(chain, n[0])

                def newton(rstd, a):
                    link(dve.reciprocal(rstd, root[:, :]))
                    link(dve.tensor_tensor(tmp[:, :], rstd, rstd, ALU.mult))
                    link(dve.tensor_tensor(tmp[:, :], tmp[:, :], a, ALU.mult))
                    link(dve.tensor_scalar(tmp[:, :], tmp[:, :], -0.5, 1.5, ALU.mult, ALU.add))
                    link(dve.tensor_tensor(rstd, rstd, tmp[:, :], ALU.mult))

                link(dve.tensor_scalar(a1[:, :], var, LN_EPS, None, ALU.add))
                dve.wait_ge(root_done, 1)
                newton(kept["stat"][:, 1], a1[:, :])
                link(dve.tensor_tensor(tmp[:, :], kept["stat"][:, 1], kept["stat"][:, 1], ALU.mult))
                link(dve.tensor_tensor(tmp[:, :], tmp[:, :], var, ALU.mult))
                link(dve.tensor_scalar(a2[:, :], tmp[:, :], RMS_EPS, None, ALU.add))
                assert n[0] == 9
                dve.wait_ge(root_done, 2)
                newton(kept["stat"][:, 2], a2[:, :])
                link(dve.tensor_copy(kept["stat"][:, 0], mv_all[:, :, 0]))


def project_phase(nc, t, kept):
    ctx, sb, ps, sem = open_scope(nc)
    MQK = 2 * KC
    with ctx:
        x_in = sb("pr_x", [P, TB, D])
        xn = sb("pr_xn", [P, TB, D])
        xf = sb("pr_xf", [P, TB, D])
        base = sb("pr_base", [P, TB, D])
        base0 = sb("pr_base0", [P, TB, D])
        stat = sb("pr_stat", [P, 3, TB])
        xT = sb("pr_xT", [P, 2, KC, BLK], F32R)
        fT = sb("pr_fT", [P, 2, KC, BLK], F32R)
        qk = sb("pr_qk", [P, 2, BLK])
        qk_part = sb("pr_qk_part", [P, 2, MQK, BLK], F32R)
        v = sb("pr_v", [P, 2, D])
        v_part = sb("pr_v_part", [P, TB, H, 2, HD], F32R)
        ps_t = [ps(f"pr_ps_t{i}", [P, KC, P]) for i in range(2)]
        ps_m = [ps(f"pr_ps_m{i}", [P, BLK]) for i in range(3)]
        ps_r = ps("pr_ps_r", [P, TB, RW])

        x_loaded = sem("pr_x_loaded")
        x_used = sem("pr_x_used")
        x_used_pool = sem("pr_x_used_pool")
        stat_set = sem("pr_stat_set")
        xn_done = sem("pr_xn_done")
        xf_done = sem("pr_xf_done")
        sum_done = sem("pr_sum_done")
        base_done = sem("pr_base_done")
        turned = sem("pr_turned")
        turned_hi = sem("pr_turned_hi")
        turned_lo = sem("pr_turned_lo")
        r_done = sem("pr_r_done")
        r_copied = sem("pr_r_copied")
        m_done = sem("pr_m_done")
        m_copied = sem("pr_m_copied")
        m_hi = sem("pr_m_hi")
        m_lo = sem("pr_m_lo")
        rows_stored = sem("pr_rows_stored")
        qkv_stored = sem("pr_qkv_stored")
        passed = sem("pr_passed")
        x_rows = t["x"].rearrange("a (b t p) d -> (a b) p t d", p=P, t=TB)
        base_rows = t["base"].rearrange("(b t p) d -> b p t d", p=P, t=TB)
        xf_rows = t["xf"].rearrange("(b t p) d -> b p t d", p=P, t=TB)
        v_rows = t["v_part"].rearrange("(b t p) n -> b p t n", p=P, t=TB)
        NM = MQK + TB
        NTR = 2 * TB
        STORES = 16 * (2 * MQK + 1)

        with nc.Block() as block:
            @block.sync
            def _(sp):
                sp.sem_inc(rows_stored, 48)
                sp.sem_inc(qkv_stored, STORES)
                with sp.Fori(0, NB) as b:
                    sp.wait_ge(xf_done, b * TB + TB)
                    sp.dma_start(xf_rows[b], xf[:, :]).then_inc(rows_stored, 16)
                    sp.wait_ge(base_done, b * TB + TB)
                    sp.dma_start(base_rows[b], base[:, :]).then_inc(rows_stored, 16)
                    sp.wait_ge(turned_lo, b * NTR + NTR + 2)
                    sp.dma_start(t["fT_part"][b], as_f32(fT[:, :])).then_inc(rows_stored, 16)
                    sp.wait_ge(m_hi, b * NM + NM)
                    sp.wait_ge(m_lo, b * NM + NM)
                    for part in range(2):
                        for m in range(MQK):
                            name, c = ("q_part", m) if m < KC else ("k_part", m - KC)
                            dst = t[name][part, c * P:(c + 1) * P, bass.ds(b * BLK, BLK)]
                            sp.dma_start(dst, as_f32(qk_part[:, part, m])).then_inc(qkv_stored, 16)
                    sp.dma_start(v_rows[b], as_f32(v_part[:, :]).rearrange("p t h a d -> p t (h a d)")).then_inc(qkv_stored, 16)
                sp.wait_ge(rows_stored, 48 * NB + 48)
                sp.wait_ge(qkv_stored, STORES * NB + STORES)

            @block.gpsimd
            def _(pool):
                pool.sem_inc(x_used_pool, 1)
                with pool.Fori(0, NB) as b:
                    pool.wait_ge(x_loaded, 16 * b + 16)
                    for k in range(TB):
                        pool.wait_ge(xn_done, b * TB + k + 1)
                        pool.tensor_tensor(base0[:, k], x_in[:, k], xn[:, k], ALU.add).then_inc(x_used_pool, 1)
                        pool.wait_ge(x_used_pool, b * TB + k + 2)
                        if k == 0:
                            pool.wait_ge(rows_stored, b * 48 + 48)
                        pool.tensor_tensor(base[:, k], base0[:, k], kept["bo"][:, :], ALU.add).then_inc(base_done, 1)
                        pool.wait_ge(base_done, b * TB + k + 1)
                    for m in range(NM):
                        pool.wait_ge(m_copied, b * NM + m + 1)
                        if m == 0:
                            pool.wait_ge(qkv_stored, b * STORES + STORES)
                        if m < MQK:
                            src, dst = qk[:, m % 2], qk_part[:, 0, m]
                        else:
                            src = v[:, m % 2].rearrange("p (h d) -> p h d", h=H)
                            dst = v_part[:, m - MQK, :, 0, :]
                        pool.sem_inc(passed, 1)
                        pool.tensor_scalar(dst, src, 1.0, 1.0, ALU.mult, ALU.mult).then_inc(m_hi, 1)

            @block.scalar
            def _(act):
                with act.Fori(0, NB) as b:
                    act.wait_ge(x_used, b * TB + 1)
                    act.wait_ge(x_used_pool, b * TB + 1)
                    act.dma_start(x_in[:, :], x_rows[b]).then_inc(x_loaded, 16)
                    act.wait_ge(m_done, b * NM + NM)
                    act.wait_ge(rows_stored, b * 48 + 48)
                    for i in range(NTR):
                        k = i // 2
                        dst = (xT, fT)[i % 2]
                        act.wait_ge(turned, b * NTR + NTR + i + 1)
                        act.activation(dst[:, 0, :, k * P:(k + 1) * P], ps_t[i % 2][:, :, :], ACT.Copy).then_inc(turned_hi, 1)
                    act.wait_ge(r_done, b + 1)
                    act.activation(kept["logits"][:, bass.ds(b * TB, TB)], ps_r[:, :, :], ACT.Copy).then_inc(r_copied, 1)

            @block.vector
            def _(dve):
                dve.sem_inc(x_used, 1)
                dve.sem_inc(turned_lo, 2)
                with dve.Fori(0, NB) as b:
                    dve.wait_ge(x_used, b * TB + 1)
                    dve.tensor_copy(stat[:, :, :], kept["stat"][:, :, bass.ds(b * TB, TB)]).then_inc(stat_set, 1)
                    dve.wait_ge(stat_set, b + 1)
                    dve.wait_ge(x_loaded, 16 * b + 16)
                    for k in range(TB):
                        if k == 0:
                            dve.wait_ge(turned, b * NTR + NTR)
                            dve.wait_ge(x_used_pool, b * TB + 1)
                            dve.wait_ge(rows_stored, b * 48 + 48)
                        dve.tensor_scalar(xn[:, k], x_in[:, k], stat[:, 0, k:k + 1], stat[:, 1, k:k + 1],
                                          ALU.subtract, ALU.mult).then_inc(xn_done, 1)
                        dve.wait_ge(xn_done, b * TB + k + 1)
                        dve.scalar_tensor_tensor(out=xf[:, k], in0=xn[:, k], scalar=stat[:, 2, k:k + 1],
                                                 in1=kept["w_norm"][:, :], op0=ALU.mult, op1=ALU.mult).then_inc(xf_done, 1)
                        dve.wait_ge(xf_done, b * TB + k + 1)
                        dve.sem_inc(x_used, 1)
                    for i in range(NTR):
                        k = i // 2
                        dst = (xT, fT)[i % 2]
                        dve.wait_ge(turned_hi, b * NTR + i + 1)
                        dve.tensor_tensor(dst[:, 1, :, k * P:(k + 1) * P], ps_t[i % 2][:, :, :],
                                          as_f32(dst[:, 0, :, k * P:(k + 1) * P]), ALU.subtract).then_inc(turned_lo, 1)

                    def low(m):
                        dve.wait_ge(m_hi, b * NM + m + 1)
                        if m < MQK:
                            dve.tensor_tensor(qk_part[:, 1, m], qk[:, m % 2], as_f32(qk_part[:, 0, m]),
                                              ALU.subtract).then_inc(m_lo, 1)
                        else:
                            dve.tensor_tensor(v_part[:, m - MQK, :, 1, :], v[:, m % 2].rearrange("p (h d) -> p h d", h=H),
                                              as_f32(v_part[:, m - MQK, :, 0, :]), ALU.subtract).then_inc(m_lo, 1)

                    for m in range(NM):
                        dve.wait_ge(m_done, b * NM + NM + m + 1)
                        if m >= 2:
                            dve.wait_ge(m_lo, b * NM + m - 1)
                        if m < KC:
                            dve.tensor_scalar(qk[:, m % 2], ps_m[m % 3][:, :], kept["bqk"][:, m:m + 1], Q_SCALE,
                                              ALU.add, ALU.mult).then_inc(m_copied, 1)
                        elif m < MQK:
                            dve.tensor_scalar(qk[:, m % 2], ps_m[m % 3][:, :], kept["bqk"][:, m:m + 1], None,
                                              ALU.add).then_inc(m_copied, 1)
                        else:
                            dve.tensor_tensor(v[:, m % 2], ps_m[m % 3][:, :], kept["bv"][:, :], ALU.add).then_inc(m_copied, 1)
                        if m >= 1:
                            low(m - 1)
                    low(NM - 1)
                    dve.wait_ge(m_lo, b * NM + NM)

            @block.tensor
            def _(pe):
                pe.sem_inc(turned, NTR)
                pe.sem_inc(m_done, NM)
                with pe.Fori(0, NB) as b:
                    for i in range(NTR):
                        k = i // 2
                        src, ready = ((xn, xn_done), (xf, xf_done))[i % 2]
                        pe.wait_ge(ready, b * TB + k + 1)
                        pe.wait_ge(turned_lo, b * NTR + i + 1)
                        for c in range(KC):
                            mm = pe.transpose(ps_t[i % 2][:, c], src[:, k, c * P:(c + 1) * P], kept["ident"][:, :])
                        mm.then_inc(turned, 1)
                    pe.wait_ge(turned_lo, b * NTR + NTR + 2)
                    for k in range(TB):
                        for c in range(KC):
                            for n, (i, j) in enumerate(THREE):
                                mm = pe.matmul(ps_r[:, k], fT[:, i, c, k * P:(k + 1) * P], kept["w_r"][:, j, c],
                                               start=(c == 0 and n == 0), stop=(c == KC - 1 and n == 2))
                    mm.then_inc(r_done, 1)
                    for m in range(NM):
                        if m >= 3:
                            pe.wait_ge(m_copied, b * NM + m - 2)
                        for c in range(KC):
                            for n, (i, j) in enumerate(THREE):
                                if m < MQK:
                                    w = kept["w_qkv"][:, j, m // KC, c, (m % KC) * P:(m % KC + 1) * P]
                                    args = (w, xT[:, i, c])
                                else:
                                    k = m - MQK
                                    args = (xT[:, i, c, k * P:(k + 1) * P], kept["w_qkv"][:, j, 2, c])
                                mm = pe.matmul(ps_m[m % 3][:, :], *args, start=(c == 0 and n == 0),
                                               stop=(c == KC - 1 and n == 2))
                        mm.then_inc(m_done, 1)
                    pe.wait_ge(m_copied, b * NM + NM)
                    pe.wait_ge(r_copied, b + 1)


MAXW = 1024
WRAP = 4
TURN_LEAD = 3
LOW_LAG = 2
LAG = 4
P_SLOTS = 6
POOL_LOWS = (2, 5)
ACT_HIGHS = (1, 4)


def high_by(pair):
    return int(pair % P_SLOTS in ACT_HIGHS)


def low_by(pair):
    return int(pair % P_SLOTS in POOL_LOWS)


def pairs_before(pair, maker, by):
    return sum(maker(p) == by for p in range(pair))


def attention_plan():
    n_u, stream, turn = 2 * NB, [], None
    for u in range(n_u):
        j = u % NB
        for i in range(TB * j, TB * j + TB):
            for k0 in range(0, P * (i + 1), MAXW):
                stream.append(["max", u, 0, i, k0, min(MAXW, P * (i + 1) - k0)])
                if turn:
                    stream.append(turn)
                    turn = None
        turn = ["turn", u, 0]
        if u in (WRAP - 1, n_u - 1):
            stream.append(turn)
            turn = None
    for a, step in enumerate(stream):
        step[2] = a
    N_A = len(stream)
    ahead = 1 + [s[:2] for s in stream].index(["turn", WRAP - 1])
    before = [("load", 0, 0)] + [tuple(s) for s in stream[:ahead]]
    queue = [tuple(s) for s in stream[ahead:]]
    queue += [(s[0], s[1] + n_u, s[2] + N_A, *s[3:]) for s in stream[:ahead]]
    cost = sum(s[5] + 64 for s in stream if s[0] == "max")
    starts, n = [], 0
    for u in range(n_u):
        starts.append(n)
        n += 2 * (u % NB) + 2
    N_P = n

    plan = [("load", 1, 0)]
    done = 0

    def maxima(pair, half):
        nonlocal done
        while queue:
            u = queue[0][1]
            due = u < n_u and starts[u] - TURN_LEAD <= pair
            if done > cost * (pair + 0.5 * half) / (N_P + LAG) and not due:
                break
            step = queue.pop(0)
            plan.append(step)
            if step[0] == "max":
                done += step[5] + 64

    b = pair = 0
    lows, values = [], []

    def value():
        plan.append(values.pop(0))
        if plan[-1][6] and plan[-1][1] == NB - 1:
            plan.append(("load", 0, 1))

    for u in range(n_u):
        pairs = 2 * (u % NB) + 2
        for p in range(pairs):
            c0 = 2 * P if p == pairs - 1 else 0
            for half in range(2):
                maxima(pair, half)
                plan.append(("score", u, b, 2 * p + half, c0))
                b += 1
            lows.append(("low", u, pair, c0))
            values.append(("value", u, pair, c0, 2 * p, p == 0, p == pairs - 1))
            pair += 1
            if len(lows) > LOW_LAG:
                plan.append(lows.pop(0))
            if len(values) > LAG:
                value()
    plan += lows
    while values:
        maxima(pair, 0)
        value()
        pair += 1
    maxima(2 * pair, 0)
    last = [s for s in plan if s[1] < n_u and s != ("load", 0, 1)]
    return before, plan, last, N_A, b, N_P


def attention_phase(nc, t, kept):
    ctx, sb, ps, sem = open_scope(nc)
    before, plan, last_plan, N_A, N_B, N_P = attention_plan()
    N_U = 2 * NB
    R_MAX = 3 * HD + 2
    R_ALL = R_MAX + 2
    with ctx:
        q = [sb(f"at_q{i}", [R_ALL, S], F32R) for i in range(2)]
        k = [sb(f"at_k{i}", [R_ALL, S], F32R) for i in range(2)]
        v = [sb(f"at_v{i}", [P, NT, 3 * HD], F32R) for i in range(2)]
        ex = sb("at_ex", [P, P_SLOTS, 2, BLK])
        ex_hi = sb("at_ex_hi", [P, P_SLOTS, 2, BLK], F32R)
        ex_lo = sb("at_ex_lo", [P, P_SLOTS, 2, BLK], F32R)
        part_max = sb("at_part_max", [P, TB, S // MAXW])
        neg_max = sb("at_neg_max", [P, TB])
        max_row = sb("at_max_row", [TB, 2, 2, P], F32R)
        out_sb = sb("at_out", [3 * HD, 2, BLK])
        mask_q = sb("at_mask_q", [P, P], BF16)
        mask_k = sb("at_mask_k", [P, 2 * P], BF16)
        ident_b = sb("at_ident_b", [P, P], BF16)
        mask_f = sb("at_mask_f", [P, 3 * P])
        ps_a = [ps(f"at_ps_a{i}", [P, MAXW]) for i in range(2)]
        ps_b = [ps(f"at_ps_b{i}", [P, BLK]) for i in range(3)]
        ps_o = ps("at_ps_o", [P, BLK])

        masks_loaded = sem("at_masks_loaded")
        consts_done = sem("at_consts_done")
        ones_done = sem("at_ones_done")
        loaded = [sem(f"at_loaded{i}") for i in range(2)]
        head_done = [sem(f"at_head_done{i}") for i in range(2)]
        a_done = sem("at_a_done")
        a_free = sem("at_a_free")
        neg_done = sem("at_neg_done")
        row_done = sem("at_row_done")
        row_loaded = [sem(f"at_row_loaded{i}") for i in range(2)]
        b_done = sem("at_b_done")
        b_free = sem("at_b_free")
        hi_done = (sem("at_hi_done_pool"), sem("at_hi_done_act"))
        lo_done = (sem("at_lo_done"), sem("at_lo_done_pool"))
        v_done = sem("at_v_done")
        o_free = sem("at_o_free")
        o_stored = [sem(f"at_o_stored{i}") for i in range(2)]
        passed = sem("at_passed")

        STORE = 16 * 3
        LO_CREDIT = [sum(low_by(p) == by for p in range(P_SLOTS)) for by in range(2)]

        def wait_high(eng, it, pair):
            by = high_by(pair)
            eng.wait_ge(hi_done[by], it * pairs_before(N_P, high_by, by) + pairs_before(pair, high_by, by) + 1)

        def wait_low(eng, it, pair, behind):
            by = low_by(pair)
            eng.wait_ge(lo_done[by], it * pairs_before(N_P, low_by, by) + pairs_before(pair, low_by, by) + 1
                        + (0 if behind else LO_CREDIT[by]))

        def wait_taken(eng, it, pair):
            eng.wait_ge(v_done, it * N_P + pair + 1)

        def exponentials(eng, it, pair):
            eng.wait_ge(b_free, it * N_B + 2 * pair + 2 + 3)

        v_src = t["v_part"].rearrange("(t p) (h n) -> h p t n", p=P, h=H)

        ITS = H // 2 - 1

        with nc.Block() as block:
            @block.scalar
            def _(act):
                act.dma_start(mask_f[:, :], t["masks"]).then_inc(masks_loaded, 16)
                act.sem_inc(b_free, 3)
                act.sem_inc(o_free, 1)

                def work(it, steps):
                    for step in steps:
                        if step[0] == "score":
                            _, u, b, kt, c0 = step
                            pair = b // 2
                            act.wait_ge(b_done, it * N_B + b + 1)
                            if b % 2 == 0:
                                wait_low(act, it, pair, behind=True)
                            act.activation(ex[:, pair % P_SLOTS, b % 2, c0:], ps_b[b % 3][:, c0:],
                                           ACT.Exp).then_inc(b_free, 1)
                        if step[0] == "low" and high_by(step[2]) == 1:
                            _, u, pair, c0 = step
                            s = pair % P_SLOTS
                            exponentials(act, it, pair)
                            wait_taken(act, it, pair)
                            act.activation(ex_hi[:, s, :, c0:], ex[:, s, :, c0:], ACT.Copy).then_inc(hi_done[1], 1)
                        if step[0] == "value" and step[6]:
                            _, u, pair, c0, kt, first, last = step
                            act.wait_ge(v_done, it * N_P + pair + P_SLOTS + 1)
                            act.wait_ge(o_stored[u % 2], it * STORE * NB + STORE * (u // 2) + STORE)
                            act.activation(out_sb[:, u % 2], ps_o[0:3 * HD, :], ACT.Copy).then_inc(o_free, 1)

                with act.Fori(0, ITS) as it:
                    work(it, plan)
                work(ITS, last_plan)

            @block.gpsimd
            def _(pool):
                ones = [x for i in range(2) for x in (q[i][3 * HD:R_ALL, :], k[i][3 * HD:R_ALL, :], v[i][:, :, 2 * HD:])]
                for n, x in enumerate(ones):
                    pool.memset(as_f32(x), 1.0).then_inc(ones_done, 1)
                    pool.wait_ge(ones_done, n + 1)
                pool.sem_inc(lo_done[1], LO_CREDIT[1])

                def work(it, steps):
                    for step in steps:
                        if step[0] != "low":
                            continue
                        _, u, pair, c0 = step
                        s = pair % P_SLOTS
                        if high_by(pair) == 0:
                            exponentials(pool, it, pair)
                            wait_taken(pool, it, pair)
                            pool.sem_inc(passed, 1)
                            pool.tensor_scalar(ex_hi[:, s, :, c0:], ex[:, s, :, c0:], 1.0, 1.0,
                                               ALU.mult, ALU.mult).then_inc(hi_done[0], 1)
                        if low_by(pair) == 1:
                            wait_high(pool, it, pair)
                            pool.tensor_tensor(ex_lo[:, s, :, c0:], ex[:, s, :, c0:], as_f32(ex_hi[:, s, :, c0:]),
                                               ALU.subtract).then_inc(lo_done[1], 1)

                with pool.Fori(0, ITS) as it:
                    work(it, plan)
                work(ITS, last_plan)

            @block.vector
            def _(dve):
                dve.wait_ge(masks_loaded, 16)
                dve.tensor_copy(mask_q[:, :], mask_f[:, 0:P]).then_inc(consts_done, 1)
                dve.tensor_copy(mask_k[:, :], mask_f[:, P:]).then_inc(consts_done, 1)
                dve.tensor_copy(ident_b[:, :], kept["ident"][:, :]).then_inc(consts_done, 1)
                dve.sem_inc(a_free, 2)
                dve.sem_inc(lo_done[0], LO_CREDIT[0])
                for i in range(2):
                    dve.sem_inc(row_loaded[i], 32)

                def work(it, steps):
                    for step in steps:
                        if step[0] == "max":
                            _, u, a, i, k0, width = step
                            dve.wait_ge(a_done, it * N_A + a + 1)
                            if k0 == 0 and i % TB == 0:
                                dve.wait_ge(neg_done, it * N_U + u + 1)
                            dve.reduce_max(part_max[:, i % TB, k0 // MAXW:k0 // MAXW + 1], ps_a[a % 2][:, 0:width],
                                           AX.X).then_inc(a_free, 1)
                            if k0 + width == P * (i + 1) and i % TB == TB - 1:
                                dve.wait_ge(a_free, it * N_A + a + 2 + 1)
                                chunks = k0 // MAXW + 1
                                dve.tensor_reduce(neg_max[:, :], part_max[:, :, 0:chunks], AX.X, ALU.max,
                                                  negate=True).then_inc(neg_done, 1)
                        if step[0] == "turn":
                            _, u, a = step
                            dve.wait_ge(a_done, it * N_A + a + 1)
                            dve.wait_ge(row_loaded[u % 2], it * 32 * NB + 32 * (u // 2) + 32)
                            dve.tensor_copy(max_row[:, u % 2, 0], ps_a[a % 2][0:TB, 0:P]).then_inc(row_done, 1)
                            dve.wait_ge(row_done, it * N_U + u + 1)
                            dve.tensor_tensor(max_row[:, u % 2, 1], ps_a[a % 2][0:TB, 0:P],
                                              as_f32(max_row[:, u % 2, 0]), ALU.subtract).then_inc(a_free, 1)
                        if step[0] == "low" and low_by(step[2]) == 0:
                            _, u, pair, c0 = step
                            s = pair % P_SLOTS
                            wait_high(dve, it, pair)
                            dve.tensor_tensor(ex_lo[:, s, :, c0:], ex[:, s, :, c0:], as_f32(ex_hi[:, s, :, c0:]),
                                              ALU.subtract).then_inc(lo_done[0], 1)

                work(0, before)
                with dve.Fori(0, ITS) as it:
                    work(it, plan)
                work(ITS, last_plan)

            @block.sync
            def _(sp):
                for i in range(2):
                    sp.sem_inc(o_stored[i], STORE)

                def work(it, steps, first=False):
                    for step in steps:
                        if step[0] == "load":
                            _, i, ahead = step
                            if first:
                                sp.wait_ge(ones_done, 3)
                            else:
                                sp.wait_ge(head_done[i], it + 1)
                            h = 2 * it + 2 * ahead + i
                            for dst, src, order in ((q[i], "q_part", (0, 1, 0)), (k[i], "k_part", (0, 0, 1))):
                                for r, part in enumerate(order):
                                    sp.dma_start(as_f32(dst[r * HD:(r + 1) * HD, :]),
                                                 t[src][part, bass.ds(h * HD, HD), :]).then_inc(loaded[i], 16)
                            sp.dma_start(as_f32(k[i][3 * HD:3 * HD + 2, :]), t["alibi_s"][h]).then_inc(loaded[i], 16)
                            sp.dma_start(as_f32(v[i][:, :, 0:2 * HD]), v_src[h]).then_inc(loaded[i], 16)
                        if step[0] == "turn":
                            _, u, a = step
                            sp.wait_ge(a_free, it * N_A + a + 2 + 1)
                            g, j = u // NB % 2, u % NB
                            for part in range(2):
                                sp.dma_start(as_f32(q[g][R_MAX + part:R_MAX + part + 1, j * BLK:(j + 1) * BLK]),
                                             as_f32(max_row[:, u % 2, part])).then_inc(row_loaded[u % 2], 16)
                        if step[0] == "value" and step[6]:
                            _, u, pair, c0, kt, first_pair, last_pair = step
                            sp.wait_ge(o_free, it * N_U + u + 2)
                            j = u % NB
                            h, cols = 2 * it + u // NB, slice(j * BLK, (j + 1) * BLK)
                            for part in range(2):
                                sp.dma_start(t["att_v"][part, bass.ds(h * HD, HD), cols],
                                             out_sb[part * HD:(part + 1) * HD, u % 2]).then_inc(o_stored[u % 2], 16)
                            sp.dma_start(t["att_sum"][bass.ds(h, 1), cols], out_sb[2 * HD:2 * HD + 1, u % 2]).then_inc(o_stored[u % 2], 16)

                work(0, before, first=True)
                sp.wait_ge(ones_done, 6)
                with sp.Fori(0, ITS) as it:
                    work(it, plan)
                work(ITS, last_plan)
                for i in range(2):
                    sp.wait_ge(o_stored[i], STORE * NB * (H // 2) + STORE)

            @block.tensor
            def _(pe):
                pe.sem_inc(head_done[1], 1)
                pe.sem_inc(v_done, P_SLOTS)
                pe.sem_inc(neg_done, 1)
                pe.wait_ge(ones_done, 6)
                pe.wait_ge(consts_done, 3)
                LOADS = 16 * 8

                def work(it, steps):
                    for step in steps:
                        if step[0] == "max":
                            _, u, a, i, k0, width = step
                            g = u // NB % 2
                            if i == 0:
                                pe.wait_ge(loaded[g], (it + u // N_U) * LOADS + LOADS)
                            pe.wait_ge(a_free, it * N_A + a + 1)
                            for w0 in range(0, width, BLK):
                                w = min(BLK, width - w0)
                                diagonal = k0 + w0 + w == P * (i + 1)
                                mm = pe.matmul(ps_a[a % 2][:, w0:w0 + w], q[g][0:R_MAX, i * P:(i + 1) * P],
                                               k[g][0:R_MAX, k0 + w0:k0 + w0 + w], start=True, stop=not diagonal)
                                if diagonal:
                                    mm = pe.matmul(ps_a[a % 2][:, w0 + w - P:w0 + w], ident_b[:, :], mask_q[:, :],
                                                   start=False, stop=True)
                            mm.then_inc(a_done, 1)
                        if step[0] == "turn":
                            _, u, a = step
                            pe.wait_ge(neg_done, it * N_U + u + 2)
                            pe.wait_ge(a_free, it * N_A + a + 1)
                            pe.transpose(ps_a[a % 2][0:TB, 0:P], neg_max[:, :], kept["ident"][:, :]).then_inc(a_done, 1)
                        if step[0] == "score":
                            _, u, b, kt, c0 = step
                            g, j = u // NB, u % NB
                            if kt == 0:
                                pe.wait_ge(row_loaded[u % 2], it * 32 * NB + 32 * (u // 2) + 64)
                            pe.wait_ge(b_free, it * N_B + b + 1)
                            r = kt - TB * j
                            mm = pe.matmul(ps_b[b % 3][:, c0:], k[g][0:R_ALL, kt * P:(kt + 1) * P],
                                           q[g][0:R_ALL, j * BLK + c0:(j + 1) * BLK], start=True, stop=r < 0)
                            if r >= 0:
                                w = P * (1 + r % 2)
                                mm = pe.matmul(ps_b[b % 3][:, c0:c0 + w], ident_b[:, :], mask_k[:, 2 * P - w:],
                                               start=False, stop=True)
                            mm.then_inc(b_done, 1)
                        if step[0] == "value":
                            _, u, pair, c0, kt, first, last = step
                            g, s = u // NB, pair % P_SLOTS
                            wait_low(pe, it, pair, behind=False)
                            if first:
                                pe.wait_ge(o_free, it * N_U + u + 1)
                            for half in range(2):
                                for x, part in enumerate((ex_hi, ex_lo)):
                                    mm = pe.matmul(ps_o[0:3 * HD, c0:], v[g][:, kt + half, :], part[:, s, half, c0:],
                                                   start=first and half == 0 and x == 0, stop=last and half == 1 and x == 1)
                            mm.then_inc(v_done, 1)
                            if last and u % NB == NB - 1:
                                pe.wait_ge(v_done, it * N_P + pair + P_SLOTS + 1)
                                pe.sem_inc(head_done[g], 1)

                work(0, before)
                with pe.Fori(0, ITS) as it:
                    work(it, plan)
                work(ITS, last_plan)


def routing_phase(nc, t, kept):
    ctx, sb, ps, sem = open_scope(nc)
    WHOLE = [P, NT, E]
    with ctx:
        logits = kept["logits"][:, :, 0:E]
        probs = sb("ro_probs", WHOLE)
        work = sb("ro_work", WHOLE)
        chosen = [sb(f"ro_chosen{k}", WHOLE) for k in range(TOPK)]
        mask = sb("ro_mask", WHOLE)
        before = [sb(f"ro_before{i}", WHOLE) for i in range(2)]
        mask_b = sb("ro_mask_b", WHOLE, BF16)
        before_b = sb("ro_before_b", WHOLE, BF16)
        experts = sb("ro_experts", [P, E])
        upper_f = sb("ro_upper_f", [P, P])
        upper = sb("ro_upper", [P, P], BF16)
        ones_b = sb("ro_ones", [P, P], BF16)
        best = sb("ro_best", [P, NT, 8])
        best_at = sb("ro_best_at", [P, NT, 8], U32)
        at_f = sb("ro_at_f", [P, NT, 8])
        one = sb("ro_one", [P, NT])
        place = sb("ro_place", [P, TOPK, NT])
        late = sb("ro_late", [P, TOPK, NT])
        slot = sb("ro_slot", [P, TOPK, NT])
        first = sb("ro_first", [P, TOPK, NT])
        zeros = sb("ro_zeros", [P, E * CAP // P], I32)
        ps_place = ps("ro_ps_place", [P, NT, E])
        consts = sem("ro_consts")
        chain = sem("ro_chain")
        exp_done = sem("ro_exp_done")
        place_done = sem("ro_place_done")
        zeros_done = sem("ro_zeros_done")
        table_clear = sem("ro_table_clear")
        iotas = sem("ro_iotas")
        counts_ready = sem("ro_counts_ready")
        probs_ready = sem("ro_probs_ready")

        def per_tile(x):
            return x.unsqueeze(2).to_broadcast(WHOLE)

        with nc.Block() as block:
            @block.sync
            def _(sp):
                sp.dma_start(experts[:, :], t["experts"].partition_broadcast(P)).then_inc(consts, 16)
                sp.dma_start(upper_f[:, :], t["upper"]).then_inc(consts, 16)
                sp.wait_ge(zeros_done, 1)
                sp.dma_start(t["slot_token"].rearrange("(p n) a -> p (n a)", p=P), zeros[:, :]).then_inc(table_clear, 16)
                sp.wait_ge(table_clear, 16)

            @block.gpsimd
            def _(pool):
                pool.memset(zeros[:, :], 0).then_inc(zeros_done, 1)
                pool.iota(kept["token"][:, :], pattern=[[P, NT]], base=0, channel_multiplier=1).then_inc(iotas, 1)

            @block.scalar
            def _(act):
                act.wait_ge(probs_ready, 1)
                act.activation(probs[:, :, :], work[:, :, :], ACT.Exp).then_inc(exp_done, 1)
                act.activation(kept["shared_gate"][:, :], kept["logits"][:, :, E], ACT.Sigmoid).then_inc(exp_done, 1)

            @block.tensor
            def _(pe):
                pe.wait_ge(counts_ready, 1)
                half = NT // 2
                for i in range(2):
                    pe.matmul(ps_place[:, i * half:(i + 1) * half], upper[:, :], mask_b[:, i * half:(i + 1) * half],
                              start=True, stop=False)
                    pe.matmul(ps_place[:, i * half:(i + 1) * half], ones_b[:, :], before_b[:, i * half:(i + 1) * half],
                              start=False, stop=True).then_inc(place_done, 1)

            @block.vector
            def _(dve):
                n = [0]

                def link(ins):
                    n[0] += 1
                    ins.then_inc(chain, 1)
                    dve.wait_ge(chain, n[0])

                dve.wait_ge(consts, 32)
                link(dve.tensor_copy(upper[:, :], upper_f[:, :]))
                link(dve.memset(ones_b[:, :], 1.0))
                link(dve.tensor_reduce(one[:, :], logits, AX.X, ALU.max))
                dve.tensor_tensor(work[:, :, :], logits, per_tile(one[:, :]), ALU.subtract).then_inc(probs_ready, 1)
                dve.wait_ge(exp_done, 1)
                link(dve.tensor_reduce(one[:, :], probs[:, :, :], AX.X, ALU.add))
                link(dve.reciprocal(one[:, :], one[:, :]))
                link(dve.tensor_tensor(probs[:, :, :], probs[:, :, :], per_tile(one[:, :]), ALU.mult))
                for i in range(NT):
                    link(dve.max(best[:, i], probs[:, i]))
                    dve.max_index(best_at[:, i], best[:, i], probs[:, i]).then_inc(iotas, 1)
                dve.wait_ge(iotas, NT + 1)
                link(dve.tensor_copy(at_f[:, :, :], best_at[:, :, :]))
                for k in range(TOPK):
                    link(dve.tensor_tensor(chosen[k][:, :, :], experts[:, :].unsqueeze(1).to_broadcast(WHOLE),
                                           per_tile(at_f[:, :, k]), ALU.is_equal))
                link(dve.tensor_tensor(mask[:, :, :], chosen[0][:, :, :], chosen[1][:, :, :], ALU.add))
                link(dve.tensor_tensor(work[:, :, :], chosen[2][:, :, :], chosen[3][:, :, :], ALU.add))
                link(dve.tensor_tensor(mask[:, :, :], mask[:, :, :], work[:, :, :], ALU.add))
                link(dve.tensor_copy(mask_b[:, :, :], mask[:, :, :]))
                link(dve.memset(before[0][:, 0:1], 0.0))
                link(dve.tensor_copy(before[0][:, 1:], mask[:, 0:NT - 1]))
                d, src = 1, 0
                while d < NT:
                    a, b = before[src], before[1 - src]
                    link(dve.tensor_copy(b[:, 0:d], a[:, 0:d]))
                    link(dve.tensor_tensor(b[:, d:], a[:, d:], a[:, 0:NT - d], ALU.add))
                    d, src = 2 * d, 1 - src
                dve.tensor_copy(before_b[:, :, :], before[src][:, :, :]).then_inc(counts_ready, 1)
                dve.wait_ge(place_done, 2)
                for k in range(TOPK):
                    link(dve.tensor_tensor(work[:, :, :], ps_place[:, :, :], chosen[k][:, :, :], ALU.mult))
                    link(dve.tensor_reduce(place[:, k], work[:, :, :], AX.X, ALU.add))
                    link(dve.tensor_scalar(first[:, k], at_f[:, :, k], float(CAP), None, ALU.mult))
                link(dve.tensor_scalar(late[:, :, :], place[:, :, :], float(CAP), None, ALU.is_ge))
                link(dve.tensor_scalar(slot[:, :, :], late[:, :, :], float(1 << 20), None, ALU.mult))
                link(dve.tensor_tensor(slot[:, :, :], slot[:, :, :], place[:, :, :], ALU.add))
                link(dve.tensor_tensor(slot[:, :, :], slot[:, :, :], first[:, :, :], ALU.add))
                link(dve.tensor_copy(kept["scatter_to"][:, :, :], slot[:, :, :]))
                link(dve.tensor_scalar(slot[:, :, :], place[:, :, :], float(CAP - 1), None, ALU.min))
                link(dve.tensor_tensor(slot[:, :, :], slot[:, :, :], first[:, :, :], ALU.add))
                link(dve.tensor_copy(kept["gather_from"][:, :, :], slot[:, :, :]))
                link(dve.tensor_scalar(late[:, :, :], late[:, :, :], -1.0, 1.0, ALU.mult, ALU.add))
                for k in range(TOPK):
                    link(dve.tensor_tensor(kept["weight"][:, k], late[:, k], best[:, :, k], ALU.mult))


def shared_phase(nc, t, kept):
    ctx, sb, ps, sem = open_scope(nc)
    FC = FS // P
    with ctx:
        w_in = sb("sh_w_in", [P, 2, 2, KC, FS], F32R)
        w_out = sb("sh_w_out", [P, 2, FC, D], F32R)
        raw = sb("sh_raw", [P, 2, FS])
        fT = sb("sh_fT", [P, 2, 2, KC, BLK], F32R)
        gate = sb("sh_gate", [P, BLK])
        hid = sb("sh_hid", [P, BLK])
        hid_part = sb("sh_hid_part", [P, 2, 2, BLK], F32R)
        base = sb("sh_base", [P, TB, D])
        idx = [sb(f"sh_idx{k}", [P, 1], U32) for k in range(TOPK)]
        tok = [sb(f"sh_tok{k}", [P, 1], I32) for k in range(TOPK)]
        ps_h = [ps(f"sh_ps_h{i}", [P, 2, BLK]) for i in range(2)]
        ps_y = ps("sh_ps_y", [P, TB, D])
        raw_loaded = [sem(f"sh_raw_loaded{i}") for i in range(2)]
        raw_hi = sem("sh_raw_hi")
        raw_lo = sem("sh_raw_lo")
        f_loaded = [sem(f"sh_f_loaded{i}") for i in range(2)]
        base_loaded = sem("sh_base_loaded")
        h_done = sem("sh_h_done")
        gate_done = sem("sh_gate_done")
        hid_done = sem("sh_hid_done")
        hid_hi = sem("sh_hid_hi")
        hid_lo = sem("sh_hid_lo")
        y_chunk = sem("sh_y_chunk")
        y_taken = sem("sh_y_taken")
        stored = sem("sh_stored")
        idx_set = sem("sh_idx_set")
        scattered = [sem(f"sh_scattered{k}") for k in range(TOPK)]
        base_rows = t["base"].rearrange("(b t p) d -> b p t d", p=P, t=TB)
        pieces = [(raw_s, w_in[:, :, i, c], t[name][c * P:(c + 1) * P, :], FS) for c in range(KC)
                  for i, (name, raw_s) in enumerate((("sw_gate", 0), ("sw_up", 1)))]
        w_down = t["sw_down"].rearrange("(c p) n -> p c n", p=P)
        for c in range(0, FC, 2):
            m = min(2, FC - c)
            pieces.append((c // 2 % 2, w_out[:, :, c:c + m].rearrange("p a c n -> p a (c n)"),
                           w_down[:, c:c + m, :], m * D))
        NPC = len(pieces)

        with nc.Block() as block:
            @block.sync
            def _(sp):
                for n, (s, _, src, width) in enumerate(pieces):
                    if n >= 2:
                        sp.wait_ge(raw_lo, n - 1)
                    dst = raw[:, s, 0:width]
                    if len(src.shape) == 3:
                        dst = dst.rearrange("p (c n) -> p c n", n=D)
                    sp.dma_start(dst, src).then_inc(raw_loaded[s], 16)
                sp.sem_inc(stored, 16)
                with sp.Fori(0, NB // 2) as it:
                    for s in range(2):
                        b = 2 * it + s
                        sp.wait_ge(h_done, it * 2 * FC + s * FC + 1)
                        sp.dma_start(as_f32(fT[:, s]), t["fT_part"][b]).then_inc(f_loaded[s], 16)
                        sp.wait_ge(stored, b * 16 + 16)
                        sp.dma_start(base[:, :], base_rows[b]).then_inc(base_loaded, 16)
                        sp.wait_ge(y_taken, b * TB + TB + TB)
                        sp.dma_start(base_rows[b], base[:, :]).then_inc(stored, 16)
                sp.wait_ge(stored, 16 * NB + 16)

            @block.gpsimd
            def _(pool):
                with pool.Fori(0, NT) as i:
                    for k in range(TOPK):
                        pool.tensor_copy(idx[k][:, :], kept["scatter_to"][:, k, bass.ds(i, 1)]).then_inc(idx_set, 1)
                        pool.tensor_copy(tok[k][:, :], kept["token"][:, bass.ds(i, 1)]).then_inc(idx_set, 1)
                    pool.wait_ge(idx_set, i * 2 * TOPK + 2 * TOPK)
                    pool.sem_inc(kept["passed"], 1)
                    for k in range(TOPK):
                        pool.indirect_dma_start(
                            out=t["slot_token"][:, :], out_offset=bass.IndirectOffsetOnAxis(ap=idx[k][:, 0:1], axis=0),
                            in_=tok[k][:, :], in_offset=None, bounds_check=E * CAP - 1, oob_is_err=False,
                        ).then_inc(scattered[k], 16)
                    for k in range(TOPK):
                        pool.wait_ge(scattered[k], i * 16 + 16)
                    pool.sem_inc(kept["passed"], 1)

            @block.scalar
            def _(act):
                for n, (s, dst, src, width) in enumerate(pieces):
                    act.wait_ge(raw_loaded[s], 16 * (1 + sum(x[0] == s for x in pieces[:n])))
                    act.activation(dst[:, 0], raw[:, s, 0:width], ACT.Copy).then_inc(raw_hi, 1)
                with act.Fori(0, NB // 2) as it:
                    for s in range(2):
                        for f in range(FC):
                            n = s * FC + f
                            act.wait_ge(h_done, it * 2 * FC + n + FC + 1)
                            act.wait_ge(hid_done, it * 2 * FC + n + 1)
                            act.activation(gate[:, :], ps_h[f % 2][:, 0], ACT.Silu).then_inc(gate_done, 1)
                            act.wait_ge(hid_done, it * 2 * FC + n + 2)
                            act.wait_ge(y_chunk, it * 2 * FC + n + 1)
                            act.activation(hid_part[:, n % 2, 0], hid[:, :], ACT.Copy).then_inc(hid_hi, 1)

            @block.vector
            def _(dve):
                for n, (s, dst, src, width) in enumerate(pieces):
                    dve.wait_ge(raw_hi, n + 1)
                    dve.tensor_tensor(dst[:, 1], raw[:, s, 0:width], as_f32(dst[:, 0]), ALU.subtract).then_inc(raw_lo, 1)
                dve.sem_inc(hid_done, 1)
                dve.sem_inc(hid_lo, 1)
                dve.sem_inc(y_taken, TB)
                with dve.Fori(0, NB // 2) as it:
                    for s in range(2):
                        for f in range(FC):
                            n = s * FC + f
                            dve.wait_ge(gate_done, it * 2 * FC + n + 1)
                            dve.wait_ge(hid_lo, it * 2 * FC + n + 1)
                            dve.tensor_tensor(hid[:, :], ps_h[f % 2][:, 1], gate[:, :], ALU.mult).then_inc(hid_done, 1)
                            dve.wait_ge(hid_hi, it * 2 * FC + n + 1)
                            dve.tensor_tensor(hid_part[:, n % 2, 1], hid[:, :], as_f32(hid_part[:, n % 2, 0]),
                                              ALU.subtract).then_inc(hid_lo, 1)
                        b = 2 * it + s
                        dve.wait_ge(base_loaded, b * 16 + 16)
                        dve.wait_ge(y_chunk, it * 2 * FC + s * FC + FC + 2)
                        for k in range(TB):
                            dve.scalar_tensor_tensor(out=base[:, k], in0=ps_y[:, k],
                                                     scalar=kept["shared_gate"][:, bass.ds(b * TB + k, 1)],
                                                     in1=base[:, k], op0=ALU.mult, op1=ALU.add).then_inc(y_taken, 1)

            @block.tensor
            def _(pe):
                pe.wait_ge(raw_lo, NPC)
                pe.sem_inc(h_done, FC)
                pe.sem_inc(y_chunk, 2)

                def down(it, s, f):
                    n = s * FC + f
                    pe.wait_ge(hid_lo, it * 2 * FC + n + 2)
                    if f == 0:
                        pe.wait_ge(y_taken, (2 * it + s) * TB + TB)
                    for k in range(TB):
                        for x, (i, j) in enumerate(THREE):
                            mm = pe.matmul(ps_y[:, k], hid_part[:, n % 2, i, k * P:(k + 1) * P], w_out[:, j, f],
                                           start=f == 0 and x == 0, stop=f == FC - 1 and x == 2)
                    mm.then_inc(y_chunk, 1)

                with pe.Fori(0, NB // 2) as it:
                    for s in range(2):
                        pe.wait_ge(f_loaded[s], 16 * it + 16)
                        for f in range(FC):
                            n = s * FC + f
                            if f >= 2:
                                pe.wait_ge(hid_done, it * 2 * FC + n)
                            for g in range(2):
                                for c in range(KC):
                                    for x, (i, j) in enumerate(THREE):
                                        mm = pe.matmul(ps_h[f % 2][:, g], w_in[:, j, g, c, f * P:(f + 1) * P],
                                                       fT[:, s, i, c], start=c == 0 and x == 0, stop=c == KC - 1 and x == 2)
                            mm.then_inc(h_done, 1)
                            if f >= 1:
                                down(it, s, f - 1)
                        down(it, s, FC - 1)


def expert_phase(nc, t, kept):
    ctx, sb, ps, sem = open_scope(nc)
    SC = CAP // P
    FP = [min(P, F - c) for c in range(0, F, P)]
    FC = len(FP)
    with ctx:
        raw_in = sb("ex_raw_in", [P, 2, 2, KC, F])
        raw_out = sb("ex_raw_out", [P, 2, FC, D])
        w_in = sb("ex_w_in", [P, 2, 2, 2, KC, F], F32R)
        w_out = sb("ex_w_out", [P, 2, 2, FC, D], F32R)
        table = sb("ex_table", [P, E, SC], U32)
        idx = [sb(f"ex_idx{i}", [P, 1], U32) for i in range(2 * SC)]
        x = [sb(f"ex_x{i}", [P, D]) for i in range(2 * SC)]
        xT = sb("ex_xT", [P, 2, KC, CAP], F32R)
        gate = sb("ex_gate", [P, 2, CAP])
        hid = sb("ex_hid", [P, CAP])
        hid_part = sb("ex_hid_part", [P, 2, FC, CAP], F32R)
        y = sb("ex_y", [P, 2, SC, D])
        ps_t = [ps(f"ex_ps_t{i}", [P, KC, P]) for i in range(2)]
        ps_h = [ps(f"ex_ps_h{i}", [P, 2, CAP]) for i in range(2)]
        ps_y = ps("ex_ps_y", [P, SC, D])
        table_loaded = sem("ex_table_loaded")
        in_loaded = [[sem(f"ex_in_loaded{i}_{g}") for g in range(2)] for i in range(2)]
        out_loaded = [sem(f"ex_out_loaded{i}") for i in range(2)]
        in_hi = [sem(f"ex_in_hi{g}") for g in range(2)]
        out_hi = sem("ex_out_hi")
        in_lo = sem("ex_in_lo")
        out_lo = sem("ex_out_lo")
        idx_set = sem("ex_idx_set")
        x_loaded = [sem(f"ex_x_loaded{i}") for i in range(2 * SC)]
        turned = sem("ex_turned")
        x_hi = sem("ex_x_hi")
        x_lo = sem("ex_x_lo")
        h_done = sem("ex_h_done")
        gate_done = sem("ex_gate_done")
        hid_done = sem("ex_hid_done")
        hid_hi = sem("ex_hid_hi")
        hid_lo = sem("ex_hid_lo")
        y_done = sem("ex_y_done")
        y_taken = sem("ex_y_taken")
        y_stored = [sem(f"ex_y_stored{i}") for i in range(2)]
        passed = sem("ex_passed")
        y_rows = t["expert_out"].rearrange("(e p c) d -> e p c d", e=E, c=SC)
        w_src = [t[name].rearrange("e (c p) f -> e p c f", p=P) for name in ("w_gate", "w_up")]
        last_rows = slice(0, FP[-1])
        ITS = E // 2 - 1

        with nc.Block() as block:
            @block.sync
            def _(sp):
                def load(it, i):
                    e = 2 * it + i
                    sp.wait_ge(in_lo, 2 * e + 4)
                    sp.sem_inc(passed, 1)
                    for g in range(2):
                        sp.dma_start(raw_in[:, i, g], w_src[g][e]).then_inc(in_loaded[i][g], 16)
                    sp.wait_ge(out_lo, e + 2)
                    sp.dma_start(raw_out[:, i, 0:FC - 1], t["w_down"][e, 0:(FC - 1) * P, :].rearrange("(c p) n -> p c n", p=P)).then_inc(out_loaded[i], 16)
                    sp.dma_start(raw_out[last_rows, i, FC - 1], t["w_down"][e, (FC - 1) * P:F, :]).then_inc(out_loaded[i], 16)

                with nc.allow_non_contiguous_dma(reason="32 KB, once"):
                    sp.dma_start(table[:, :, :], t["slot_token"].bitcast(U32).rearrange("(e p c) a -> p e (c a)", e=E, c=SC)).then_inc(table_loaded, 16)
                for i in range(2):
                    sp.sem_inc(y_stored[i], 16)
                load(0, 0)
                load(0, 1)

                def work(it, last):
                    for i in range(2):
                        if not last:
                            load(it + 1, i)
                        e = 2 * it + i
                        sp.wait_ge(y_taken, e + 2)
                        sp.dma_start(y_rows[e], y[:, i]).then_inc(y_stored[i], 16)

                with sp.Fori(0, ITS) as it:
                    work(it, False)
                work(ITS, True)
                for i in range(2):
                    sp.wait_ge(y_stored[i], 16 * (E // 2) + 16)

            @block.gpsimd
            def _(pool):
                def gather(it, i):
                    e = 2 * it + i
                    for c in range(SC):
                        pool.wait_ge(turned, e * SC + c + 1)
                        pool.tensor_copy(idx[i * SC + c][:, :], table[:, bass.ds(e, 1), c]).then_inc(idx_set, 1)
                        pool.wait_ge(idx_set, e * SC + c + 1)
                        pool.sem_inc(passed, 1)
                        pool.indirect_dma_start(
                            out=x[i * SC + c][:, :], out_offset=None, in_=t["xf"][:, :],
                            in_offset=bass.IndirectOffsetOnAxis(ap=idx[i * SC + c][:, 0:1], axis=0),
                            bounds_check=S - 1, oob_is_err=False,
                        ).then_inc(x_loaded[i * SC + c], 16)

                def low_in(it, i):
                    for g in range(2):
                        pool.wait_ge(in_hi[g], 2 * it + i + 1)
                        pool.tensor_tensor(w_in[:, i, 1, g], raw_in[:, i, g], as_f32(w_in[:, i, 0, g]),
                                           ALU.subtract).then_inc(in_lo, 1)

                pool.sem_inc(in_lo, 4)
                pool.wait_ge(table_loaded, 16)
                gather(0, 0)
                gather(0, 1)
                low_in(0, 0)

                def work(it, last):
                    for i in range(2):
                        if i == 0 or not last:
                            low_in(it + i, 1 - i)
                        if not last:
                            gather(it + 1, i)

                with pool.Fori(0, ITS) as it:
                    work(it, False)
                work(ITS, True)

            @block.scalar
            def _(act):
                act.sem_inc(y_taken, 1)

                def high_up(it, i):
                    e = 2 * it + i
                    act.wait_ge(in_loaded[i][1], 16 * it + 16)
                    act.wait_ge(y_done, e + 1)
                    act.activation(w_in[:, i, 0, 1], raw_in[:, i, 1], ACT.Copy).then_inc(in_hi[1], 1)

                def high_out(it, i):
                    e = 2 * it + i
                    act.wait_ge(out_loaded[i], 32 * it + 32)
                    act.wait_ge(y_done, e + 1)
                    act.activation(w_out[:, i, 0, 0:FC - 1], raw_out[:, i, 0:FC - 1], ACT.Copy)
                    act.activation(w_out[last_rows, i, 0, FC - 1], raw_out[last_rows, i, FC - 1], ACT.Copy).then_inc(out_hi, 1)

                def high_x(it, i):
                    e = 2 * it + i
                    for c in range(SC):
                        act.wait_ge(turned, e * SC + c + 2 * SC + 1)
                        act.wait_ge(h_done, e * FC + FC)
                        act.activation(xT[:, 0, :, c * P:(c + 1) * P], ps_t[c % 2][:, :, :], ACT.Copy).then_inc(x_hi, 1)

                high_up(0, 0)
                high_x(0, 0)
                high_out(0, 0)

                def work(it, last):
                    for i in range(2):
                        e = 2 * it + i
                        more = i == 0 or not last
                        for f in range(FC):
                            n = i * FC + f
                            act.wait_ge(h_done, it * 2 * FC + n + FC + 1)
                            act.wait_ge(hid_done, it * 2 * FC + n + 1)
                            act.activation(gate[0:FP[f], n % 2, :], ps_h[n % 2][0:FP[f], 0], ACT.Silu).then_inc(gate_done, 1)
                            if f == 0 and more:
                                high_up(it + i, 1 - i)
                        if more:
                            high_x(it + i, 1 - i)
                            high_out(it + i, 1 - i)
                        act.wait_ge(y_done, e + 3)
                        act.wait_ge(y_stored[i], 16 * it + 16)
                        act.activation(y[:, i], ps_y[:, :, :], ACT.Copy).then_inc(y_taken, 1)

                with act.Fori(0, ITS) as it:
                    work(it, False)
                work(ITS, True)

            @block.vector
            def _(dve):
                dve.sem_inc(out_lo, 2)
                dve.sem_inc(hid_done, 2)
                dve.sem_inc(hid_lo, 1)
                dve.sem_inc(x_lo, SC)

                def high_gate(it, i):
                    e = 2 * it + i
                    dve.wait_ge(in_loaded[i][0], 16 * it + 16)
                    dve.wait_ge(y_done, e + 1)
                    dve.tensor_copy(w_in[:, i, 0, 0], raw_in[:, i, 0]).then_inc(in_hi[0], 1)

                def low_out(it, i):
                    dve.wait_ge(out_hi, 2 * it + i + 1)
                    dve.tensor_tensor(w_out[:, i, 1, 0:FC - 1], raw_out[:, i, 0:FC - 1],
                                      as_f32(w_out[:, i, 0, 0:FC - 1]), ALU.subtract)
                    dve.tensor_tensor(w_out[last_rows, i, 1, FC - 1], raw_out[last_rows, i, FC - 1],
                                      as_f32(w_out[last_rows, i, 0, FC - 1]), ALU.subtract).then_inc(out_lo, 1)

                def low_x(it, i):
                    for c in range(SC):
                        dve.wait_ge(x_hi, (2 * it + i) * SC + c + 1)
                        dve.tensor_tensor(xT[:, 1, :, c * P:(c + 1) * P], ps_t[c % 2][:, :, :],
                                          as_f32(xT[:, 0, :, c * P:(c + 1) * P]), ALU.subtract).then_inc(x_lo, 1)

                high_gate(0, 0)
                low_x(0, 0)
                low_out(0, 0)

                def work(it, last):
                    for i in range(2):
                        e = 2 * it + i
                        more = i == 0 or not last
                        for f in range(FC):
                            n = i * FC + f
                            rows = slice(0, FP[f])
                            if f == 0:
                                dve.wait_ge(y_done, e + 2)
                            dve.wait_ge(gate_done, it * 2 * FC + n + 1)
                            dve.wait_ge(hid_lo, it * 2 * FC + n + 1)
                            dve.tensor_tensor(hid[rows, :], ps_h[n % 2][rows, 1], gate[rows, n % 2], ALU.mult).then_inc(hid_done, 1)
                            dve.wait_ge(hid_done, it * 2 * FC + n + 3)
                            dve.tensor_copy(hid_part[rows, 0, f], hid[rows, :]).then_inc(hid_hi, 1)
                            dve.wait_ge(hid_hi, it * 2 * FC + n + 1)
                            dve.tensor_tensor(hid_part[rows, 1, f], hid[rows, :], as_f32(hid_part[rows, 0, f]),
                                              ALU.subtract).then_inc(hid_lo, 1)
                            if f == 0 and more:
                                high_gate(it + i, 1 - i)
                        if more:
                            low_x(it + i, 1 - i)
                            low_out(it + i, 1 - i)

                with dve.Fori(0, ITS) as it:
                    work(it, False)
                work(ITS, True)

            @block.tensor
            def _(pe):
                pe.sem_inc(turned, 2 * SC)
                pe.sem_inc(h_done, FC)
                pe.sem_inc(y_done, 2)

                def turn(it, i):
                    e = 2 * it + i
                    for c in range(SC):
                        pe.wait_ge(x_loaded[i * SC + c], 16 * it + 16)
                        pe.wait_ge(x_lo, e * SC + c + 1)
                        for m in range(KC):
                            mm = pe.transpose(ps_t[c % 2][:, m], x[i * SC + c][:, m * P:(m + 1) * P], kept["ident"][:, :])
                        mm.then_inc(turned, 1)

                turn(0, 0)

                def work(it, last):
                    for i in range(2):
                        e = 2 * it + i
                        pe.wait_ge(in_lo, 2 * e + 6)
                        pe.wait_ge(x_lo, e * SC + 2 * SC)
                        for f in range(FC):
                            n = i * FC + f
                            pe.wait_ge(hid_done, it * 2 * FC + n + 1)
                            for g in range(2):
                                for c in range(KC):
                                    for m, (a, b) in enumerate(THREE):
                                        mm = pe.matmul(ps_h[n % 2][0:FP[f], g], w_in[:, i, b, g, c, f * P:f * P + FP[f]],
                                                       xT[:, a, c], start=c == 0 and m == 0, stop=c == KC - 1 and m == 2)
                            mm.then_inc(h_done, 1)
                        if i == 0 or not last:
                            turn(it + i, 1 - i)
                        pe.wait_ge(out_lo, e + 3)
                        pe.wait_ge(y_taken, e + 1)
                        for f in range(FC):
                            pe.wait_ge(hid_lo, it * 2 * FC + i * FC + f + 2)
                            for s in range(SC):
                                for m, (a, b) in enumerate(THREE):
                                    mm = pe.matmul(ps_y[:, s], hid_part[0:FP[f], a, f, s * P:(s + 1) * P],
                                                   w_out[0:FP[f], i, b, f], start=f == 0 and m == 0,
                                                   stop=f == FC - 1 and m == 2)
                        mm.then_inc(y_done, 1)

                with pe.Fori(0, ITS) as it:
                    work(it, False)
                work(ITS, True)


def output_phase(nc, t, kept):
    ctx, sb, ps, sem = open_scope(nc)
    SROW = S // P
    with ctx:
        raw = sb("ou_raw", [P, KC, D])
        w = sb("ou_w", [P, 2, KC, D], F32R)
        sums = sb("ou_sums", [P, H, SROW])
        inv = sb("ou_inv", [P, H, SROW])
        inv_rows = sb("ou_inv_rows", [H, S])
        spread = sb("ou_spread", [H, KC, HPC, HD])
        att = sb("ou_att", [P, 2, 2, KC, BLK])
        z = sb("ou_z", [P, 2, BLK])
        z_part = sb("ou_z_part", [P, 2, 2, KC, BLK], F32R)
        acc = sb("ou_acc", [P, 2, TB, D])
        idx = sb("ou_idx", [P, 2, TOPK, TB], U32)
        ey = [[sb(f"ou_ey{i}_{k}", [P, D]) for k in range(TOPK)] for i in range(2)]
        weight = sb("ou_weight", [P, 2, TOPK, TB])
        ps_z = [ps(f"ou_ps_z{i}", [P, D]) for i in range(TB)]
        ps_i = [ps(f"ou_ps_i{i}", [P, BLK]) for i in range(2)]
        w_loaded = sem("ou_w_loaded")
        w_hi = sem("ou_w_hi")
        w_lo = sem("ou_w_lo")
        sums_loaded = sem("ou_sums_loaded")
        inv_made = sem("ou_inv_made")
        inv_stored = sem("ou_inv_stored")
        inv_loaded = sem("ou_inv_loaded")
        spread_made = sem("ou_spread_made")
        att_loaded = [sem(f"ou_att_loaded{i}") for i in range(2)]
        parts_added = sem("ou_parts_added")
        i_done = sem("ou_i_done")
        z_made = sem("ou_z_made")
        z_hi = sem("ou_z_hi")
        z_lo = sem("ou_z_lo")
        base_loaded = [sem(f"ou_base_loaded{i}") for i in range(2)]
        idx_set = sem("ou_idx_set")
        gathered = [[sem(f"ou_gathered{i}_{k}") for k in range(TOPK)] for i in range(2)]
        o_done = sem("ou_o_done")
        o_taken = sem("ou_o_taken")
        added = sem("ou_added")
        rows_done = sem("ou_rows_done")
        weight_set = sem("ou_weight_set")
        stored = [sem(f"ou_stored{i}") for i in range(2)]
        passed = sem("ou_passed")
        passed_pe = sem("ou_passed_pe")
        base_rows = t["base"].rearrange("(b t p) d -> b p t d", p=P, t=TB)
        out_rows = t["out"].rearrange("a (b t p) d -> (a b) p t d", p=P, t=TB)
        att_rows = t["att_v"].rearrange("a (c p) (b n) -> b a p c n", p=P, n=BLK)
        ITS = NB // 2 - 1

        with nc.Block() as block:
            @block.sync
            def _(sp):
                with nc.allow_non_contiguous_dma(reason="256 KB, once"):
                    sp.dma_start(sums[:, :, :], t["att_sum"].rearrange("h (p j) -> p h j", p=P)).then_inc(sums_loaded, 16)
                sp.dma_start(raw[:, :, :], t["wo"].rearrange("(c p) n -> p c n", p=P)).then_inc(w_loaded, 16)
                sp.wait_ge(inv_made, 1)
                with nc.allow_non_contiguous_dma(reason="256 KB, once"):
                    sp.dma_start(t["att_inv"].rearrange("h (p j) -> p h j", p=P), inv[:, :, :]).then_inc(inv_stored, 16)
                sp.wait_ge(inv_stored, 16)
                sp.dma_start(inv_rows[:, :], t["att_inv"]).then_inc(inv_loaded, 16)
                for i in range(2):
                    for part in range(2):
                        sp.dma_start(att[:, i, part], att_rows[i, part]).then_inc(att_loaded[i], 16)
                with sp.Fori(0, ITS) as it:
                    for i in range(2):
                        sp.wait_ge(z_made, (2 * it + i) * KC + 3 * KC)
                        for part in range(2):
                            sp.dma_start(att[:, i, part], att_rows[2 * it + 2 + i, part]).then_inc(att_loaded[i], 16)

            @block.gpsimd
            def _(pool):
                def work(it):
                    for i in range(2):
                        b = 2 * it + i
                        pool.wait_ge(idx_set, b + 1)
                        for k in range(TB):
                            pool.wait_ge(rows_done, b * TB + k + TB - 1)
                            pool.sem_inc(passed, 1)
                            for j in range(TOPK):
                                pool.indirect_dma_start(
                                    out=ey[k % 2][j][:, :], out_offset=None, in_=t["expert_out"][:, :],
                                    in_offset=bass.IndirectOffsetOnAxis(ap=idx[:, i, j, k:k + 1], axis=0),
                                    bounds_check=E * CAP - 1, oob_is_err=False,
                                ).then_inc(gathered[k % 2][j], 16)

                with pool.Fori(0, NB // 2) as it:
                    work(it)

            @block.scalar
            def _(act):
                for i in range(2):
                    act.sem_inc(stored[i], 16)
                act.wait_ge(w_loaded, 16)
                act.activation(w[:, 0], raw[:, :, :], ACT.Copy).then_inc(w_hi, 1)

                def base(it, i):
                    act.wait_ge(stored[i], 16 * it + 16)
                    act.dma_start(acc[:, i], base_rows[2 * it + i]).then_inc(base_loaded[i], 16)

                def high(it, i):
                    b = 2 * it + i
                    for c in range(KC):
                        act.wait_ge(z_made, b * KC + c + 2 * KC + 1)
                        act.wait_ge(o_done, b * TB + TB)
                        act.activation(z_part[:, i, 0, c], z[:, c % 2], ACT.Copy).then_inc(z_hi, 1)

                base(0, 0)
                high(0, 0)

                def work(it, last):
                    for i in range(2):
                        if i == 0 or not last:
                            base(it + i, 1 - i)
                            high(it + i, 1 - i)
                        act.wait_ge(rows_done, (2 * it + i) * TB + 2 * TB)
                        act.dma_start(out_rows[2 * it + i], acc[:, i]).then_inc(stored[i], 16)

                with act.Fori(0, ITS) as it:
                    work(it, False)
                work(ITS, True)
                for i in range(2):
                    act.wait_ge(stored[i], 16 * (NB // 2) + 16)

            @block.vector
            def _(dve):
                dve.sem_inc(z_made, 2 * KC)
                dve.sem_inc(z_lo, 2)
                dve.sem_inc(o_taken, TB)
                dve.sem_inc(rows_done, TB)
                for i in range(2):
                    for src, dst, done in (("gather_from", idx, idx_set), ("weight", weight, weight_set)):
                        dve.tensor_copy(dst[:, i], kept[src][:, :, i * TB:(i + 1) * TB]).then_inc(done, 1)
                dve.tensor_copy(spread[:, :, :, :], kept["ident"][0:H, 0:H].rearrange("p (c g) -> p c g", c=KC)
                                .unsqueeze(3).to_broadcast([H, KC, HPC, HD])).then_inc(spread_made, 1)
                dve.wait_ge(sums_loaded, 16)
                dve.reciprocal(inv[:, :, :], sums[:, :, :]).then_inc(inv_made, 1)
                dve.wait_ge(w_hi, 1)
                dve.tensor_tensor(w[:, 1], raw[:, :, :], as_f32(w[:, 0]), ALU.subtract).then_inc(w_lo, 1)

                def low(it, i, c):
                    dve.wait_ge(z_hi, (2 * it + i) * KC + c + 1)
                    dve.tensor_tensor(z_part[:, i, 1, c], z[:, c % 2], as_f32(z_part[:, i, 0, c]), ALU.subtract).then_inc(z_lo, 1)

                def normal(it, i, c):
                    b = 2 * it + i
                    if c == 0:
                        dve.wait_ge(att_loaded[i], 32 * it + 32)
                    dve.tensor_tensor(att[:, i, 0, c], att[:, i, 0, c], att[:, i, 1, c], ALU.add).then_inc(parts_added, 1)
                    dve.wait_ge(parts_added, b * KC + c + 1)
                    dve.wait_ge(i_done, b * KC + c + 1)
                    dve.wait_ge(z_lo, b * KC + c + 1)
                    dve.tensor_tensor(z[:, c % 2], att[:, i, 0, c], ps_i[c % 2][:, :], ALU.mult).then_inc(z_made, 1)

                for c in range(KC):
                    normal(0, 0, c)
                    if c >= 1:
                        low(0, 0, c - 1)
                low(0, 0, KC - 1)

                def work(it, last):
                    for i in range(2):
                        b = 2 * it + i
                        more = i == 0 or not last
                        dve.wait_ge(base_loaded[i], 16 * it + 16)
                        dve.wait_ge(weight_set, b + 1)
                        for k in range(TB):
                            if more:
                                normal(it + i, 1 - i, k)
                            n = (b * TB + k) * TOPK
                            dve.wait_ge(o_done, b * TB + k + 2 * TB + 1)
                            dve.tensor_tensor(acc[:, i, k], ps_z[k][:, :], acc[:, i, k], ALU.add).then_inc(o_taken, 1)
                            for j in range(TOPK):
                                if j == 0:
                                    dve.wait_ge(o_taken, b * TB + k + TB + 1)
                                else:
                                    dve.wait_ge(added, n + j)
                                dve.wait_ge(gathered[k % 2][j], (2 * b + k // 2 + 1) * 16)
                                dve.scalar_tensor_tensor(out=acc[:, i, k], in0=ey[k % 2][j][:, :], scalar=weight[:, i, j, k:k + 1],
                                                         in1=acc[:, i, k], op0=ALU.mult, op1=ALU.add).then_inc(added, 1)
                            dve.wait_ge(added, n + TOPK)
                            dve.sem_inc(rows_done, 1)
                            if more:
                                low(it + i, 1 - i, k)
                        if not last:
                            cols = bass.ds((b + 2) * TB, TB)
                            dve.tensor_copy(idx[:, i], kept["gather_from"][:, :, cols]).then_inc(idx_set, 1)
                            dve.tensor_copy(weight[:, i], kept["weight"][:, :, cols]).then_inc(weight_set, 1)

                with dve.Fori(0, ITS) as it:
                    work(it, False)
                work(ITS, True)

            @block.tensor
            def _(pe):
                pe.sem_inc(o_done, 2 * TB)
                pe.wait_ge(spread_made, 1)
                pe.wait_ge(inv_loaded, 16)

                def inverses(it, i, c):
                    b = 2 * it + i
                    pe.wait_ge(z_made, b * KC + c + 2 * KC - 1)
                    pe.sem_inc(passed_pe, 1)
                    pe.matmul(ps_i[c % 2][:, :], spread[:, c].rearrange("p g d -> p (g d)"), inv_rows[:, bass.ds(b * BLK, BLK)],
                              start=True, stop=True).then_inc(i_done, 1)

                for c in range(KC):
                    inverses(0, 0, c)
                pe.wait_ge(w_lo, 1)

                def work(it, last):
                    for i in range(2):
                        b = 2 * it + i
                        pe.wait_ge(z_lo, b * KC + KC + 2)
                        for k in range(TB):
                            pe.wait_ge(o_taken, b * TB + k + 1)
                            for c in range(KC):
                                for n, (x, y) in enumerate(THREE):
                                    mm = pe.matmul(ps_z[k][:, :], z_part[:, i, x, c, k * P:(k + 1) * P], w[:, y, c],
                                                   start=c == 0 and n == 0, stop=c == KC - 1 and n == 2)
                            mm.then_inc(o_done, 1)
                            if i == 0 or not last:
                                inverses(it + i, 1 - i, k)

                with pe.Fori(0, ITS) as it:
                    work(it, False)
                work(ITS, True)


def host_constants():
    start = 2.0 ** (-8.0 / H_ALL)
    slopes = np.array([start * start ** i for i in range(H_ALL)], np.float32).astype(np.float64)
    bias = slopes[:, None] * (np.arange(S) - S // 2)[None, :]

    def twelve_bits(x):
        m, e = np.frexp(x)
        return np.ldexp(np.rint(m * 4096) / 4096, e)

    hi = twelve_bits(bias)
    alibi = np.stack([hi, twelve_bits(bias - hi)], axis=1).astype(np.float32)
    row, col = np.arange(P)[:, None], np.arange(P)[None, :]
    masks = np.zeros((P, 3 * P), np.float32)
    masks[:, 0:P][col > row] = MASKED
    masks[:, P:2 * P] = MASKED
    masks[:, 2 * P:][row > col] = MASKED
    return alibi, masks


KEPT = (
    ("ident", [P, P], F32), ("token", [P, NT], I32), ("shared_gate", [P, NT], F32),
    ("scatter_to", [P, TOPK, NT], U32), ("gather_from", [P, TOPK, NT], U32), ("weight", [P, TOPK, NT], F32),
)
PROJECTION = (
    ("w_norm", [P, D], F32), ("bv", [P, D], F32), ("bo", [P, D], F32), ("bqk", [P, 2 * KC], F32),
    ("w_qkv", [P, 2, 3, KC, D], F32R), ("w_r", [P, 2, KC, RW], F32R), ("stat", [P, 3, NT], F32),
)
SCRATCH = (
    ("base", [S, D], F32), ("xf", [S, D], F32), ("fT_part", [NB, P, 2, KC, BLK], F32),
    ("q_part", [2, D, S], F32), ("k_part", [2, D, S], F32), ("v_part", [S, H * 2 * HD], F32),
    ("att_v", [2, D, S], F32), ("att_sum", [H, S], F32), ("att_inv", [H, S], F32),
    ("slot_token", [E * CAP, 1], I32), ("expert_out", [E * CAP, D], F32),
    ("alibi_s", [H, 2, S], F32),
)


def build(nc, t):
    for name, shape, dt in SCRATCH:
        if name not in t:
            t[name] = nc.dram_tensor("scratch_" + name, shape, dt, kind="Internal").ap()
    with ExitStack() as whole:
        kept = {n: whole.enter_context(nc.sbuf_tensor("kept_" + n, shape, dt)) for n, shape, dt in KEPT}
        kept["passed"] = whole.enter_context(nc.semaphore("kept_passed"))
        with ExitStack() as front:
            kept["logits"] = front.enter_context(nc.sbuf_tensor("kept_logits", [P, NT, RW], F32))
            with ExitStack() as projection:
                for n, shape, dt in PROJECTION:
                    kept[n] = projection.enter_context(nc.sbuf_tensor("kept_" + n, shape, dt))
                statistics_phase(nc, t, kept)
                project_phase(nc, t, kept)
            routing_phase(nc, t, kept)
        shared_phase(nc, t, kept)
        attention_phase(nc, t, kept)
        expert_phase(nc, t, kept)
        output_phase(nc, t, kept)


_INS = {
    "L0_attn_x": "x", "L0_attn_wq": "wq", "L0_attn_bq": "bq", "L0_attn_wk": "wk", "L0_attn_bk": "bk",
    "L0_attn_wv": "wv", "L0_attn_bv": "bv", "L0_attn_wo": "wo", "L0_attn_bo": "bo", "L0_ffn_w_norm": "w_norm",
    "L0_ffn_w_router": "w_router", "L0_ffn_w_gate": "w_gate", "L0_ffn_w_up": "w_up", "L0_ffn_w_down": "w_down",
    "L0_ffn_sw_gate": "sw_gate", "L0_ffn_sw_up": "sw_up", "L0_ffn_sw_down": "sw_down",
    "L0_ffn_w_shared_gate": "w_sgate",
}


def kernel(**inputs):
    import numpy as _np
    import concourse.bacc as _bacc
    from concourse.bass_utils import run_bass_kernel_spmd as _run

    nc = _bacc.Bacc("TRN2", target_bir_lowering=False, num_devices=1)
    alibi, masks = host_constants()
    arrays = {name: _np.ascontiguousarray(inputs[long]) for long, name in _INS.items()}
    arrays |= {
        "alibi": alibi, "masks": masks, "ident": _np.eye(P, dtype=_np.float32),
        "upper": _np.triu(_np.ones((P, P), _np.float32), 1), "experts": _np.arange(E, dtype=_np.float32),
    }
    t = {n: nc.dram_tensor(f"in_{n}", a.shape, mybir.dt.from_np(a.dtype), kind="ExternalInput").ap() for n, a in arrays.items()}
    t["out"] = nc.dram_tensor("out_x", (1, S, D), F32, kind="ExternalOutput").ap()
    build(nc, t)
    r = _run(nc, [{f"in_{n}": a for n, a in arrays.items()}], core_ids=[0])
    return r.results[0]["out_x"]
```

```python
from contextlib import ExitStack

import concourse.bass as bass
import numpy as np
from concourse import mybir

ALU = mybir.AluOpType
ACT = mybir.ActivationFunctionType
AX = mybir.AxisListType
F32 = mybir.dt.float32
F32R = mybir.dt.float32r
BF16 = mybir.dt.bfloat16
I32 = mybir.dt.int32
U32 = mybir.dt.uint32

P = 128
S = 4096
D = 512
KC = D // P
H = H_ALL = 16
HD = D // H
E = 32
TOPK = 4
CAP = 256
F = 352
FS = 1408
BLK = 512
NB = S // BLK
TB = BLK // P
NT = S // P
RW = E + 2
HPC = P // HD
LN_EPS = 1e-5
RMS_EPS = 1e-6
Q_SCALE = float(1.0 / np.sqrt(np.float32(HD)))
MASKED = -1e30


THREE = ((0, 0), (0, 1), (1, 0))


def as_f32(ap):
    return ap.bitcast(F32)


def open_scope(nc):
    ctx = ExitStack()

    def sb(name, shape, dt=F32):
        return ctx.enter_context(nc.sbuf_tensor(name, shape, dt))

    def ps(name, shape, dt=F32):
        return ctx.enter_context(nc.psum_tensor(name, shape, dt))

    def sem(name):
        return ctx.enter_context(nc.semaphore(name))

    return ctx, sb, ps, sem


def project_phase(nc, t, kept):
    ctx, sb, ps, sem = open_scope(nc)
    MQK = 2 * KC
    NM = MQK + TB
    NTR = 2 * TB
    GROUPS = ((0, KC), (KC, MQK), (MQK, NM))
    NORM_AT, TURN_AT, LOW_AT = 4, 5, 6
    ITS = NB // 2 - 1
    with ctx:
        x_in = sb("pr_x", [P, TB, D])
        xn = sb("pr_xn", [P, TB, D])
        xf = sb("pr_xf", [P, TB, D])
        base = sb("pr_base", [P, TB, D])
        six = sb("pr_six", [P, TB, 6])
        mean_var = sb("pr_mean_var", [P, TB, 2])
        a1 = sb("pr_a1", [P, TB])
        a2 = sb("pr_a2", [P, TB])
        root = sb("pr_root", [P, TB])
        tmp = sb("pr_tmp", [P, TB])
        rstd = sb("pr_rstd", [P, 2, TB])
        raw_r = sb("pr_raw_r", [P, KC, RW])
        xT = sb("pr_xT", [P, 2, 2, KC, BLK], F32R)
        fT = sb("pr_fT", [P, 2, KC, BLK], F32R)
        qk = sb("pr_qk", [P, 2, BLK])
        qk_part = sb("pr_qk_part", [P, 2, MQK, BLK], F32R)
        v = sb("pr_v", [P, 2, D])
        lT = sb("pr_lT", [RW, BLK])
        v_part = sb("pr_v_part", [P, TB, H, 2, HD], F32R)
        ps_t = [ps(f"pr_ps_t{i}", [P, KC, P]) for i in range(2)]
        ps_m = [ps(f"pr_ps_m{i}", [P, BLK]) for i in range(3)]
        ps_l = ps("pr_ps_l", [RW, BLK])
        ps_r = ps("pr_ps_r", [P, TB, RW])
        raw = [as_f32(qk_part[:, i // 2, i % 2 * KC:(i % 2 + 1) * KC]) for i in range(3)]

        w_loaded = [sem(f"pr_w_loaded{i}") for i in range(4)]
        consts_loaded = sem("pr_consts_loaded")
        pad_done = sem("pr_pad_done")
        w_hi = sem("pr_w_hi")
        w_lo = sem("pr_w_lo")
        wq_lo = sem("pr_wq_lo")
        x_loaded = sem("pr_x_loaded")
        six_done = sem("pr_six_done")
        mv_done = sem("pr_mv_done")
        chain = sem("pr_chain")
        root_done = sem("pr_root_done")
        xn_done = sem("pr_xn_done")
        xf_done = sem("pr_xf_done")
        base_sum = sem("pr_base_sum")
        base_done = sem("pr_base_done")
        turned = sem("pr_turned")
        turned_hi = sem("pr_turned_hi")
        turned_lo = sem("pr_turned_lo")
        r_done = sem("pr_r_done")
        l_copied = sem("pr_l_copied")
        r_back = sem("pr_r_back")
        r_copied = sem("pr_r_copied")
        m_done = sem("pr_m_done")
        m_copied = sem("pr_m_copied")
        m_hi = sem("pr_m_hi")
        m_lo = sem("pr_m_lo")
        xf_stored = sem("pr_xf_stored")
        base_stored = sem("pr_base_stored")
        fT_stored = sem("pr_fT_stored")
        qkv_stored = [sem(f"pr_qkv_stored{g}") for g in range(3)]
        STORES = (32, 32, 16)
        x_rows = t["x"].rearrange("a (b t p) d -> (a b) p t d", p=P, t=TB)
        base_rows = t["base"].rearrange("(b t p) d -> b p t d", p=P, t=TB)
        xf_rows = t["xf"].rearrange("(b t p) d -> b p t d", p=P, t=TB)
        v_rows = t["v_part"].rearrange("(b t p) n -> b p t n", p=P, t=TB)
        CONSTS = 16 * 6
        CHAIN = 14
        AT_A1, AT_A2 = 1, 9

        with nc.Block() as block:
            @block.sync
            def _(sp):
                for stored, n in ((xf_stored, 16), (base_stored, 16), (fT_stored, 16), *zip(qkv_stored, STORES)):
                    sp.sem_inc(stored, n)

                def rows(it, i):
                    b = 2 * it + i
                    sp.wait_ge(xf_done, b * TB + 2 * TB)
                    sp.dma_start(xf_rows[b], xf[:, :]).then_inc(xf_stored, 16)
                    sp.wait_ge(base_done, b * TB + TB)
                    sp.dma_start(base_rows[b], base[:, :]).then_inc(base_stored, 16)

                def turned_tokens(it, i):
                    b = 2 * it + i
                    sp.wait_ge(turned_lo, b * NTR + NTR + 2)
                    sp.dma_start(t["fT_part"][b], as_f32(fT[:, :])).then_inc(fT_stored, 16)

                rows(0, 0)
                turned_tokens(0, 0)

                def work(it, last):
                    for i in range(2):
                        b = 2 * it + i
                        for g, (_, end) in enumerate(GROUPS):
                            sp.wait_ge(m_lo, b * NM + end + 2)
                            if g < 2:
                                dst = t[("q_part", "k_part")[g]].rearrange("a (c p) (b n) -> b a p c n", p=P, n=BLK)[b]
                                for part in range(2):
                                    sp.dma_start(dst[part], as_f32(qk_part[:, part, g * KC:(g + 1) * KC])).then_inc(qkv_stored[g], 16)
                            else:
                                sp.dma_start(v_rows[b], as_f32(v_part[:, :]).rearrange("p t h a d -> p t (h a d)")).then_inc(qkv_stored[g], 16)
                            if g == 1 and (i == 0 or not last):
                                rows(it + i, 1 - i)
                                turned_tokens(it + i, 1 - i)

                with sp.Fori(0, ITS) as it:
                    work(it, False)
                work(ITS, True)
                for stored, n in ((xf_stored, 16), (base_stored, 16), (fT_stored, 16), *zip(qkv_stored, STORES)):
                    sp.wait_ge(stored, n * NB + n)

            @block.gpsimd
            def _(pool):
                pool.sem_inc(base_sum, TB)
                pool.memset(raw_r[:, :, E:RW], 0.0).then_inc(pad_done, 1)

                def add_up(it, i, k):
                    n = (2 * it + i) * TB + k
                    pool.wait_ge(xn_done, n + 1)
                    if k == 0:
                        pool.wait_ge(base_stored, (2 * it + i) * 16 + 16)
                    pool.tensor_tensor(base[:, k], x_in[:, k], xn[:, k], ALU.add).then_inc(base_sum, 1)
                    pool.wait_ge(base_sum, n + TB + 1)
                    pool.tensor_tensor(base[:, k], base[:, k], kept["bo"][:, :], ALU.add).then_inc(base_done, 1)

                for i in range(1, 3):
                    pool.wait_ge(w_hi, i + 1)
                    pool.tensor_tensor(kept["w_qkv"][:, 1, i], raw[i], as_f32(kept["w_qkv"][:, 0, i]),
                                       ALU.subtract).then_inc(w_lo, 1)
                pool.wait_ge(w_hi, 4)
                pool.tensor_tensor(kept["w_r"][:, 1], raw_r[:, :, :], as_f32(kept["w_r"][:, 0]),
                                   ALU.subtract).then_inc(w_lo, 1)
                pool.wait_ge(consts_loaded, CONSTS)
                for k in range(TB):
                    add_up(0, 0, k)

                def work(it, last):
                    for i in range(2):
                        b = 2 * it + i
                        for m in range(NM):
                            pool.wait_ge(m_copied, b * NM + m + 3 + 1)
                            g = m // KC
                            if m % KC == 0:
                                pool.wait_ge(qkv_stored[g], b * STORES[g] + STORES[g])
                            if m < MQK:
                                src, dst = qk[:, m % 2], qk_part[:, 0, m]
                            else:
                                src = v[:, m % 2].rearrange("p (h d) -> p h d", h=H)
                                dst = v_part[:, m - MQK, :, 0, :]
                            pool.sem_inc(kept["passed_pool"], 1)
                            pool.tensor_scalar(dst, src, 1.0, 1.0, ALU.mult, ALU.mult).then_inc(m_hi, 1)
                            if 0 <= m - NORM_AT < TB and (i == 0 or not last):
                                add_up(it + i, 1 - i, m - NORM_AT)

                with pool.Fori(0, ITS) as it:
                    work(it, False)
                work(ITS, True)

            @block.scalar
            def _(act):
                act.dma_start(x_in[:, :], x_rows[0]).then_inc(x_loaded, 16)
                for i, name in enumerate(("wq", "wk", "wv")):
                    act.dma_start(raw[i], t[name].rearrange("(c p) n -> p c n", p=P)).then_inc(w_loaded[i], 16)
                act.dma_start(kept["ident"][:, :], t["ident"]).then_inc(consts_loaded, 16)
                act.dma_start(kept["w_norm"][:, :], t["w_norm"].partition_broadcast(P)).then_inc(consts_loaded, 16)
                act.dma_start(kept["bv"][:, :], t["bv"].partition_broadcast(P)).then_inc(consts_loaded, 16)
                act.dma_start(kept["bo"][:, :], t["bo"].partition_broadcast(P)).then_inc(consts_loaded, 16)
                with nc.allow_non_contiguous_dma(reason="2 KB, once"):
                    act.dma_start(kept["bqk"][:, 0:KC], t["bq"].rearrange("(c p) -> p c", p=P)).then_inc(consts_loaded, 16)
                    act.dma_start(kept["bqk"][:, KC:2 * KC], t["bk"].rearrange("(c p) -> p c", p=P)).then_inc(consts_loaded, 16)
                act.wait_ge(pad_done, 1)
                act.dma_start(raw_r[:, :, 0:E], t["w_router"].rearrange("(c p) n -> p c n", p=P)).then_inc(w_loaded[3], 16)
                with nc.allow_non_contiguous_dma(reason="one column, once"):
                    act.dma_start(raw_r[:, :, E:E + 1], t["w_sgate"].rearrange("(c p) n -> p c n", p=P)).then_inc(w_loaded[3], 16)

                def roots(it, i):
                    b = 2 * it + i
                    for src, at in ((a1, AT_A1), (a2, AT_A2)):
                        act.wait_ge(chain, b * CHAIN + at)
                        act.activation(root[:, :], src[:, :], ACT.Sqrt).then_inc(root_done, 1)

                def high(it, i, k):
                    b = 2 * it + i
                    for j in range(2):
                        n = 2 * k + j
                        act.wait_ge(turned, b * NTR + NTR + n + 1)
                        if n == 0:
                            act.wait_ge(m_done, b * NM + NM)
                        if n == 1:
                            act.wait_ge(r_done, b + 1)
                            act.wait_ge(fT_stored, 16 * b + 16)
                        dst = (xT[:, i], fT)[j]
                        act.activation(dst[:, 0, :, k * P:(k + 1) * P], ps_t[j][:, :, :], ACT.Copy).then_inc(turned_hi, 1)

                def load(it, i):
                    b = 2 * it + i
                    act.wait_ge(xf_done, b * TB + TB)
                    act.wait_ge(base_sum, b * TB + TB)
                    act.dma_start(x_in[:, :], x_rows[b]).then_inc(x_loaded, 16)

                def logits_turned(it, i):
                    b = 2 * it + i
                    act.wait_ge(r_done, b + 2)
                    act.wait_ge(r_back, b + 1)
                    act.activation(lT[:, :], ps_l[:, :], ACT.Copy).then_inc(l_copied, 1)

                def logits(it, i):
                    b = 2 * it + i
                    act.wait_ge(r_back, b + 2)
                    act.activation(kept["logits"][:, bass.ds(b * TB, TB)], ps_r[:, :, :], ACT.Copy).then_inc(r_copied, 1)

                act.sem_inc(r_copied, 1)
                act.wait_ge(w_loaded[0], 16)
                act.activation(kept["w_qkv"][:, 0, 0], raw[0], ACT.Copy).then_inc(w_hi, 1)
                roots(0, 0)
                for i in range(1, 3):
                    act.wait_ge(w_loaded[i], 16)
                    act.activation(kept["w_qkv"][:, 0, i], raw[i], ACT.Copy).then_inc(w_hi, 1)
                act.wait_ge(w_loaded[3], 32)
                act.activation(kept["w_r"][:, 0], raw_r[:, :, :], ACT.Copy).then_inc(w_hi, 1)
                for k in range(TB):
                    high(0, 0, k)
                load(0, 1)
                act.dma_start(t["alibi_s"], t["alibi"]).then_inc(consts_loaded, 16)
                logits_turned(0, 0)

                def work(it, last):
                    for i in range(2):
                        if i == 0 or not last:
                            roots(it + i, 1 - i)
                        logits(it, i)
                        if i == 0 or not last:
                            for k in range(TB):
                                high(it + i, 1 - i, k)
                            if not last:
                                load(it + 1, i)
                            logits_turned(it + i, 1 - i)

                with act.Fori(0, ITS) as it:
                    work(it, False)
                work(ITS, True)
                act.wait_ge(consts_loaded, CONSTS + 16)

            @block.vector
            def _(dve):
                for credit, n in ((xf_done, TB), (turned_lo, 2), (m_copied, 3), (m_lo, 2)):
                    dve.sem_inc(credit, n)
                var = mean_var[:, :, 1]

                def statistics(it, i, stage):
                    b = 2 * it + i
                    n = [(0, 0, 1, 9)[stage]]

                    def link(ins):
                        n[0] += 1
                        ins.then_inc(chain, 1)
                        dve.wait_ge(chain, b * CHAIN + n[0])

                    def newton(to, a):
                        link(dve.reciprocal(to, root[:, :]))
                        link(dve.tensor_tensor(tmp[:, :], to, to, ALU.mult))
                        link(dve.tensor_tensor(tmp[:, :], tmp[:, :], a, ALU.mult))
                        link(dve.tensor_scalar(tmp[:, :], tmp[:, :], -0.5, 1.5, ALU.mult, ALU.add))
                        link(dve.tensor_tensor(to, to, tmp[:, :], ALU.mult))

                    if stage == 0:
                        dve.wait_ge(x_loaded, 16 * b + 16)
                        for k in range(TB):
                            dve.bn_stats(six[:, k], x_in[:, k]).then_inc(six_done, 1)
                    if stage == 1:
                        dve.wait_ge(xf_done, b * TB + TB)
                        dve.wait_ge(six_done, b * TB + TB)
                        dve.sem_inc(kept["passed_dve"], 1)
                        for k in range(TB):
                            dve.bn_aggr(mean_var[:, k], six[:, k]).then_inc(mv_done, 1)
                        dve.wait_ge(mv_done, b * TB + TB)
                        link(dve.tensor_scalar(a1[:, :], var, LN_EPS, None, ALU.add))
                    if stage == 2:
                        dve.wait_ge(root_done, 2 * b + 1)
                        newton(rstd[:, 0], a1[:, :])
                        link(dve.tensor_tensor(tmp[:, :], rstd[:, 0], rstd[:, 0], ALU.mult))
                        link(dve.tensor_tensor(tmp[:, :], tmp[:, :], var, ALU.mult))
                        link(dve.tensor_scalar(a2[:, :], tmp[:, :], RMS_EPS, None, ALU.add))
                    if stage == 3:
                        dve.wait_ge(root_done, 2 * b + 2)
                        newton(rstd[:, 1], a2[:, :])

                def normal(it, i, k):
                    b = 2 * it + i
                    dve.wait_ge(turned, b * NTR + 2 * k + 2)
                    dve.wait_ge(base_sum, b * TB + k + 1)
                    if k == 0:
                        dve.wait_ge(xf_stored, 16 * b + 16)
                    dve.tensor_scalar(xn[:, k], x_in[:, k], mean_var[:, k, 0:1], rstd[:, 0, k:k + 1],
                                      ALU.subtract, ALU.mult).then_inc(xn_done, 1)
                    dve.wait_ge(xn_done, b * TB + k + 1)
                    dve.scalar_tensor_tensor(out=xf[:, k], in0=xn[:, k], scalar=rstd[:, 1, k:k + 1],
                                             in1=kept["w_norm"][:, :], op0=ALU.mult, op1=ALU.mult).then_inc(xf_done, 1)

                def low_turned(it, i, k):
                    for j in range(2):
                        dst = (xT[:, i], fT)[j]
                        dve.wait_ge(turned_hi, (2 * it + i) * NTR + 2 * k + j + 1)
                        dve.tensor_tensor(dst[:, 1, :, k * P:(k + 1) * P], ps_t[j][:, :, :],
                                          as_f32(dst[:, 0, :, k * P:(k + 1) * P]), ALU.subtract).then_inc(turned_lo, 1)

                for stage in range(4):
                    statistics(0, 0, stage)
                dve.wait_ge(consts_loaded, CONSTS)
                for k in range(TB):
                    normal(0, 0, k)
                dve.wait_ge(w_hi, 1)
                dve.tensor_tensor(kept["w_qkv"][:, 1, 0], raw[0], as_f32(kept["w_qkv"][:, 0, 0]),
                                  ALU.subtract).then_inc(wq_lo, 1)
                for k in range(TB):
                    low_turned(0, 0, k)

                def work(it, last):
                    for i in range(2):
                        b = 2 * it + i
                        more = i == 0 or not last

                        def low(m):
                            dve.wait_ge(m_hi, b * NM + m + 1)
                            if m < MQK:
                                src, dst, high = qk[:, m % 2], qk_part[:, 1, m], qk_part[:, 0, m]
                            else:
                                src = v[:, m % 2].rearrange("p (h d) -> p h d", h=H)
                                dst, high = v_part[:, m - MQK, :, 1, :], v_part[:, m - MQK, :, 0, :]
                            dve.tensor_tensor(dst, src, as_f32(high), ALU.subtract).then_inc(m_lo, 1)

                        for m in range(NM):
                            if more and 0 <= m - LOW_AT < TB:
                                low_turned(it + i, 1 - i, m - LOW_AT)
                            dve.wait_ge(m_done, b * NM + 2 * NM + m + 1)
                            dve.wait_ge(m_lo, b * NM + m + 1)
                            if m < MQK:
                                bias = kept["bqk"][:, m:m + 1]
                                scaling = (Q_SCALE, ALU.add, ALU.mult) if m < KC else (None, ALU.add)
                                dve.tensor_scalar(qk[:, m % 2], ps_m[m % 3][:, :], bias, *scaling).then_inc(m_copied, 1)
                            else:
                                dve.tensor_tensor(v[:, m % 2], ps_m[m % 3][:, :], kept["bv"][:, :], ALU.add).then_inc(m_copied, 1)
                            if m >= 1:
                                low(m - 1)
                            if more and m < 4:
                                statistics(it + i, 1 - i, m)
                            if more and 0 <= m - NORM_AT < TB:
                                normal(it + i, 1 - i, m - NORM_AT)
                        low(NM - 1)

                with dve.Fori(0, ITS) as it:
                    work(it, False)
                work(ITS, True)

            @block.tensor
            def _(pe):
                for credit, n in ((turned, NTR), (m_done, 2 * NM), (r_done, 1), (r_back, 1)):
                    pe.sem_inc(credit, n)

                def turn(it, i, k):
                    b = 2 * it + i
                    for j, (src, ready, credit) in enumerate(((xn, xn_done, 0), (xf, xf_done, TB))):
                        pe.wait_ge(ready, b * TB + k + 1 + credit)
                        pe.wait_ge(turned_lo, b * NTR + 2 * k + j + 1)
                        for c in range(KC):
                            mm = pe.transpose(ps_t[j][:, c], src[:, k, c * P:(c + 1) * P], kept["ident"][:, :])
                        mm.then_inc(turned, 1)

                def route(it, i, first=False):
                    b = 2 * it + i
                    pe.wait_ge(turned_lo, b * NTR + NTR + 2)
                    if not first:
                        pe.wait_ge(l_copied, b)
                    for c in range(KC):
                        for n, (x, y) in enumerate(THREE):
                            mm = pe.matmul(ps_l[:, :], kept["w_r"][:, x, c], fT[:, y, c],
                                           start=(c == 0 and n == 0), stop=(c == KC - 1 and n == 2))
                    mm.then_inc(r_done, 1)

                def turn_logits(it, i):
                    b = 2 * it + i
                    pe.wait_ge(l_copied, b + 1)
                    pe.wait_ge(r_copied, b + 1)
                    pe.sem_inc(kept["passed_pe"], 1)
                    for k in range(TB):
                        mm = pe.transpose(ps_r[:, k], lT[:, k * P:(k + 1) * P], kept["ident"][0:RW, 0:RW])
                    mm.then_inc(r_back, 1)

                pe.wait_ge(consts_loaded, CONSTS)
                for k in range(TB):
                    turn(0, 0, k)
                pe.wait_ge(w_lo, 3)
                pe.wait_ge(wq_lo, 1)
                route(0, 0, first=True)

                def work(it, last):
                    for i in range(2):
                        b = 2 * it + i
                        more = i == 0 or not last
                        for m in range(NM):
                            pe.wait_ge(m_copied, b * NM + m + 1)
                            for c in range(KC):
                                for n, (x, y) in enumerate(THREE):
                                    if m < MQK:
                                        w = kept["w_qkv"][:, y, m // KC, c, (m % KC) * P:(m % KC + 1) * P]
                                        args = (w, xT[:, i, x, c])
                                    else:
                                        k = m - MQK
                                        args = (xT[:, i, x, c, k * P:(k + 1) * P], kept["w_qkv"][:, y, 2, c])
                                    mm = pe.matmul(ps_m[m % 3][:, :], *args, start=(c == 0 and n == 0),
                                                   stop=(c == KC - 1 and n == 2))
                            mm.then_inc(m_done, 1)
                            if m == 1:
                                turn_logits(it, i)
                            if more and 0 <= m - TURN_AT < TB:
                                turn(it + i, 1 - i, m - TURN_AT)
                        if more:
                            route(it + i, 1 - i)

                with pe.Fori(0, ITS) as it:
                    work(it, False)
                work(ITS, True)


MAXW = 1024
AHEAD = 2
WRAP = 4
TURN_LEAD = 3
LOW_LAG = 1
LAG = 3
P_SLOTS = 4


def high_by(pair):
    return int(pair % 2 == 0)


def low_by(pair):
    return int(pair % 2 == 1)


def pairs_before(pair, maker, by):
    return sum(maker(p) == by for p in range(pair))


def attention_plan():
    n_u, stream, turn = 2 * NB, [], None
    for u in range(n_u):
        j = u % NB
        for i in range(TB * j, TB * j + TB):
            for k0 in range(0, P * (i + 1), MAXW):
                stream.append(["max", u, 0, i, k0, min(MAXW, P * (i + 1) - k0)])
                if turn:
                    stream.append(turn)
                    turn = None
        turn = ["turn", u, 0]
        if u in (WRAP - 1, n_u - 1):
            stream.append(turn)
            turn = None
    for a, step in enumerate(stream):
        step[2] = a
    N_A = len(stream)
    ahead = 1 + [s[:2] for s in stream].index(["turn", WRAP - 1])
    before = [("load", 0, 0)] + [tuple(s) for s in stream[:ahead]]
    queue = [tuple(s) for s in stream[ahead:]]
    queue += [(s[0], s[1] + n_u, s[2] + N_A, *s[3:]) for s in stream[:ahead]]
    n_max = sum(s[0] == "max" for s in stream)
    starts, n = [], 0
    for u in range(n_u):
        starts.append(n)
        n += 2 * (u % NB) + 2
    N_P = n

    plan = [("load", 1, 0)]
    done = 0

    def maxima(pair, half):
        nonlocal done
        while queue:
            u = queue[0][1]
            due = u < n_u and starts[u] - TURN_LEAD <= pair
            if done > n_max * (pair + 0.5 * half) / (N_P - AHEAD) and not due:
                break
            step = queue.pop(0)
            plan.append(step)
            if step[0] == "max":
                done += 1

    b = pair = 0
    lows, values = [], []


    def value():
        step = values.pop(0)
        plan.append(step)
        if step[6]:
            plan.append(("out", step[1], step[2]))
            if step[1] == NB - 1:
                plan.append(("load", 0, 1))

    for u in range(n_u):
        pairs = 2 * (u % NB) + 2
        for p in range(pairs):
            c0 = 2 * P if p == pairs - 1 else 0
            for half in range(2):
                plan.append(("score", u, b, 2 * p + half, c0))
                b += 1
            for half in range(2):
                maxima(pair, half)
            if len(lows) >= LOW_LAG:
                plan.append(lows.pop(0))
            if len(values) >= LAG:
                value()
            lows.append(("low", u, pair, c0))
            values.append(("value", u, pair, c0, 2 * p, p == 0, p == pairs - 1))
            pair += 1
    plan += lows
    while values:
        maxima(pair, 0)
        value()
        pair += 1
    maxima(2 * pair, 0)
    last = [s for s in plan if s[1] < n_u and s != ("load", 0, 1)]
    return before, plan, last, N_A, b, N_P


def attention_phase(nc, t, kept):
    ctx, sb, ps, sem = open_scope(nc)
    before, plan, last_plan, N_A, N_B, N_P = attention_plan()
    N_U = 2 * NB
    R_MAX = 3 * HD + 2
    R_ALL = R_MAX + 2
    with ctx:
        q = [sb(f"at_q{i}", [R_ALL, S], F32R) for i in range(2)]
        k = [sb(f"at_k{i}", [R_ALL, S], F32R) for i in range(2)]
        v = [sb(f"at_v{i}", [P, NT, 3 * HD], F32R) for i in range(2)]
        ex = sb("at_ex", [P, P_SLOTS, 2, BLK])
        ex_hi = sb("at_ex_hi", [P, P_SLOTS, 2, BLK], F32R)
        ex_lo = sb("at_ex_lo", [P, P_SLOTS, 2, BLK], F32R)
        part_max = sb("at_part_max", [P, TB, S // MAXW])
        neg_max = sb("at_neg_max", [P, TB])
        max_row = sb("at_max_row", [TB, 2, 2, P], F32R)
        out_sb = sb("at_out", [3 * HD, 2, BLK])
        mask_q = sb("at_mask_q", [P, P], BF16)
        mask_k = sb("at_mask_k", [P, 2 * P], BF16)
        ident_b = sb("at_ident_b", [P, P], BF16)
        mask_f = sb("at_mask_f", [P, 3 * P])
        ps_a = [ps(f"at_ps_a{i}", [P, MAXW]) for i in range(2)]
        ps_b = [ps(f"at_ps_b{i}", [P, BLK]) for i in range(3)]
        ps_o = ps("at_ps_o", [P, BLK])

        masks_loaded = sem("at_masks_loaded")
        consts_done = sem("at_consts_done")
        ones_done = sem("at_ones_done")
        ones_dve = sem("at_ones_dve")
        loaded = [sem(f"at_loaded{i}") for i in range(2)]
        v_loaded = [sem(f"at_v_loaded{i}") for i in range(2)]
        head_done = [sem(f"at_head_done{i}") for i in range(2)]
        a_done = sem("at_a_done")
        a_free = sem("at_a_free")
        neg_done = sem("at_neg_done")
        row_done = sem("at_row_done")
        row_loaded = [sem(f"at_row_loaded{i}") for i in range(2)]
        b_done = sem("at_b_done")
        b_free = sem("at_b_free")
        hi_done = (sem("at_hi_done_pool"), sem("at_hi_done_act"))
        lo_done = (sem("at_lo_done"), sem("at_lo_done_pool"))
        v_done = sem("at_v_done")
        o_free = sem("at_o_free")
        o_stored = [sem(f"at_o_stored{i}") for i in range(2)]

        STORE = 16 * 3
        LO_CREDIT = [sum(low_by(p) == by for p in range(P_SLOTS)) for by in range(2)]

        def wait_high(eng, it, pair):
            by = high_by(pair)
            eng.wait_ge(hi_done[by], it * pairs_before(N_P, high_by, by) + pairs_before(pair, high_by, by) + 1)

        def wait_low(eng, it, pair, behind):
            by = low_by(pair)
            eng.wait_ge(lo_done[by], it * pairs_before(N_P, low_by, by) + pairs_before(pair, low_by, by) + 1
                        + (0 if behind else LO_CREDIT[by]))

        def wait_taken(eng, it, pair):
            eng.wait_ge(v_done, it * N_P + pair + 1)

        def exponentials(eng, it, pair):
            eng.wait_ge(b_free, it * N_B + 2 * pair + 2 + 3)

        v_src = t["v_part"].rearrange("(t p) (h n) -> h p t n", p=P, h=H)

        ITS = H // 2 - 1

        with nc.Block() as block:
            @block.scalar
            def _(act):
                act.dma_start(mask_f[:, :], t["masks"]).then_inc(masks_loaded, 16)
                act.sem_inc(b_free, 3)
                act.sem_inc(o_free, 1)

                def work(it, steps):
                    for step in steps:
                        if step[0] == "score":
                            _, u, b, kt, c0 = step
                            pair = b // 2
                            act.wait_ge(b_done, it * N_B + b + 1)
                            if b % 2 == 0:
                                wait_low(act, it, pair, behind=True)
                            act.activation(ex[:, pair % P_SLOTS, b % 2, c0:], ps_b[b % 3][:, c0:],
                                           ACT.Exp).then_inc(b_free, 1)
                        if step[0] == "low" and high_by(step[2]) == 1:
                            _, u, pair, c0 = step
                            s = pair % P_SLOTS
                            exponentials(act, it, pair)
                            wait_taken(act, it, pair)
                            act.activation(ex_hi[:, s, :, c0:], ex[:, s, :, c0:], ACT.Copy).then_inc(hi_done[1], 1)
                        if step[0] == "out":
                            _, u, pair = step
                            act.wait_ge(v_done, it * N_P + pair + P_SLOTS + 1)
                            act.wait_ge(o_stored[u % 2], it * STORE * NB + STORE * (u // 2) + STORE)
                            act.activation(out_sb[:, u % 2], ps_o[0:3 * HD, :], ACT.Copy).then_inc(o_free, 1)

                with act.Fori(0, ITS) as it:
                    work(it, plan)
                work(ITS, last_plan)

            @block.gpsimd
            def _(pool):
                for n, x in enumerate((v[0][:, :, 2 * HD:], q[1][3 * HD:R_ALL, :], v[1][:, :, 2 * HD:])):
                    pool.memset(as_f32(x), 1.0).then_inc(ones_done, 1)
                    pool.wait_ge(ones_done, n + 1)
                pool.sem_inc(lo_done[1], LO_CREDIT[1])

                def work(it, steps):
                    for step in steps:
                        if step[0] != "low":
                            continue
                        _, u, pair, c0 = step
                        s = pair % P_SLOTS
                        if high_by(pair) == 0:
                            exponentials(pool, it, pair)
                            wait_taken(pool, it, pair)
                            pool.sem_inc(kept["passed_pool"], 1)
                            pool.tensor_scalar(ex_hi[:, s, :, c0:], ex[:, s, :, c0:], 1.0, 1.0,
                                               ALU.mult, ALU.mult).then_inc(hi_done[0], 1)
                        if low_by(pair) == 1:
                            wait_high(pool, it, pair)
                            pool.tensor_tensor(ex_lo[:, s, :, c0:], ex[:, s, :, c0:], as_f32(ex_hi[:, s, :, c0:]),
                                               ALU.subtract).then_inc(lo_done[1], 1)

                with pool.Fori(0, ITS) as it:
                    work(it, plan)
                work(ITS, last_plan)

            @block.vector
            def _(dve):
                for x in (q[0], k[0], k[1]):
                    dve.memset(as_f32(x[3 * HD:R_ALL, :]), 1.0).then_inc(ones_dve, 1)
                dve.wait_ge(masks_loaded, 16)
                dve.tensor_copy(mask_q[:, :], mask_f[:, 0:P]).then_inc(consts_done, 1)
                dve.tensor_copy(mask_k[:, :], mask_f[:, P:]).then_inc(consts_done, 1)
                dve.tensor_copy(ident_b[:, :], kept["ident"][:, :]).then_inc(consts_done, 1)
                dve.sem_inc(a_free, 2)
                dve.sem_inc(lo_done[0], LO_CREDIT[0])
                for i in range(2):
                    dve.sem_inc(row_loaded[i], 32)

                def work(it, steps):
                    for step in steps:
                        if step[0] == "max":
                            _, u, a, i, k0, width = step
                            dve.wait_ge(a_done, it * N_A + a + 1)
                            if k0 == 0 and i % TB == 0:
                                dve.wait_ge(neg_done, it * N_U + u + 1)
                            dve.reduce_max(part_max[:, i % TB, k0 // MAXW:k0 // MAXW + 1], ps_a[a % 2][:, 0:width],
                                           AX.X).then_inc(a_free, 1)
                            if k0 + width == P * (i + 1) and i % TB == TB - 1:
                                dve.wait_ge(a_free, it * N_A + a + 2 + 1)
                                chunks = k0 // MAXW + 1
                                dve.tensor_reduce(neg_max[:, :], part_max[:, :, 0:chunks], AX.X, ALU.max,
                                                  negate=True).then_inc(neg_done, 1)
                        if step[0] == "turn":
                            _, u, a = step
                            dve.wait_ge(a_done, it * N_A + a + 1)
                            dve.wait_ge(row_loaded[u % 2], it * 32 * NB + 32 * (u // 2) + 32)
                            dve.tensor_copy(max_row[:, u % 2, 0], ps_a[a % 2][0:TB, 0:P]).then_inc(row_done, 1)
                            dve.wait_ge(row_done, it * N_U + u + 1)
                            dve.tensor_tensor(max_row[:, u % 2, 1], ps_a[a % 2][0:TB, 0:P],
                                              as_f32(max_row[:, u % 2, 0]), ALU.subtract).then_inc(a_free, 1)
                        if step[0] == "low" and low_by(step[2]) == 0:
                            _, u, pair, c0 = step
                            s = pair % P_SLOTS
                            wait_high(dve, it, pair)
                            dve.tensor_tensor(ex_lo[:, s, :, c0:], ex[:, s, :, c0:], as_f32(ex_hi[:, s, :, c0:]),
                                              ALU.subtract).then_inc(lo_done[0], 1)

                work(0, before)
                with dve.Fori(0, ITS) as it:
                    work(it, plan)
                work(ITS, last_plan)

            @block.sync
            def _(sp):
                for i in range(2):
                    sp.sem_inc(o_stored[i], STORE)

                def work(it, steps, first=False):
                    for step in steps:
                        if step[0] == "load":
                            _, i, ahead = step
                            if not first:
                                sp.wait_ge(head_done[i], it + 1)
                            h = 2 * it + 2 * ahead + i
                            for dst, src, order in ((q[i], "q_part", (0, 1, 0)), (k[i], "k_part", (0, 0, 1))):
                                for r, part in enumerate(order):
                                    sp.dma_start(as_f32(dst[r * HD:(r + 1) * HD, :]),
                                                 t[src][part, bass.ds(h * HD, HD), :]).then_inc(loaded[i], 16)
                            if first:
                                sp.wait_ge(ones_dve, 2)
                            sp.dma_start(as_f32(k[i][3 * HD:3 * HD + 2, :]), t["alibi_s"][h]).then_inc(loaded[i], 16)
                            sp.dma_start(as_f32(v[i][:, :, 0:2 * HD]), v_src[h]).then_inc(v_loaded[i], 16)
                        if step[0] == "turn":
                            _, u, a = step
                            sp.wait_ge(a_free, it * N_A + a + 2 + 1)
                            g, j = u // NB % 2, u % NB
                            for part in range(2):
                                sp.dma_start(as_f32(q[g][R_MAX + part:R_MAX + part + 1, j * BLK:(j + 1) * BLK]),
                                             as_f32(max_row[:, u % 2, part])).then_inc(row_loaded[u % 2], 16)
                        if step[0] == "out":
                            _, u, pair = step
                            sp.wait_ge(o_free, it * N_U + u + 2)
                            j = u % NB
                            h, cols = 2 * it + u // NB, slice(j * BLK, (j + 1) * BLK)
                            for part in range(2):
                                sp.dma_start(t["att_v"][part, bass.ds(h * HD, HD), cols],
                                             out_sb[part * HD:(part + 1) * HD, u % 2]).then_inc(o_stored[u % 2], 16)
                            sp.dma_start(t["att_sum"][bass.ds(h, 1), cols], out_sb[2 * HD:2 * HD + 1, u % 2]).then_inc(o_stored[u % 2], 16)

                work(0, before, first=True)
                sp.wait_ge(ones_dve, 3)
                sp.wait_ge(ones_done, 3)
                with sp.Fori(0, ITS) as it:
                    work(it, plan)
                work(ITS, last_plan)
                for i in range(2):
                    sp.wait_ge(o_stored[i], STORE * NB * (H // 2) + STORE)

            @block.tensor
            def _(pe):
                pe.sem_inc(head_done[1], 1)
                pe.sem_inc(v_done, P_SLOTS)
                pe.sem_inc(neg_done, 1)
                pe.wait_ge(ones_dve, 3)
                pe.wait_ge(ones_done, 3)
                pe.wait_ge(consts_done, 3)
                LOADS = 16 * 7

                def work(it, steps):
                    for step in steps:
                        if step[0] == "max":
                            _, u, a, i, k0, width = step
                            g = u // NB % 2
                            if i == 0:
                                pe.wait_ge(loaded[g], (it + u // N_U) * LOADS + LOADS)
                            pe.wait_ge(a_free, it * N_A + a + 1)
                            for w0 in range(0, width, BLK):
                                w = min(BLK, width - w0)
                                diagonal = k0 + w0 + w == P * (i + 1)
                                mm = pe.matmul(ps_a[a % 2][:, w0:w0 + w], q[g][0:R_MAX, i * P:(i + 1) * P],
                                               k[g][0:R_MAX, k0 + w0:k0 + w0 + w], start=True, stop=not diagonal)
                                if diagonal:
                                    mm = pe.matmul(ps_a[a % 2][:, w0 + w - P:w0 + w], ident_b[:, :], mask_q[:, :],
                                                   start=False, stop=True)
                            mm.then_inc(a_done, 1)
                        if step[0] == "turn":
                            _, u, a = step
                            pe.wait_ge(neg_done, it * N_U + u + 2)
                            pe.wait_ge(a_free, it * N_A + a + 1)
                            pe.transpose(ps_a[a % 2][0:TB, 0:P], neg_max[:, :], kept["ident"][:, :]).then_inc(a_done, 1)
                        if step[0] == "score":
                            _, u, b, kt, c0 = step
                            g, j = u // NB, u % NB
                            if kt == 0:
                                pe.wait_ge(row_loaded[u % 2], it * 32 * NB + 32 * (u // 2) + 64)
                            pe.wait_ge(b_free, it * N_B + b + 1)
                            r = kt - TB * j
                            mm = pe.matmul(ps_b[b % 3][:, c0:], k[g][0:R_ALL, kt * P:(kt + 1) * P],
                                           q[g][0:R_ALL, j * BLK + c0:(j + 1) * BLK], start=True, stop=r < 0)
                            if r >= 0:
                                w = P * (1 + r % 2)
                                mm = pe.matmul(ps_b[b % 3][:, c0:c0 + w], ident_b[:, :], mask_k[:, 2 * P - w:],
                                               start=False, stop=True)
                            mm.then_inc(b_done, 1)
                        if step[0] == "value":
                            _, u, pair, c0, kt, first, last = step
                            g, s = u // NB, pair % P_SLOTS
                            wait_low(pe, it, pair, behind=False)
                            if first and kt == 0 and u % NB == 0:
                                pe.wait_ge(v_loaded[g], 16 * it + 16)
                            if first:
                                pe.wait_ge(o_free, it * N_U + u + 1)
                            for half in range(2):
                                for x, part in enumerate((ex_hi, ex_lo)):
                                    mm = pe.matmul(ps_o[0:3 * HD, c0:], v[g][:, kt + half, :], part[:, s, half, c0:],
                                                   start=first and half == 0 and x == 0, stop=last and half == 1 and x == 1)
                            mm.then_inc(v_done, 1)
                            if last and u % NB == NB - 1:
                                pe.wait_ge(v_done, it * N_P + pair + P_SLOTS + 1)
                                pe.sem_inc(head_done[g], 1)

                work(0, before)
                with pe.Fori(0, ITS) as it:
                    work(it, plan)
                work(ITS, last_plan)


def routing_phase(nc, t, kept):
    ctx, sb, ps, sem = open_scope(nc)
    WHOLE = [P, NT, E]
    with ctx:
        logits = kept["logits"][:, :, 0:E]
        probs = sb("ro_probs", WHOLE)
        work = sb("ro_work", WHOLE)
        chosen = [sb(f"ro_chosen{k}", WHOLE) for k in range(TOPK)]
        mask = sb("ro_mask", WHOLE)
        before = [sb(f"ro_before{i}", WHOLE) for i in range(2)]
        mask_b = sb("ro_mask_b", WHOLE, BF16)
        before_b = sb("ro_before_b", WHOLE, BF16)
        experts = sb("ro_experts", [P, E])
        upper_f = sb("ro_upper_f", [P, P])
        upper = sb("ro_upper", [P, P], BF16)
        ones_b = sb("ro_ones", [P, P], BF16)
        best = sb("ro_best", [P, NT, 8])
        best_at = sb("ro_best_at", [P, NT, 8], U32)
        at_f = sb("ro_at_f", [P, NT, 8])
        one = sb("ro_one", [P, NT])
        place = sb("ro_place", [P, TOPK, NT])
        late = sb("ro_late", [P, TOPK, NT])
        slot = sb("ro_slot", [P, TOPK, NT])
        first = sb("ro_first", [P, TOPK, NT])
        zeros = sb("ro_zeros", [P, E * CAP // P], I32)
        SLOTS = 4
        raw = sb("ro_raw", [P, SLOTS, FS])
        ps_place = ps("ro_ps_place", [P, NT, E])
        raw_loaded = [sem(f"ro_raw_loaded{i}") for i in range(SLOTS)]
        raw_hi = sem("ro_raw_hi")
        raw_lo = sem("ro_raw_lo")
        consts = sem("ro_consts")
        chain = sem("ro_chain")
        exp_done = sem("ro_exp_done")
        place_done = sem("ro_place_done")
        zeros_done = sem("ro_zeros_done")
        table_clear = sem("ro_table_clear")
        iotas = sem("ro_iotas")
        counts_ready = sem("ro_counts_ready")
        probs_ready = sem("ro_probs_ready")

        w_in, w_out = kept["shared_in"], kept["shared_out"]
        pieces = [(w_in[:, :, i, c], t[name][c * P:(c + 1) * P, :], FS) for c in range(KC)
                  for i, name in enumerate(("sw_gate", "sw_up"))]
        w_down = t["sw_down"].rearrange("(c p) n -> p c n", p=P)
        for c in range(0, FS // P, 2):
            m = min(2, FS // P - c)
            pieces.append((w_out[:, :, c:c + m].rearrange("p a c n -> p a (c n)"),
                           w_down[:, c:c + m, :], m * D))
        EARLY = 1

        def per_tile(x):
            return x.unsqueeze(2).to_broadcast(WHOLE)

        with nc.Block() as block:
            @block.sync
            def _(sp):
                sp.dma_start(experts[:, :], t["experts"].partition_broadcast(P)).then_inc(consts, 16)
                sp.dma_start(upper_f[:, :], t["upper"]).then_inc(consts, 16)
                for n, (_, src, width) in enumerate(pieces):
                    if n >= SLOTS:
                        sp.wait_ge(raw_lo, n - SLOTS + 1)
                    dst = raw[:, n % SLOTS, 0:width]
                    if len(src.shape) == 3:
                        dst = dst.rearrange("p (c n) -> p c n", n=D)
                    sp.dma_start(dst, src).then_inc(raw_loaded[n % SLOTS], 16)
                sp.wait_ge(zeros_done, 1)
                sp.dma_start(t["slot_token"].rearrange("(p n) a -> p (n a)", p=P), zeros[:, :]).then_inc(table_clear, 16)
                sp.wait_ge(table_clear, 16)

            @block.gpsimd
            def _(pool):
                pool.memset(zeros[:, :], 0).then_inc(zeros_done, 1)
                pool.iota(kept["token"][:, :], pattern=[[P, NT]], base=0, channel_multiplier=1).then_inc(iotas, 1)
                for n, (dst, src, width) in enumerate(pieces):
                    pool.wait_ge(raw_hi, n + 1)
                    pool.tensor_tensor(dst[:, 1], raw[:, n % SLOTS, 0:width], as_f32(dst[:, 0]), ALU.subtract).then_inc(raw_lo, 1)

            @block.scalar
            def _(act):
                def high(start, end):
                    for n, (dst, src, width) in enumerate(pieces[start:end], start):
                        act.wait_ge(raw_loaded[n % SLOTS], 16 * (n // SLOTS + 1))
                        act.activation(dst[:, 0], raw[:, n % SLOTS, 0:width], ACT.Copy).then_inc(raw_hi, 1)

                high(0, EARLY)
                act.wait_ge(probs_ready, 1)
                act.activation(probs[:, :, :], work[:, :, :], ACT.Exp).then_inc(exp_done, 1)
                act.activation(kept["shared_gate"][:, :], kept["logits"][:, :, E], ACT.Sigmoid).then_inc(exp_done, 1)
                high(EARLY, len(pieces))

            @block.tensor
            def _(pe):
                pe.wait_ge(counts_ready, 1)
                half = NT // 2
                for i in range(2):
                    pe.matmul(ps_place[:, i * half:(i + 1) * half], upper[:, :], mask_b[:, i * half:(i + 1) * half],
                              start=True, stop=False)
                    pe.matmul(ps_place[:, i * half:(i + 1) * half], ones_b[:, :], before_b[:, i * half:(i + 1) * half],
                              start=False, stop=True).then_inc(place_done, 1)

            @block.vector
            def _(dve):
                n = [0]

                def link(ins):
                    n[0] += 1
                    ins.then_inc(chain, 1)
                    dve.wait_ge(chain, n[0])

                dve.wait_ge(consts, 32)
                link(dve.tensor_copy(upper[:, :], upper_f[:, :]))
                link(dve.memset(ones_b[:, :], 1.0))
                link(dve.tensor_reduce(one[:, :], logits, AX.X, ALU.max))
                dve.tensor_tensor(work[:, :, :], logits, per_tile(one[:, :]), ALU.subtract).then_inc(probs_ready, 1)
                dve.wait_ge(exp_done, 1)
                link(dve.tensor_reduce(one[:, :], probs[:, :, :], AX.X, ALU.add))
                link(dve.reciprocal(one[:, :], one[:, :]))
                link(dve.tensor_tensor(probs[:, :, :], probs[:, :, :], per_tile(one[:, :]), ALU.mult))
                for i in range(NT):
                    link(dve.max(best[:, i], probs[:, i]))
                    dve.max_index(best_at[:, i], best[:, i], probs[:, i]).then_inc(iotas, 1)
                dve.wait_ge(iotas, NT + 1)
                link(dve.tensor_copy(at_f[:, :, :], best_at[:, :, :]))
                for k in range(TOPK):
                    link(dve.tensor_tensor(chosen[k][:, :, :], experts[:, :].unsqueeze(1).to_broadcast(WHOLE),
                                           per_tile(at_f[:, :, k]), ALU.is_equal))
                link(dve.tensor_tensor(mask[:, :, :], chosen[0][:, :, :], chosen[1][:, :, :], ALU.add))
                link(dve.tensor_tensor(work[:, :, :], chosen[2][:, :, :], chosen[3][:, :, :], ALU.add))
                link(dve.tensor_tensor(mask[:, :, :], mask[:, :, :], work[:, :, :], ALU.add))
                link(dve.tensor_copy(mask_b[:, :, :], mask[:, :, :]))
                link(dve.memset(before[0][:, 0:1], 0.0))
                link(dve.tensor_copy(before[0][:, 1:], mask[:, 0:NT - 1]))
                d, src = 1, 0
                while d < NT:
                    a, b = before[src], before[1 - src]
                    link(dve.tensor_copy(b[:, 0:d], a[:, 0:d]))
                    link(dve.tensor_tensor(b[:, d:], a[:, d:], a[:, 0:NT - d], ALU.add))
                    d, src = 2 * d, 1 - src
                dve.tensor_copy(before_b[:, :, :], before[src][:, :, :]).then_inc(counts_ready, 1)
                dve.wait_ge(place_done, 2)
                for k in range(TOPK):
                    link(dve.tensor_tensor(work[:, :, :], ps_place[:, :, :], chosen[k][:, :, :], ALU.mult))
                    link(dve.tensor_reduce(place[:, k], work[:, :, :], AX.X, ALU.add))
                    link(dve.tensor_scalar(first[:, k], at_f[:, :, k], float(CAP), None, ALU.mult))
                link(dve.tensor_scalar(late[:, :, :], place[:, :, :], float(CAP), None, ALU.is_ge))
                link(dve.tensor_scalar(slot[:, :, :], late[:, :, :], float(1 << 20), None, ALU.mult))
                link(dve.tensor_tensor(slot[:, :, :], slot[:, :, :], place[:, :, :], ALU.add))
                link(dve.tensor_tensor(slot[:, :, :], slot[:, :, :], first[:, :, :], ALU.add))
                link(dve.tensor_copy(kept["scatter_to"][:, :, :], slot[:, :, :]))
                link(dve.tensor_scalar(slot[:, :, :], place[:, :, :], float(CAP - 1), None, ALU.min))
                link(dve.tensor_tensor(slot[:, :, :], slot[:, :, :], first[:, :, :], ALU.add))
                link(dve.tensor_copy(kept["gather_from"][:, :, :], slot[:, :, :]))
                link(dve.tensor_scalar(late[:, :, :], late[:, :, :], -1.0, 1.0, ALU.mult, ALU.add))
                for k in range(TOPK):
                    link(dve.tensor_tensor(kept["weight"][:, k], late[:, k], best[:, :, k], ALU.mult))


def shared_phase(nc, t, kept):
    ctx, sb, ps, sem = open_scope(nc)
    FC = FS // P
    N = 2 * FC
    ITS = NB // 2 - 1
    with ctx:
        w_in, w_out = kept["shared_in"], kept["shared_out"]
        fT = sb("sh_fT", [P, 2, 2, KC, BLK], F32R)
        gate = sb("sh_gate", [P, 2, BLK])
        hid = sb("sh_hid", [P, BLK])
        hid_part = sb("sh_hid_part", [P, 2, 2, BLK], F32R)
        base = sb("sh_base", [P, 2, TB, D])
        idx = [sb(f"sh_idx{k}", [P, 1], U32) for k in range(TOPK)]
        tok = [sb(f"sh_tok{k}", [P, 1], I32) for k in range(TOPK)]
        ps_h = [ps(f"sh_ps_h{i}", [P, 2, BLK]) for i in range(2)]
        ps_y = ps("sh_ps_y", [P, TB, D])
        f_loaded = [sem(f"sh_f_loaded{i}") for i in range(2)]
        base_loaded = [sem(f"sh_base_loaded{i}") for i in range(2)]
        h_done = sem("sh_h_done")
        gate_done = sem("sh_gate_done")
        hid_done = sem("sh_hid_done")
        hid_hi = sem("sh_hid_hi")
        hid_lo = sem("sh_hid_lo")
        y_chunk = sem("sh_y_chunk")
        y_taken = sem("sh_y_taken")
        stored = [sem(f"sh_stored{i}") for i in range(2)]
        idx_set = sem("sh_idx_set")
        scattered = sem("sh_scattered")
        base_rows = t["base"].rearrange("(b t p) d -> b p t d", p=P, t=TB)

        with nc.Block() as block:
            @block.sync
            def _(sp):
                for s in range(2):
                    sp.sem_inc(stored[s], 16)

                def load_tokens(it, s):
                    sp.dma_start(as_f32(fT[:, s]), t["fT_part"][2 * it + s]).then_inc(f_loaded[s], 16)

                def load_base(it, s):
                    sp.wait_ge(stored[s], 16 * it + 16)
                    sp.dma_start(base[:, s], base_rows[2 * it + s]).then_inc(base_loaded[s], 16)

                for s in range(2):
                    load_tokens(0, s)
                    load_base(0, s)

                def work(it, last):
                    for s in range(2):
                        b = 2 * it + s
                        if not last:
                            sp.wait_ge(h_done, b * FC + FC)
                            load_tokens(it + 1, s)
                        sp.wait_ge(y_taken, b * TB + 2 * TB)
                        sp.dma_start(base_rows[b], base[:, s]).then_inc(stored[s], 16)
                        if not last:
                            load_base(it + 1, s)

                with sp.Fori(0, ITS) as it:
                    work(it, False)
                work(ITS, True)
                for s in range(2):
                    sp.wait_ge(stored[s], 16 * (NB // 2) + 16)

            @block.gpsimd
            def _(pool):
                with pool.Fori(0, NT) as i:
                    for k in range(TOPK):
                        pool.tensor_copy(idx[k][:, :], kept["scatter_to"][:, k, bass.ds(i, 1)]).then_inc(idx_set, 1)
                        pool.tensor_copy(tok[k][:, :], kept["token"][:, bass.ds(i, 1)]).then_inc(idx_set, 1)
                    pool.wait_ge(idx_set, i * 2 * TOPK + 2 * TOPK)
                    pool.sem_inc(kept["passed_pool"], 1)
                    for k in range(TOPK):
                        pool.indirect_dma_start(
                            out=t["slot_token"][:, :], out_offset=bass.IndirectOffsetOnAxis(ap=idx[k][:, 0:1], axis=0),
                            in_=tok[k][:, :], in_offset=None, bounds_check=E * CAP - 1, oob_is_err=False,
                        ).then_inc(scattered, 16)
                    pool.wait_ge(scattered, i * 16 * TOPK + 16 * TOPK)
                    pool.sem_inc(kept["passed_pool"], 1)

            @block.scalar
            def _(act):
                def silu(it, n):
                    act.wait_ge(h_done, it * N + n + 1)
                    act.wait_ge(hid_done, it * N + n + 1)
                    act.activation(gate[:, n % 2], ps_h[n % 2][:, 0], ACT.Silu).then_inc(gate_done, 1)

                with act.Fori(0, NB // 2) as it:
                    for n in range(N):
                        silu(it, n)

            @block.vector
            def _(dve):
                dve.sem_inc(hid_done, 2)
                dve.sem_inc(hid_lo, 1)
                dve.sem_inc(y_taken, TB)

                def hidden(it, n):
                    g = it * N + n
                    dve.wait_ge(gate_done, g + 1)
                    dve.wait_ge(hid_lo, g + 1)
                    dve.tensor_tensor(hid[:, :], ps_h[n % 2][:, 1], gate[:, n % 2], ALU.mult).then_inc(hid_done, 1)
                    dve.wait_ge(hid_done, g + 3)
                    dve.wait_ge(y_chunk, g + 1)
                    dve.tensor_copy(hid_part[:, n % 2, 0], hid[:, :]).then_inc(hid_hi, 1)
                    dve.wait_ge(hid_hi, g + 1)
                    dve.tensor_tensor(hid_part[:, n % 2, 1], hid[:, :], as_f32(hid_part[:, n % 2, 0]),
                                      ALU.subtract).then_inc(hid_lo, 1)

                def take(it, s):
                    b = 2 * it + s
                    dve.wait_ge(base_loaded[s], it * 16 + 16)
                    dve.wait_ge(y_chunk, b * FC + FC + 2)
                    for k in range(TB):
                        dve.scalar_tensor_tensor(out=base[:, s, k], in0=ps_y[:, k],
                                                 scalar=kept["shared_gate"][:, bass.ds(b * TB + k, 1)],
                                                 in1=base[:, s, k], op0=ALU.mult, op1=ALU.add).then_inc(y_taken, 1)

                hidden(0, 0)

                def work(it, last):
                    for n in range(N):
                        if n + 1 < N:
                            hidden(it, n + 1)
                        elif not last:
                            hidden(it + 1, 0)
                        if n % FC == FC - 1:
                            take(it, n // FC)

                with dve.Fori(0, ITS) as it:
                    work(it, False)
                work(ITS, True)

            @block.tensor
            def _(pe):
                pe.sem_inc(y_chunk, 2)

                def hidden(it, n):
                    s, f = divmod(n, FC)
                    if f == 0:
                        pe.wait_ge(f_loaded[s], 16 * it + 16)
                    pe.wait_ge(hid_done, it * N + n + 1)
                    for g in range(2):
                        for c in range(KC):
                            for x, (i, j) in enumerate(THREE):
                                mm = pe.matmul(ps_h[n % 2][:, g], w_in[:, j, g, c, f * P:(f + 1) * P],
                                               fT[:, s, i, c], start=c == 0 and x == 0, stop=c == KC - 1 and x == 2)
                    mm.then_inc(h_done, 1)

                def down(it, n):
                    s, f = divmod(n, FC)
                    pe.wait_ge(hid_lo, it * N + n + 2)
                    if f == 0:
                        pe.wait_ge(y_taken, (2 * it + s) * TB + TB)
                    for k in range(TB):
                        for x, (i, j) in enumerate(THREE):
                            mm = pe.matmul(ps_y[:, k], hid_part[:, n % 2, i, k * P:(k + 1) * P], w_out[:, j, f],
                                           start=f == 0 and x == 0, stop=f == FC - 1 and x == 2)
                    mm.then_inc(y_chunk, 1)

                hidden(0, 0)

                def work(it, last):
                    for n in range(N):
                        if n + 1 < N:
                            hidden(it, n + 1)
                        elif not last:
                            hidden(it + 1, 0)
                        down(it, n)

                with pe.Fori(0, ITS) as it:
                    work(it, False)
                work(ITS, True)


def expert_phase(nc, t, kept):
    ctx, sb, ps, sem = open_scope(nc)
    SC = CAP // P
    FP = [min(P, F - c) for c in range(0, F, P)]
    FC = len(FP)
    with ctx:
        raw_in = sb("ex_raw_in", [P, 2, 2, KC, F])
        raw_out = sb("ex_raw_out", [P, 2, FC, D])
        w_in = sb("ex_w_in", [P, 2, 2, 2, KC, F], F32R)
        w_out = sb("ex_w_out", [P, 2, 2, FC, D], F32R)
        table = sb("ex_table", [P, E, SC], U32)
        idx = [sb(f"ex_idx{i}", [P, 1], U32) for i in range(2 * SC)]
        x = [sb(f"ex_x{i}", [P, D]) for i in range(2 * SC)]
        xT = sb("ex_xT", [P, 2, KC, CAP], F32R)
        gate = sb("ex_gate", [P, 2, CAP])
        hid = sb("ex_hid", [P, CAP])
        hid_part = sb("ex_hid_part", [P, 2, FC, CAP], F32R)
        y = sb("ex_y", [P, 2, SC, D])
        ps_t = [ps(f"ex_ps_t{i}", [P, KC, P]) for i in range(2)]
        ps_h = [ps(f"ex_ps_h{i}", [P, 2, CAP]) for i in range(2)]
        ps_y = ps("ex_ps_y", [P, SC, D])
        table_loaded = sem("ex_table_loaded")
        in_loaded = [[sem(f"ex_in_loaded{i}_{g}") for g in range(2)] for i in range(2)]
        out_loaded = [sem(f"ex_out_loaded{i}") for i in range(2)]
        in_hi = [sem(f"ex_in_hi{g}") for g in range(2)]
        out_hi = sem("ex_out_hi")
        in_lo = sem("ex_in_lo")
        out_lo = sem("ex_out_lo")
        idx_set = sem("ex_idx_set")
        x_loaded = [sem(f"ex_x_loaded{i}") for i in range(2 * SC)]
        turned = sem("ex_turned")
        x_hi = sem("ex_x_hi")
        x_lo = sem("ex_x_lo")
        h_done = sem("ex_h_done")
        gate_done = sem("ex_gate_done")
        hid_done = sem("ex_hid_done")
        hid_hi = sem("ex_hid_hi")
        hid_lo = sem("ex_hid_lo")
        y_done = sem("ex_y_done")
        y_taken = sem("ex_y_taken")
        y_stored = [sem(f"ex_y_stored{i}") for i in range(2)]
        raw_wo = sb("ex_raw_wo", [P, KC, D])
        sums = sb("ex_sums", [P, H, S // P])
        inv = sb("ex_inv", [P, H, S // P])
        wo, inv_rows = kept["wo"], kept["inv_rows"]
        sums_loaded = sem("ex_sums_loaded")
        inv_made = sem("ex_inv_made")
        wo_loaded = sem("ex_wo_loaded")
        wo_hi = sem("ex_wo_hi")
        wo_lo = sem("ex_wo_lo")
        y_rows = t["expert_out"].rearrange("(e p c) d -> e p c d", e=E, c=SC)
        w_src = [t[name].rearrange("e (c p) f -> e p c f", p=P) for name in ("w_gate", "w_up")]
        last_rows = slice(0, FP[-1])
        ITS = E // 2 - 1

        with nc.Block() as block:
            @block.sync
            def _(sp):
                def load(it, i):
                    e = 2 * it + i
                    sp.wait_ge(in_lo, 2 * e + 4)
                    sp.sem_inc(kept["passed_sync"], 1)
                    for g in range(2):
                        sp.dma_start(raw_in[:, i, g], w_src[g][e]).then_inc(in_loaded[i][g], 16)
                    sp.wait_ge(out_lo, e + 2)
                    sp.dma_start(raw_out[:, i, 0:FC - 1], t["w_down"][e, 0:(FC - 1) * P, :].rearrange("(c p) n -> p c n", p=P)).then_inc(out_loaded[i], 16)
                    sp.dma_start(raw_out[last_rows, i, FC - 1], t["w_down"][e, (FC - 1) * P:F, :]).then_inc(out_loaded[i], 16)

                with nc.allow_non_contiguous_dma(reason="32 KB, once"):
                    sp.dma_start(table[:, :, :], t["slot_token"].bitcast(U32).rearrange("(e p c) a -> p e (c a)", e=E, c=SC)).then_inc(table_loaded, 16)
                for i in range(2):
                    sp.sem_inc(y_stored[i], 16)
                load(0, 0)
                load(0, 1)
                sp.dma_start(raw_wo[:, :, :], t["wo"].rearrange("(c p) n -> p c n", p=P)).then_inc(wo_loaded, 16)
                with nc.allow_non_contiguous_dma(reason="256 KB, once"):
                    sp.dma_start(sums[:, :, :], t["att_sum"].rearrange("h (p j) -> p h j", p=P)).then_inc(sums_loaded, 16)

                def work(it, last):
                    for i in range(2):
                        if not last:
                            load(it + 1, i)
                        e = 2 * it + i
                        sp.wait_ge(y_taken, e + 2)
                        sp.dma_start(y_rows[e], y[:, i]).then_inc(y_stored[i], 16)

                with sp.Fori(0, ITS) as it:
                    work(it, False)
                work(ITS, True)
                sp.wait_ge(inv_made, 1)
                with nc.allow_non_contiguous_dma(reason="256 KB, once"):
                    sp.dma_start(t["att_inv"].rearrange("h (p j) -> p h j", p=P), inv[:, :, :]).then_inc(inv_made, 16)
                sp.wait_ge(inv_made, 17)
                sp.dma_start(inv_rows[:, :], t["att_inv"]).then_inc(inv_made, 16)
                sp.wait_ge(inv_made, 33)
                for i in range(2):
                    sp.wait_ge(y_stored[i], 16 * (E // 2) + 16)

            @block.gpsimd
            def _(pool):
                def gather(it, i):
                    e = 2 * it + i
                    for c in range(SC):
                        pool.wait_ge(turned, e * SC + c + 1)
                        pool.tensor_copy(idx[i * SC + c][:, :], table[:, bass.ds(e, 1), c]).then_inc(idx_set, 1)
                        pool.wait_ge(idx_set, e * SC + c + 1)
                        pool.sem_inc(kept["passed_pool"], 1)
                        pool.indirect_dma_start(
                            out=x[i * SC + c][:, :], out_offset=None, in_=t["xf"][:, :],
                            in_offset=bass.IndirectOffsetOnAxis(ap=idx[i * SC + c][:, 0:1], axis=0),
                            bounds_check=S - 1, oob_is_err=False,
                        ).then_inc(x_loaded[i * SC + c], 16)

                def low_in(it, i):
                    for g in range(2):
                        pool.wait_ge(in_hi[g], 2 * it + i + 1)
                        pool.tensor_tensor(w_in[:, i, 1, g], raw_in[:, i, g], as_f32(w_in[:, i, 0, g]),
                                           ALU.subtract).then_inc(in_lo, 1)

                pool.sem_inc(in_lo, 4)
                pool.wait_ge(table_loaded, 16)
                gather(0, 0)
                gather(0, 1)
                low_in(0, 0)

                def work(it, last):
                    for i in range(2):
                        if i == 0 or not last:
                            low_in(it + i, 1 - i)
                        if not last:
                            gather(it + 1, i)

                with pool.Fori(0, ITS) as it:
                    work(it, False)
                work(ITS, True)
                pool.wait_ge(wo_hi, 1)
                pool.tensor_tensor(wo[:, 1], raw_wo[:, :, :], as_f32(wo[:, 0]), ALU.subtract).then_inc(wo_lo, 1)

            @block.scalar
            def _(act):
                act.sem_inc(y_taken, 1)

                def high_up(it, i):
                    e = 2 * it + i
                    act.wait_ge(in_loaded[i][1], 16 * it + 16)
                    act.wait_ge(y_done, e + 1)
                    act.activation(w_in[:, i, 0, 1], raw_in[:, i, 1], ACT.Copy).then_inc(in_hi[1], 1)

                def high_out(it, i):
                    e = 2 * it + i
                    act.wait_ge(out_loaded[i], 32 * it + 32)
                    act.wait_ge(y_done, e + 1)
                    act.activation(w_out[:, i, 0, 0:FC - 1], raw_out[:, i, 0:FC - 1], ACT.Copy)
                    act.activation(w_out[last_rows, i, 0, FC - 1], raw_out[last_rows, i, FC - 1], ACT.Copy).then_inc(out_hi, 1)

                def high_x(it, i):
                    e = 2 * it + i
                    for c in range(SC):
                        act.wait_ge(turned, e * SC + c + 2 * SC + 1)
                        act.wait_ge(h_done, e * FC + FC)
                        act.activation(xT[:, 0, :, c * P:(c + 1) * P], ps_t[c % 2][:, :, :], ACT.Copy).then_inc(x_hi, 1)

                high_up(0, 0)
                high_x(0, 0)
                high_out(0, 0)

                def work(it, last):
                    for i in range(2):
                        e = 2 * it + i
                        more = i == 0 or not last
                        for f in range(FC):
                            n = i * FC + f
                            act.wait_ge(h_done, it * 2 * FC + n + FC + 1)
                            act.wait_ge(hid_done, it * 2 * FC + n + 1)
                            act.activation(gate[0:FP[f], n % 2, :], ps_h[n % 2][0:FP[f], 0], ACT.Silu).then_inc(gate_done, 1)
                            if f == 0 and more:
                                high_up(it + i, 1 - i)
                        if more:
                            high_x(it + i, 1 - i)
                            high_out(it + i, 1 - i)
                        act.wait_ge(y_done, e + 3)
                        act.wait_ge(y_stored[i], 16 * it + 16)
                        act.activation(y[:, i], ps_y[:, :, :], ACT.Copy).then_inc(y_taken, 1)

                with act.Fori(0, ITS) as it:
                    work(it, False)
                act.wait_ge(wo_loaded, 16)
                act.activation(wo[:, 0], raw_wo[:, :, :], ACT.Copy).then_inc(wo_hi, 1)
                work(ITS, True)

            @block.vector
            def _(dve):
                dve.sem_inc(out_lo, 2)
                dve.sem_inc(hid_done, 2)
                dve.sem_inc(hid_lo, 1)
                dve.sem_inc(x_lo, SC)

                def high_gate(it, i):
                    e = 2 * it + i
                    dve.wait_ge(in_loaded[i][0], 16 * it + 16)
                    dve.wait_ge(y_done, e + 1)
                    dve.tensor_copy(w_in[:, i, 0, 0], raw_in[:, i, 0]).then_inc(in_hi[0], 1)

                def low_out(it, i):
                    dve.wait_ge(out_hi, 2 * it + i + 1)
                    dve.tensor_tensor(w_out[:, i, 1, 0:FC - 1], raw_out[:, i, 0:FC - 1],
                                      as_f32(w_out[:, i, 0, 0:FC - 1]), ALU.subtract)
                    dve.tensor_tensor(w_out[last_rows, i, 1, FC - 1], raw_out[last_rows, i, FC - 1],
                                      as_f32(w_out[last_rows, i, 0, FC - 1]), ALU.subtract).then_inc(out_lo, 1)

                def low_x(it, i):
                    for c in range(SC):
                        dve.wait_ge(x_hi, (2 * it + i) * SC + c + 1)
                        dve.tensor_tensor(xT[:, 1, :, c * P:(c + 1) * P], ps_t[c % 2][:, :, :],
                                          as_f32(xT[:, 0, :, c * P:(c + 1) * P]), ALU.subtract).then_inc(x_lo, 1)

                high_gate(0, 0)
                low_x(0, 0)
                low_out(0, 0)

                def work(it, last):
                    for i in range(2):
                        e = 2 * it + i
                        more = i == 0 or not last
                        for f in range(FC):
                            n = i * FC + f
                            rows = slice(0, FP[f])
                            if f == 0:
                                dve.wait_ge(y_done, e + 2)
                            dve.wait_ge(gate_done, it * 2 * FC + n + 1)
                            dve.wait_ge(hid_lo, it * 2 * FC + n + 1)
                            dve.tensor_tensor(hid[rows, :], ps_h[n % 2][rows, 1], gate[rows, n % 2], ALU.mult).then_inc(hid_done, 1)
                            dve.wait_ge(hid_done, it * 2 * FC + n + 3)
                            dve.tensor_copy(hid_part[rows, 0, f], hid[rows, :]).then_inc(hid_hi, 1)
                            dve.wait_ge(hid_hi, it * 2 * FC + n + 1)
                            dve.tensor_tensor(hid_part[rows, 1, f], hid[rows, :], as_f32(hid_part[rows, 0, f]),
                                              ALU.subtract).then_inc(hid_lo, 1)
                            if f == 0 and more:
                                high_gate(it + i, 1 - i)
                        if more:
                            low_x(it + i, 1 - i)
                            low_out(it + i, 1 - i)

                with dve.Fori(0, ITS) as it:
                    work(it, False)
                dve.wait_ge(sums_loaded, 16)
                dve.reciprocal(inv[:, :, :], sums[:, :, :]).then_inc(inv_made, 1)
                work(ITS, True)

            @block.tensor
            def _(pe):
                pe.sem_inc(turned, 2 * SC)
                pe.sem_inc(h_done, FC)
                pe.sem_inc(y_done, 2)

                def turn(it, i):
                    e = 2 * it + i
                    for c in range(SC):
                        pe.wait_ge(x_loaded[i * SC + c], 16 * it + 16)
                        pe.wait_ge(x_lo, e * SC + c + 1)
                        for m in range(KC):
                            mm = pe.transpose(ps_t[c % 2][:, m], x[i * SC + c][:, m * P:(m + 1) * P], kept["ident"][:, :])
                        mm.then_inc(turned, 1)

                turn(0, 0)

                def work(it, last):
                    for i in range(2):
                        e = 2 * it + i
                        pe.wait_ge(in_lo, 2 * e + 6)
                        pe.wait_ge(x_lo, e * SC + 2 * SC)
                        for f in range(FC):
                            n = i * FC + f
                            pe.wait_ge(hid_done, it * 2 * FC + n + 1)
                            for g in range(2):
                                for c in range(KC):
                                    for m, (a, b) in enumerate(THREE):
                                        mm = pe.matmul(ps_h[n % 2][0:FP[f], g], w_in[:, i, b, g, c, f * P:f * P + FP[f]],
                                                       xT[:, a, c], start=c == 0 and m == 0, stop=c == KC - 1 and m == 2)
                            mm.then_inc(h_done, 1)
                        if i == 0 or not last:
                            turn(it + i, 1 - i)
                        pe.wait_ge(out_lo, e + 3)
                        pe.wait_ge(y_taken, e + 1)
                        for f in range(FC):
                            pe.wait_ge(hid_lo, it * 2 * FC + i * FC + f + 2)
                            for s in range(SC):
                                for m, (a, b) in enumerate(THREE):
                                    mm = pe.matmul(ps_y[:, s], hid_part[0:FP[f], a, f, s * P:(s + 1) * P],
                                                   w_out[0:FP[f], i, b, f], start=f == 0 and m == 0,
                                                   stop=f == FC - 1 and m == 2)
                        mm.then_inc(y_done, 1)

                with pe.Fori(0, ITS) as it:
                    work(it, False)
                work(ITS, True)


def output_phase(nc, t, kept):
    ctx, sb, ps, sem = open_scope(nc)
    with ctx:
        w, inv_rows = kept["wo"], kept["inv_rows"]
        spread = sb("ou_spread", [H, KC, HPC, HD])
        att = sb("ou_att", [P, 2, 2, KC, BLK])
        z = sb("ou_z", [P, 2, BLK])
        z_part = sb("ou_z_part", [P, 2, 2, KC, BLK], F32R)
        acc = sb("ou_acc", [P, 2, TB, D])
        idx = sb("ou_idx", [P, 2, TOPK, TB], U32)
        ey = [[sb(f"ou_ey{i}_{k}", [P, D]) for k in range(TOPK)] for i in range(TB)]
        weight = sb("ou_weight", [P, 2, TOPK, TB])
        ps_z = [ps(f"ou_ps_z{i}", [P, D]) for i in range(TB)]
        ps_i = [ps(f"ou_ps_i{i}", [P, BLK]) for i in range(2)]
        spread_made = sem("ou_spread_made")
        att_loaded = [sem(f"ou_att_loaded{i}") for i in range(2)]
        parts_added = sem("ou_parts_added")
        i_done = sem("ou_i_done")
        z_made = sem("ou_z_made")
        z_hi = sem("ou_z_hi")
        z_lo = sem("ou_z_lo")
        base_loaded = [sem(f"ou_base_loaded{i}") for i in range(2)]
        idx_set = sem("ou_idx_set")
        gathered = [sem(f"ou_gathered{i}") for i in range(TB)]
        o_done = sem("ou_o_done")
        o_taken = sem("ou_o_taken")
        added = sem("ou_added")
        rows_done = sem("ou_rows_done")
        weight_set = sem("ou_weight_set")
        stored = [sem(f"ou_stored{i}") for i in range(2)]
        base_rows = t["base"].rearrange("(b t p) d -> b p t d", p=P, t=TB)
        out_rows = t["out"].rearrange("a (b t p) d -> (a b) p t d", p=P, t=TB)
        att_rows = t["att_v"].rearrange("a (c p) (b n) -> b a p c n", p=P, n=BLK)
        ITS = NB // 2 - 1

        with nc.Block() as block:
            @block.sync
            def _(sp):
                for i in range(2):
                    for part in range(2):
                        sp.dma_start(att[:, i, part], att_rows[i, part]).then_inc(att_loaded[i], 16)
                with sp.Fori(0, ITS) as it:
                    for i in range(2):
                        sp.wait_ge(z_made, (2 * it + i) * KC + 3 * KC)
                        for part in range(2):
                            sp.dma_start(att[:, i, part], att_rows[2 * it + 2 + i, part]).then_inc(att_loaded[i], 16)

            @block.gpsimd
            def _(pool):
                def add_parts(it, i, c):
                    if c == 0:
                        pool.wait_ge(att_loaded[i], 32 * it + 32)
                    pool.tensor_tensor(att[:, i, 0, c], att[:, i, 0, c], att[:, i, 1, c], ALU.add).then_inc(parts_added, 1)

                for c in range(KC):
                    add_parts(0, 0, c)

                def work(it, last):
                    for i in range(2):
                        b = 2 * it + i
                        pool.wait_ge(idx_set, b + 1)
                        for k in range(TB):
                            pool.wait_ge(rows_done, b * TB + k + 1)
                            pool.sem_inc(kept["passed_pool"], 1)
                            for j in range(TOPK):
                                pool.indirect_dma_start(
                                    out=ey[k][j][:, :], out_offset=None, in_=t["expert_out"][:, :],
                                    in_offset=bass.IndirectOffsetOnAxis(ap=idx[:, i, j, k:k + 1], axis=0),
                                    bounds_check=E * CAP - 1, oob_is_err=False,
                                ).then_inc(gathered[k], 16)
                            if i == 0 or not last:
                                add_parts(it + i, 1 - i, k)

                with pool.Fori(0, ITS) as it:
                    work(it, False)
                work(ITS, True)

            @block.scalar
            def _(act):
                for i in range(2):
                    act.sem_inc(stored[i], 16)

                def base(it, i):
                    act.wait_ge(stored[i], 16 * it + 16)
                    act.dma_start(acc[:, i], base_rows[2 * it + i]).then_inc(base_loaded[i], 16)

                def high(it, i):
                    b = 2 * it + i
                    for c in range(KC):
                        act.wait_ge(z_made, b * KC + c + 2 * KC + 1)
                        act.wait_ge(o_done, b * TB + TB)
                        act.activation(z_part[:, i, 0, c], z[:, c % 2], ACT.Copy).then_inc(z_hi, 1)

                base(0, 0)
                high(0, 0)

                def work(it, last):
                    for i in range(2):
                        if i == 0 or not last:
                            base(it + i, 1 - i)
                            high(it + i, 1 - i)
                        act.wait_ge(rows_done, (2 * it + i) * TB + 2 * TB)
                        act.dma_start(out_rows[2 * it + i], acc[:, i]).then_inc(stored[i], 16)

                with act.Fori(0, ITS) as it:
                    work(it, False)
                work(ITS, True)
                for i in range(2):
                    act.wait_ge(stored[i], 16 * (NB // 2) + 16)

            @block.vector
            def _(dve):
                dve.sem_inc(z_made, 2 * KC)
                dve.sem_inc(z_lo, 2)
                dve.sem_inc(o_taken, TB)
                dve.sem_inc(rows_done, TB)
                for i in range(2):
                    for src, dst, done in (("gather_from", idx, idx_set), ("weight", weight, weight_set)):
                        dve.tensor_copy(dst[:, i], kept[src][:, :, i * TB:(i + 1) * TB]).then_inc(done, 1)
                dve.tensor_copy(spread[:, :, :, :], kept["ident"][0:H, 0:H].rearrange("p (c g) -> p c g", c=KC)
                                .unsqueeze(3).to_broadcast([H, KC, HPC, HD])).then_inc(spread_made, 1)

                def low(it, i, c):
                    dve.wait_ge(z_hi, (2 * it + i) * KC + c + 1)
                    dve.tensor_tensor(z_part[:, i, 1, c], z[:, c % 2], as_f32(z_part[:, i, 0, c]), ALU.subtract).then_inc(z_lo, 1)

                def normal(it, i, c):
                    b = 2 * it + i
                    dve.wait_ge(parts_added, b * KC + c + 1)
                    dve.wait_ge(i_done, b * KC + c + 1)
                    dve.wait_ge(z_lo, b * KC + c + 1)
                    dve.tensor_tensor(z[:, c % 2], att[:, i, 0, c], ps_i[c % 2][:, :], ALU.mult).then_inc(z_made, 1)

                for c in range(KC):
                    normal(0, 0, c)
                    if c >= 1:
                        low(0, 0, c - 1)
                low(0, 0, KC - 1)

                def work(it, last):
                    for i in range(2):
                        b = 2 * it + i
                        more = i == 0 or not last
                        dve.wait_ge(weight_set, b + 1)
                        for k in range(TB):
                            if more:
                                normal(it + i, 1 - i, k)
                            n = (b * TB + k) * (TOPK - 1)
                            dve.wait_ge(o_done, b * TB + k + 2 * TB + 1)
                            dve.wait_ge(gathered[k], (b + 1) * 16 * TOPK)
                            for j in range(TOPK):
                                if j == 1:
                                    dve.wait_ge(o_taken, b * TB + k + TB + 1)
                                if j > 1:
                                    dve.wait_ge(added, n + j - 1)
                                so_far = acc[:, i, k] if j else ps_z[k][:, :]
                                dve.scalar_tensor_tensor(out=acc[:, i, k], in0=ey[k][j][:, :], scalar=weight[:, i, j, k:k + 1],
                                                         in1=so_far, op0=ALU.mult, op1=ALU.add).then_inc(added if j else o_taken, 1)
                            dve.wait_ge(added, n + TOPK - 1)
                            dve.sem_inc(rows_done, 1)
                            if more:
                                low(it + i, 1 - i, k)
                        if not last:
                            cols = bass.ds((b + 2) * TB, TB)
                            dve.tensor_copy(idx[:, i], kept["gather_from"][:, :, cols]).then_inc(idx_set, 1)
                            dve.tensor_copy(weight[:, i], kept["weight"][:, :, cols]).then_inc(weight_set, 1)

                with dve.Fori(0, ITS) as it:
                    work(it, False)
                work(ITS, True)

            @block.tensor
            def _(pe):
                pe.sem_inc(o_done, 2 * TB)
                pe.wait_ge(spread_made, 1)

                def inverses(it, i, c):
                    b = 2 * it + i
                    pe.wait_ge(z_made, b * KC + c + 2 * KC - 1)
                    pe.sem_inc(kept["passed_pe"], 1)
                    pe.matmul(ps_i[c % 2][:, :], spread[:, c].rearrange("p g d -> p (g d)"), inv_rows[:, bass.ds(b * BLK, BLK)],
                              start=True, stop=True).then_inc(i_done, 1)

                for c in range(KC):
                    inverses(0, 0, c)

                def work(it, last):
                    for i in range(2):
                        b = 2 * it + i
                        pe.wait_ge(z_lo, b * KC + KC + 2)
                        pe.wait_ge(base_loaded[i], 16 * it + 16)
                        for k in range(TB):
                            pe.wait_ge(o_taken, b * TB + k + 1)
                            for c in range(KC):
                                for n, (x, y) in enumerate(THREE):
                                    pe.matmul(ps_z[k][:, :], z_part[:, i, x, c, k * P:(k + 1) * P], w[:, y, c],
                                              start=c == 0 and n == 0, stop=False)
                            pe.matmul(ps_z[k][:, :], kept["ident"][:, :], acc[:, i, k], start=False,
                                      stop=True).then_inc(o_done, 1)
                            if i == 0 or not last:
                                inverses(it + i, 1 - i, k)

                with pe.Fori(0, ITS) as it:
                    work(it, False)
                work(ITS, True)


def host_constants():
    start = 2.0 ** (-8.0 / H_ALL)
    slopes = np.array([start * start ** i for i in range(H_ALL)], np.float32).astype(np.float64)
    bias = slopes[:, None] * (np.arange(S) - S // 2)[None, :]

    def twelve_bits(x):
        m, e = np.frexp(x)
        return np.ldexp(np.rint(m * 4096) / 4096, e)

    hi = twelve_bits(bias)
    alibi = np.stack([hi, twelve_bits(bias - hi)], axis=1).astype(np.float32)
    row, col = np.arange(P)[:, None], np.arange(P)[None, :]
    masks = np.zeros((P, 3 * P), np.float32)
    masks[:, 0:P][col > row] = MASKED
    masks[:, P:2 * P] = MASKED
    masks[:, 2 * P:][row > col] = MASKED
    return alibi, masks


KEPT = (
    ("ident", [P, P], F32), ("token", [P, NT], I32), ("shared_gate", [P, NT], F32),
    ("logits", [P, NT, RW], F32), ("scatter_to", [P, TOPK, NT], U32), ("gather_from", [P, TOPK, NT], U32), ("weight", [P, TOPK, NT], F32),
)
PROJECTION = (
    ("w_norm", [P, D], F32), ("bv", [P, D], F32), ("bo", [P, D], F32), ("bqk", [P, 2 * KC], F32),
    ("w_qkv", [P, 2, 3, KC, D], F32R), ("w_r", [P, 2, KC, RW], F32R),
)
SHARED = (
    ("shared_in", [P, 2, 2, KC, FS], F32R), ("shared_out", [P, 2, FS // P, D], F32R),
)
FINISH = (
    ("wo", [P, 2, KC, D], F32R), ("inv_rows", [H, S], F32),
)
SCRATCH = (
    ("base", [S, D], F32), ("xf", [S, D], F32), ("fT_part", [NB, P, 2, KC, BLK], F32),
    ("q_part", [2, D, S], F32), ("k_part", [2, D, S], F32), ("v_part", [S, H * 2 * HD], F32),
    ("att_v", [2, D, S], F32), ("att_sum", [H, S], F32), ("att_inv", [H, S], F32),
    ("slot_token", [E * CAP, 1], I32), ("expert_out", [E * CAP, D], F32),
    ("alibi_s", [H, 2, S], F32),
)


def build(nc, t):
    for name, shape, dt in SCRATCH:
        if name not in t:
            t[name] = nc.dram_tensor("scratch_" + name, shape, dt, kind="Internal").ap()
    with ExitStack() as whole:
        kept = {n: whole.enter_context(nc.sbuf_tensor("kept_" + n, shape, dt)) for n, shape, dt in KEPT}
        for name in ("passed_pool", "passed_dve", "passed_sync", "passed_pe"):
            kept[name] = whole.enter_context(nc.semaphore("kept_" + name))
        with ExitStack() as front:
            with ExitStack() as projection:
                for n, shape, dt in PROJECTION:
                    kept[n] = projection.enter_context(nc.sbuf_tensor("kept_" + n, shape, dt))
                project_phase(nc, t, kept)
            for n, shape, dt in SHARED:
                kept[n] = front.enter_context(nc.sbuf_tensor("kept_" + n, shape, dt))
            routing_phase(nc, t, kept)
            shared_phase(nc, t, kept)
        attention_phase(nc, t, kept)
        for n, shape, dt in FINISH:
            kept[n] = whole.enter_context(nc.sbuf_tensor("kept_" + n, shape, dt))
        expert_phase(nc, t, kept)
        output_phase(nc, t, kept)


_INS = {
    "L0_attn_x": "x", "L0_attn_wq": "wq", "L0_attn_bq": "bq", "L0_attn_wk": "wk", "L0_attn_bk": "bk",
    "L0_attn_wv": "wv", "L0_attn_bv": "bv", "L0_attn_wo": "wo", "L0_attn_bo": "bo", "L0_ffn_w_norm": "w_norm",
    "L0_ffn_w_router": "w_router", "L0_ffn_w_gate": "w_gate", "L0_ffn_w_up": "w_up", "L0_ffn_w_down": "w_down",
    "L0_ffn_sw_gate": "sw_gate", "L0_ffn_sw_up": "sw_up", "L0_ffn_sw_down": "sw_down",
    "L0_ffn_w_shared_gate": "w_sgate",
}


def kernel(**inputs):
    import numpy as _np
    import concourse.bacc as _bacc
    from concourse.bass_utils import run_bass_kernel_spmd as _run

    nc = _bacc.Bacc("TRN2", target_bir_lowering=False, num_devices=1)
    alibi, masks = host_constants()
    arrays = {name: _np.ascontiguousarray(inputs[long]) for long, name in _INS.items()}
    arrays |= {
        "alibi": alibi, "masks": masks, "ident": _np.eye(P, dtype=_np.float32),
        "upper": _np.triu(_np.ones((P, P), _np.float32), 1), "experts": _np.arange(E, dtype=_np.float32),
    }
    t = {n: nc.dram_tensor(f"in_{n}", a.shape, mybir.dt.from_np(a.dtype), kind="ExternalInput").ap() for n, a in arrays.items()}
    t["out"] = nc.dram_tensor("out_x", (1, S, D), F32, kind="ExternalOutput").ap()
    build(nc, t)
    r = _run(nc, [{f"in_{n}": a for n, a in arrays.items()}], core_ids=[0])
    return r.results[0]["out_x"]
```
